# Optimizing a Trainium2 kernel written in Bass

```python
import numpy as np
import jax
import jax.numpy as jnp

def _softmax(x, axis=-1):
    return jax.nn.softmax(x, axis=axis)

def _gelu(x):
    return jax.nn.gelu(x, approximate=True)

def _silu(x):
    return jax.nn.silu(x)

def _sigmoid(x):
    return jax.nn.sigmoid(x)

def _layernorm(x, axis=-1, eps=1e-05):
    m = jnp.mean(x, axis=axis, keepdims=True)
    v = jnp.var(x, axis=axis, keepdims=True)
    return (x - m) / jnp.sqrt(v + eps)

def _scatter_add(tgt, idx, src, axis=0):
    return tgt.at[idx].add(src)

def _segment_sum(src, seg, n):
    return jax.ops.segment_sum(src, seg, n)
kernel_name = 'mk_gnn_resnorm_d4_gnn_r64_8df693'

def setup_inputs(seed: int=0):
    np.random.seed(seed)
    _w = jnp.asarray

    def _rec_inputs():
        import jax
        import jax.numpy as jnp
        _gk = jax.random.key(seed)
        x = -0.000202 + 1 * jax.random.normal(jax.random.fold_in(_gk, 1), (100000, 64), jnp.float32)
        src = jax.random.randint(jax.random.fold_in(_gk, 2), (25000,), 0, 100000, jnp.int32)
        dst = jnp.minimum((100000 * jax.random.uniform(jax.random.fold_in(_gk, 3), (25000,)) ** 2.0).astype(jnp.int32), 99999)
        _o = jnp.argsort(dst, stable=True)
        src = src[_o]
        dst = dst[_o]
        edge_attr_16 = 1.36993e-05 + 0.999972 * jax.random.normal(jax.random.fold_in(_gk, 12), (25000, 16), jnp.float32)
        edge_weight = jax.random.uniform(jax.random.fold_in(_gk, 14), (25000,), jnp.float32, 0.0, 0.999999)
        return (x, src, dst, edge_attr_16, edge_weight)
    x, src, dst, edge_attr_16, edge_weight = _rec_inputs()

    def _L0_gnn_setup():
        import jax, jax.numpy as jnp
        import numpy as np
        N = 100000
        E = 20000
        D_IN = 64
        D_OUT = 64
        D_EDGE = 16
        NEG_SLOPE = 0.01
        key = jax.random.key(seed)
        ks = jax.random.split(key, 8)
        x = jax.random.normal(ks[0], (N, D_IN), dtype=jnp.float32)
        edge_attr = jax.random.normal(ks[1], (E, D_EDGE), dtype=jnp.float32)
        src = jax.random.randint(ks[2], (E,), 0, N, dtype=jnp.int32)
        dst = jax.random.randint(ks[3], (E,), 0, N, dtype=jnp.int32)
        W1 = jax.random.normal(ks[4], (D_OUT, D_IN + D_EDGE), dtype=jnp.float32) * (2.0 / (D_OUT + D_IN + D_EDGE)) ** 0.5
        W2 = jax.random.normal(ks[5], (D_OUT, D_IN), dtype=jnp.float32) * (2.0 / (D_OUT + D_IN)) ** 0.5
        attn = jax.random.normal(ks[6], (D_OUT + D_IN,), dtype=jnp.float32) * (2.0 / (1 + D_OUT + D_IN)) ** 0.5
        bias = jnp.zeros((D_OUT,), dtype=jnp.float32)
        return {'x': x, 'edge_attr': edge_attr, 'src': src, 'dst': dst, 'W1': W1, 'W2': W2, 'attn': attn, 'bias': bias}
    _L0_gnn_all = _L0_gnn_setup()
    _L0_gnn_in = {k: v for k, v in _L0_gnn_all.items() if k in ('W1', 'W2', 'attn', 'bias')}
    del _L0_gnn_all

    def _L1_gnn_setup():
        import jax, jax.numpy as jnp
        import numpy as np
        N = 100000
        E = 25000
        D = 64
        LN_EPS = 1e-05

        def _layernorm(h, g, b):
            mu = jnp.mean(h, axis=-1, keepdims=True)
            var = jnp.var(h, axis=-1, keepdims=True)
            return (h - mu) * jax.lax.rsqrt(var + LN_EPS) * g + b
        key = jax.random.key(seed)
        ks = jax.random.split(key, 12)
        s = 1.0 / np.sqrt(D)
        x = jax.random.normal(ks[0], (N, D), dtype=jnp.float32)
        edge_index = jax.random.randint(ks[1], (2, E), 0, N, dtype=jnp.int32)
        routing_factor = jax.random.uniform(ks[2], (E,), dtype=jnp.float32)
        return {'x': x, 'edge_index': edge_index, 'routing_factor': routing_factor, 'W_phys': jax.random.normal(ks[3], (D, D), dtype=jnp.float32) * s, 'W_neur': jax.random.normal(ks[4], (D, D), dtype=jnp.float32) * s, 'att_w': jax.random.normal(ks[5], (2 * D,), dtype=jnp.float32) * s, 'channel_fusion': jnp.float32(0.5), 'mlp_w1': jax.random.normal(ks[6], (2 * D, D), dtype=jnp.float32) * s, 'mlp_b1': jnp.zeros((2 * D,), dtype=jnp.float32), 'mlp_w2': jax.random.normal(ks[7], (D, 2 * D), dtype=jnp.float32) / np.sqrt(2 * D), 'mlp_b2': jnp.zeros((D,), dtype=jnp.float32), 'ln1_g': jnp.ones((D,), dtype=jnp.float32), 'ln1_b': jnp.zeros((D,), dtype=jnp.float32), 'ln2_g': jnp.ones((D,), dtype=jnp.float32), 'ln2_b': jnp.zeros((D,), dtype=jnp.float32)}
    _L1_gnn_all = _L1_gnn_setup()
    _L1_gnn_in = {k: v for k, v in _L1_gnn_all.items() if k in ('W_phys', 'W_neur', 'att_w', 'channel_fusion', 'mlp_w1', 'mlp_b1', 'mlp_w2', 'mlp_b2', 'ln1_g', 'ln1_b', 'ln2_g', 'ln2_b')}
    del _L1_gnn_all

    def _L2_gnn_setup():
        import jax, jax.numpy as jnp
        import numpy as np
        N_NODES = 100000
        IN_FEATS = 64
        OUT_FEATS = 64
        N_EDGES = 18750

        def _symmetric_normalization(edge_index, num_nodes):
            row, col = (edge_index[0], edge_index[1])
            ones = jnp.ones(row.shape[0], dtype=jnp.float32)
            deg = jax.ops.segment_sum(ones, row, num_segments=num_nodes)
            deg_inv_sqrt = jnp.where(deg > 0, jax.lax.rsqrt(jnp.maximum(deg, 1.0)), 0.0)
            return deg_inv_sqrt[row] * deg_inv_sqrt[col]
        key = jax.random.key(seed)
        k1, k2, k3, k4 = jax.random.split(key, 4)
        x = jax.random.normal(k1, (N_NODES, IN_FEATS), dtype=jnp.float32)
        edge_index = jax.random.randint(k2, (2, N_EDGES), 0, N_NODES, dtype=jnp.int64)
        W = jax.random.normal(k3, (OUT_FEATS, IN_FEATS), dtype=jnp.float32) / np.sqrt(IN_FEATS)
        b = jax.random.normal(k4, (OUT_FEATS,), dtype=jnp.float32) * 0.01
        return {'x': x, 'edge_index': edge_index, 'W': W, 'b': b}
    _L2_gnn_all = _L2_gnn_setup()
    _L2_gnn_in = {k: v for k, v in _L2_gnn_all.items() if k in ('W', 'b')}
    del _L2_gnn_all

    def _L3_gnn_setup():
        import jax, jax.numpy as jnp
        import numpy as np
        N = 100000
        NNZ = 25000
        D = 64
        key = jax.random.key(seed)
        k1, k2, k3, k4 = jax.random.split(key, 4)
        x = jax.random.normal(k1, (N, D), dtype=jnp.float32)
        row = jax.random.randint(k2, (NNZ,), 0, N, dtype=jnp.int64)
        col = jax.random.randint(k3, (NNZ,), 0, N, dtype=jnp.int64)
        value = jax.random.uniform(k4, (NNZ,), dtype=jnp.float32)
        return {'x': x, 'row': row, 'col': col, 'value': value, 'size': N}
    _L3_gnn_all = _L3_gnn_setup()
    _L3_gnn_in = {k: v for k, v in _L3_gnn_all.items() if k in ()}
    del _L3_gnn_all
    return {'x': x, 'src': src, 'dst': dst, 'edge_attr_16': edge_attr_16, 'edge_weight': edge_weight, 'L0_gnn_W1': _L0_gnn_in['W1'], 'L0_gnn_W2': _L0_gnn_in['W2'], 'L0_gnn_attn': _L0_gnn_in['attn'], 'L0_gnn_bias': _L0_gnn_in['bias'], 'L1_gnn_W_phys': _L1_gnn_in['W_phys'], 'L1_gnn_W_neur': _L1_gnn_in['W_neur'], 'L1_gnn_att_w': _L1_gnn_in['att_w'], 'L1_gnn_channel_fusion': _L1_gnn_in['channel_fusion'], 'L1_gnn_mlp_w1': _L1_gnn_in['mlp_w1'], 'L1_gnn_mlp_b1': _L1_gnn_in['mlp_b1'], 'L1_gnn_mlp_w2': _L1_gnn_in['mlp_w2'], 'L1_gnn_mlp_b2': _L1_gnn_in['mlp_b2'], 'L1_gnn_ln1_g': _L1_gnn_in['ln1_g'], 'L1_gnn_ln1_b': _L1_gnn_in['ln1_b'], 'L1_gnn_ln2_g': _L1_gnn_in['ln2_g'], 'L1_gnn_ln2_b': _L1_gnn_in['ln2_b'], 'L2_gnn_W': _L2_gnn_in['W'], 'L2_gnn_b': _L2_gnn_in['b']}

def reference(x, src, dst, edge_attr_16, edge_weight, L0_gnn_W1, L0_gnn_W2, L0_gnn_attn, L0_gnn_bias, L1_gnn_W_phys, L1_gnn_W_neur, L1_gnn_att_w, L1_gnn_channel_fusion, L1_gnn_mlp_w1, L1_gnn_mlp_b1, L1_gnn_mlp_w2, L1_gnn_mlp_b2, L1_gnn_ln1_g, L1_gnn_ln1_b, L1_gnn_ln2_g, L1_gnn_ln2_b, L2_gnn_W, L2_gnn_b):
    import jax
    import jax.numpy as jnp

    def _L0_gnn_ref(x, edge_attr, src, dst, W1, W2, attn, bias):
        import jax, jax.numpy as jnp
        import numpy as np
        N = 100000
        E = 20000
        D_IN = 64
        D_OUT = 64
        D_EDGE = 16
        NEG_SLOPE = 0.01
        x_t = x @ W2.T
        x_l = x[src]
        x_r = x[dst]
        f_srt = jnp.concatenate([x_l, edge_attr], axis=-1) @ W1.T
        e = jax.nn.leaky_relu(jnp.concatenate([f_srt, x_r], axis=-1), NEG_SLOPE)
        logits = e @ attn
        seg_max = jax.ops.segment_max(logits, dst, num_segments=N)
        seg_max = jnp.where(jnp.isfinite(seg_max), seg_max, 0.0)
        expd = jnp.exp(logits - seg_max[dst])
        denom = jax.ops.segment_sum(expd, dst, num_segments=N)
        alpha = expd / denom[dst]
        msgs = x_t[src] * alpha[:, None]
        h = jax.ops.segment_sum(msgs, dst, num_segments=N)
        return h + bias

    def _L1_gnn_ref(x, edge_index, routing_factor, W_phys, W_neur, att_w, channel_fusion, mlp_w1, mlp_b1, mlp_w2, mlp_b2, ln1_g, ln1_b, ln2_g, ln2_b):
        import jax, jax.numpy as jnp
        import numpy as np
        N = 100000
        E = 25000
        D = 64
        LN_EPS = 1e-05

        def _layernorm(h, g, b):
            mu = jnp.mean(h, axis=-1, keepdims=True)
            var = jnp.var(h, axis=-1, keepdims=True)
            return (h - mu) * jax.lax.rsqrt(var + LN_EPS) * g + b
        src, dst = (edge_index[0], edge_index[1])
        x_src = x[src]
        att_scores = x_src @ att_w[:D] + x[dst] @ att_w[D:]
        seg_max = jax.ops.segment_max(att_scores, dst, num_segments=N)
        e = jnp.exp(att_scores - seg_max[dst])
        denom = jax.ops.segment_sum(e, dst, num_segments=N)
        att = e / denom[dst]
        phys = routing_factor[:, None] * (x_src @ W_phys.T)
        neur = x_src @ W_neur.T
        alpha = jax.nn.sigmoid(channel_fusion)
        messages = att[:, None] * (alpha * phys + (1.0 - alpha) * neur)
        out = jax.ops.segment_sum(messages, dst, num_segments=N)
        h = _layernorm(jax.nn.gelu(out, approximate=False) + x, ln1_g, ln1_b)
        m = jax.nn.gelu(h @ mlp_w1.T + mlp_b1, approximate=False) @ mlp_w2.T + mlp_b2
        return _layernorm(m + h, ln2_g, ln2_b)

    def _L2_gnn_ref(x, edge_index, W, b):
        import jax, jax.numpy as jnp
        import numpy as np
        N_NODES = 100000
        IN_FEATS = 64
        OUT_FEATS = 64
        N_EDGES = 18750

        def _symmetric_normalization(edge_index, num_nodes):
            row, col = (edge_index[0], edge_index[1])
            ones = jnp.ones(row.shape[0], dtype=jnp.float32)
            deg = jax.ops.segment_sum(ones, row, num_segments=num_nodes)
            deg_inv_sqrt = jnp.where(deg > 0, jax.lax.rsqrt(jnp.maximum(deg, 1.0)), 0.0)
            return deg_inv_sqrt[row] * deg_inv_sqrt[col]
        row, col = (edge_index[0], edge_index[1])
        edge_attr = _symmetric_normalization(edge_index, N_NODES)
        msgs = x[col] * edge_attr[:, None]
        h = jax.ops.segment_sum(msgs, row, num_segments=N_NODES)
        return h @ W.T + b

    def _L3_gnn_ref(x, row, col, value, size):
        import jax, jax.numpy as jnp
        import numpy as np
        N = 100000
        NNZ = 25000
        D = 64
        gathered = value[:, None] * x[col]
        y = jax.ops.segment_sum(gathered, row, num_segments=size)
        return y
    edge_index = jnp.stack([src, dst])
    x = _layernorm(x + _L0_gnn_ref(x, edge_attr_16, src, dst, L0_gnn_W1, L0_gnn_W2, L0_gnn_attn, L0_gnn_bias), axis=-1)
    x = _layernorm(x + _L1_gnn_ref(x, edge_index, edge_weight, L1_gnn_W_phys, L1_gnn_W_neur, L1_gnn_att_w, L1_gnn_channel_fusion, L1_gnn_mlp_w1, L1_gnn_mlp_b1, L1_gnn_mlp_w2, L1_gnn_mlp_b2, L1_gnn_ln1_g, L1_gnn_ln1_b, L1_gnn_ln2_g, L1_gnn_ln2_b), axis=-1)
    x = _layernorm(x + _L2_gnn_ref(x, edge_index, L2_gnn_W, L2_gnn_b), axis=-1)
    x = _layernorm(x + _L3_gnn_ref(x, src, dst, edge_weight, 100000), axis=-1)
    return x

_drawn_inputs = setup_inputs


def setup_inputs(seed=0):
    import zlib

    import numpy as np

    out = dict(_drawn_inputs(seed))
    spreads = {'L0_gnn_bias': (0.0, 0.1),
     'L1_gnn_mlp_b1': (0.0, 0.1),
     'L1_gnn_mlp_b2': (0.0, 0.1),
     'L1_gnn_ln1_g': (1.0, 0.2),
     'L1_gnn_ln1_b': (0.0, 0.1),
     'L1_gnn_ln2_g': (1.0, 0.2),
     'L1_gnn_ln2_b': (0.0, 0.1)}
    factors = {'L1_gnn_att_w': 4.118, 'L2_gnn_b': 4.396}
    for name, (base, spread) in spreads.items():
        noise = np.random.default_rng([zlib.crc32(name.encode()), seed]).standard_normal(out[name].shape)
        drawn = base * np.exp(spread * noise) if base else spread * noise
        out[name] = jnp.asarray(drawn.astype(out[name].dtype))
    for name, factor in factors.items():
        out[name] = (out[name] * factor).astype(out[name].dtype)
    return out
```

```python
import concourse.bass as bass
from concourse import mybir
from contextlib import ExitStack

fp32 = mybir.dt.float32
bf16 = mybir.dt.bfloat16
i32 = mybir.dt.int32
ALU = mybir.AluOpType
ACT = mybir.ActivationFunctionType
AX = mybir.AxisListType


def gnn_resnorm_kernel(nc, x, src, dst, edge_attr, edge_weight, W1, W2, attn, bias0, W_phys, W_neur, att_w,
                       fusion, mlp_w1, mlp_b1, mlp_w2, mlp_b2, ln1_g, ln1_b, ln2_g, ln2_b, L2_W, L2_b, out):
    N, D = x.shape
    E, DE = edge_attr.shape
    HID = mlp_w1.shape[0]
    P = 125
    TC = E // P
    GC = 8
    NGR = TC // GC
    Q = GC // 2
    EW = Q * P
    NB = 1024
    NBLK = -(-N // NB)
    R = 16
    NT = 128 * R
    NTILE = -(-N // NT)
    K = 2
    HB = 782
    HH = HB // 2
    EPS = 1e-5
    NEG = -1e30
    SKIP = 1 << 22

    agg0 = nc.dram_tensor("agg0", (N, D), fp32).ap()
    x2tab = nc.dram_tensor("x2tab", (N, D), fp32).ap()
    acc2 = nc.dram_tensor("acc2", (N, K * D), fp32).ap()
    acc3 = nc.dram_tensor("acc3", (N, K * D), fp32).ap()
    distab = nc.dram_tensor("distab", (128 * HB,), fp32).ap()
    acc2_rows = acc2.rearrange("n (k d) -> (n k) d", k=K)
    acc3_rows = acc3.rearrange("n (k d) -> (n k) d", k=K)

    ctx = ExitStack()
    with ctx:
        def sb(name, shape, dt=fp32):
            return ctx.enter_context(nc.sbuf_tensor(name, shape, dt))

        xsn = sb("xsn", [128, TC, D])
        xdt = sb("xdt", [128, TC // 2 * P])
        ag = sb("ag", [128, D, TC])
        src_i, dst_i, last_i, acc_i = (sb(n, [P, TC + 2 * GC], i32) for n in ("src_i", "dst_i", "last_i", "acc_i"))
        ew, same, nxt, last, pen_f, pen_b, score, sm1, sm2, dis = (
            sb(n, [P, TC]) for n in ("ew", "same", "nxt", "last", "pen_f", "pen_b", "score", "sm1", "sm2", "dis"))
        edge_col, carry = (sb(n, [P, D]) for n in ("edge_col", "carry"))
        rows = sb("rows", [D, P + 1])
        ends = sb("ends", [P, 4])
        row_flags = sb("row_flags", [D, 4, P])
        ident, blk_j, blk_c, low = (sb(n, [128, 128]) for n in ("ident", "blk_j", "blk_c", "low"))
        wt = sb("wt", [128, 7, 128])
        A2C, W1X, PHY, NEU, L2W, W1T, DG2 = range(7)
        w2p = sb("w2p", [128, 2, 128])
        att = sb("att", [128, 4, 2])
        vec = sb("vec", [128, 17])
        B0, G1, LB1, G2, LB2, MB2, MB1, L2B, FUS, EPSV, CB0, CR, CT, C2, HB1, FUN, T0 = range(17)
        b2_row = sb("b2_row", [128, D])
        zero = sb("zero", [128, 250])
        LANES = range(2)

        def lane(name, cols):
            return [sb(f"{name}{l}", [128, cols]) for l in LANES]

        xin, b_u, b_sq, b_r, b_x1, b_h = (lane(n, 512) for n in ("xin", "b_u", "b_sq", "b_r", "b_x1", "b_h"))
        b_gl = lane("b_gl", 1024)
        g_s = lane("g_s", GC * D)
        ix_a = [sb(f"ix_a{l}", [P, GC], i32) for l in LANES]
        ix_b = [sb(f"ix_b{l}", [P, GC], i32) for l in LANES]
        sf, cnt, chain_of = (sb(n, [P, GC]) for n in ("sf", "cnt", "chain_of"))

        psA, psB = ([ctx.enter_context(nc.psum_tensor(f"ps{b}{l}", [128, 512], fp32)) for l in LANES] for b in "AB")
        psGH = [ctx.enter_context(nc.psum_tensor(f"psGH{l}", [128, 1024], fp32)) for l in LANES]

        def psG(l):
            return psGH[l][:, 0:512]

        def psH(l):
            return psGH[l][:, 512:1024]

        agf = ag[:, :, :].rearrange("p d t -> p (d t)")
        at_ = [0]

        def in_ag(cols):
            at_[0] += cols
            return agf[:, at_[0] - cols:at_[0]]

        wbd = in_ag(6 * 128).rearrange("p (w c) -> p w c", w=6)
        w_e = in_ag(Q * 128).rearrange("p (w c) -> p w c", w=Q)
        w1e_s, w1e_t, w1d, w2s = in_ag(DE), in_ag(D), in_ag(128), in_ag(HID)
        g_d = [in_ag(GC * D) for _ in LANES]
        ea_s = [in_ag(GC * DE) for _ in LANES]
        ea_t = in_ag(P)
        iota_lo, iota_hi = in_ag(128), in_ag(HB)
        oh_lo = [in_ag(64).bitcast(bf16) for _ in LANES]
        oh_hi = [in_ag(HH).bitcast(bf16) for _ in LANES]
        deg, deg_on = in_ag(HB), in_ag(HB)
        src_lo, src_hi, dst_f, prev_f, next_f, tmp_f = (in_ag(TC) for _ in range(6))
        tmp_i = in_ag(TC).bitcast(i32)

        xsf = xsn[:, :, :].rearrange("p t d -> p (t d)")
        xt_ = [0]

        def in_xsn(cols):
            xt_[0] += cols
            return xsf[:, xt_[0] - cols:xt_[0]]

        xrow = [in_xsn(GC * D) for _ in LANES]
        zrow = [in_xsn(GC * D) for _ in LANES]
        g_a = [in_xsn(GC * K * D) for _ in LANES]
        zs = in_xsn(GC * D)
        same_src = in_xsn(GC * P)
        dup = in_xsn(GC * P)

        LOADED = 16 * (2 * 7 + 2 + 2 * 5 + 2 * 5 + 3 + 3 + 4)
        names = {}

        def S(name):
            if name not in names:
                names[name] = ctx.enter_context(nc.semaphore(name))
            return names[name]

        def col(v):
            return vec[:, v:v + 1]

        def grp(a, g):
            return a[:, bass.ds(g * GC, GC)]

        def xg(g):
            return xdt[:, bass.ds(g * EW, EW)]

        def xsg(g):
            return xsf[0:P, bass.ds(g * (GC * D), GC * D)]

        def bc(a, d):
            return a.unsqueeze(2).broadcast_to((a.shape[0], a.shape[1], d))

        def t3(a, c=GC):
            return a.rearrange("p (c d) -> p c d", c=c)

        block = ctx.enter_context(nc.Block())

        def groups(eng, body):
            with eng.Fori(0, NGR // 2) as i:
                body(0, i, 2 * i)
                body(1, i, 2 * i + 1)
            body(0, NGR // 2, NGR - 1)

        def of_parity(par):
            return (NGR + 1 - par) // 2

        def both(*programs):
            at = [next(p) for p in programs]
            while any(a is not None for a in at):
                j = min((j for j in range(len(at)) if at[j] is not None), key=lambda j: at[j])
                at[j] = next(programs[j], None)

        LOOPS = 3
        PAIRS = (NBLK - LOOPS * NGR) // 2
        assert 2 * PAIRS + 1 + LOOPS * NGR == NBLK

        def run1(loop, g):
            return PAIRS + 1 + loop * NGR + g

        def row1(loop, g):
            if loop == LOOPS - 1 and isinstance(g, int) and g == NGR - 1:
                return N - NB
            return (2 * PAIRS + 1 + loop * NGR + g) * NB

        def mlp_pe(pe, h, l, n, w, w4):
            yield h + 1
            pe.wait_ge(S(f"mlp_h{l}"), n + 1)
            nc.tensor.matmul(psGH[l][:, 0:w], wt[0:64, W1T, :], b_h[l][0:64, 0:w], start=True, stop=True)
            nc.tensor.matmul(psGH[l][:, 512:512 + w], wt[64:128, W1T, :], b_h[l][64:128, 0:w], start=True,
                             stop=True).then_inc(S(f"mlp_m1{l}"), 1)
            nc.tensor.matmul(psA[l][:, 0:w], blk_c[:, :], b_h[l][:, 0:w], start=True, stop=False)
            yield h + 3
            pe.wait_ge(S(f"mlp_gelu{l}"), n + 1)
            nc.tensor.matmul(psA[l][:, 0:w], w2p[:, 0, :], b_gl[l][:, 0:w], start=False, stop=False)
            nc.tensor.matmul(psA[l][:, 0:w], w2p[:, 1, :], b_gl[l][:, 512:512 + w], start=False,
                             stop=True).then_inc(S(f"mlp_m2{l}"), 1)
            yield h + 5
            pe.wait_ge(S(f"mlp_q3{l}"), n + 1)
            nc.tensor.matmul(psG(l)[:, 0:w], blk_j[:, :], b_sq[l][:, 0:w], start=True,
                             stop=True).then_inc(S(f"mlp_j3{l}"), 1)
            yield h + 8
            pe.wait_ge(S(f"mlp_t{l}"), n + 1)
            nc.tensor.matmul(psB[l][:, 0:w], wt[:, DG2, :], b_u[l][:, 0:w], start=True,
                             stop=True).then_inc(S(f"mlp_d{l}"), 1)
            yield h + 11
            pe.wait_ge(S(f"mlp_q4{l}"), n + 1)
            nc.tensor.matmul(psG(l)[:, 0:w], blk_j[:, :], b_sq[l][:, 0:w], start=True,
                             stop=True).then_inc(S(f"mlp_j4{l}"), 1)
            yield h + 14
            pe.wait_ge(S(f"mlp_x2{l}"), n + 1)
            for q in range(4):
                last_t = nc.tensor.transpose(psA[l][0:w4, 128 * q:128 * q + 128], b_h[l][:, w4 * q:w4 * q + w4], ident[:, :])
            last_t.then_inc(S(f"mlp_t9{l}"), 1)

        def mlp_act(act, h, l, n, w, stored=None):
            yield h + 2
            act.wait_ge(S(f"mlp_m1{l}"), n + 1)
            if stored is not None:
                act.wait_ge(S(f"blk_st{l}"), stored)
            nc.scalar.activation(b_gl[l][:, :].rearrange("p (b f) -> p b f", b=2)[:, :, 0:w],
                                 psGH[l][:, :].rearrange("p (b f) -> p b f", b=2)[:, :, 0:w], ACT.Gelu,
                                 bias=col(HB1)).then_inc(S(f"mlp_gelu{l}"), 1)
            yield h + 4
            act.wait_ge(S(f"mlp_m2{l}"), n + 1)
            nc.scalar.activation(b_sq[l][:, 0:w], psA[l][:, 0:w], ACT.Square, bias=col(CR)).then_inc(S(f"mlp_q3{l}"), 1)
            yield h + 6
            act.wait_ge(S(f"mlp_j3{l}"), n + 1)
            nc.scalar.activation(b_r[l][:, 0:w], psG(l)[:, 0:w], ACT.Abs_reciprocal_sqrt,
                                 bias=col(EPSV)).then_inc(S(f"mlp_r3{l}"), 1)
            yield h + 10
            act.wait_ge(S(f"mlp_v{l}"), n + 1)
            nc.scalar.activation(b_sq[l][:, 0:w], b_u[l][:, 0:w], ACT.Square).then_inc(S(f"mlp_q4{l}"), 1)
            yield h + 12
            act.wait_ge(S(f"mlp_j4{l}"), n + 1)
            nc.scalar.activation(b_r[l][:, 0:w], psG(l)[:, 0:w], ACT.Abs_reciprocal_sqrt,
                                 bias=col(EPSV)).then_inc(S(f"mlp_r4{l}"), 1)

        def mlp_dve(dve, h, l, n, w, x1):
            yield h + 7
            dve.wait_ge(S(f"mlp_r3{l}"), n + 1)
            nc.vector.scalar_tensor_tensor(b_u[l][:, 0:w], psA[l][:, 0:w], col(CR), b_r[l][:, 0:w], ALU.add,
                                           ALU.mult).then_inc(S(f"mlp_t{l}"), 1)
            yield h + 9
            dve.wait_ge(S(f"mlp_d{l}"), n + 1)
            nc.vector.scalar_tensor_tensor(b_u[l][:, 0:w], psB[l][:, 0:w], col(CT), x1, ALU.add,
                                           ALU.add).then_inc(S(f"mlp_v{l}"), 1)
            yield h + 13
            dve.wait_ge(S(f"mlp_r4{l}"), n + 1)
            nc.vector.tensor_tensor(b_h[l][:, 0:w], b_u[l][:, 0:w], b_r[l][:, 0:w], ALU.mult).then_inc(S(f"mlp_x2{l}"), 1)

        def dense_pe(pe, l, n):
            yield 0
            pe.wait_ge(S(f"blk_in{l}"), 16 * (n + 1))
            pe.wait_ge(S(f"blk_xo{l}"), n)
            for q in range(4):
                last_t = nc.tensor.transpose(psA[l][:, 128 * q:128 * q + 128], xin[l][:, 128 * q:128 * q + 128], ident[:, :])
            last_t.then_inc(S(f"blk_t1{l}"), 1)
            yield 2
            pe.wait_ge(S(f"blk_u{l}"), n + 1)
            nc.tensor.matmul(psB[l][:, :], blk_c[:, :], b_u[l][:, :], start=True, stop=True).then_inc(S(f"blk_c1{l}"), 1)
            yield 4
            pe.wait_ge(S(f"blk_q1{l}"), n + 1)
            nc.tensor.matmul(psG(l), blk_j[:, :], b_sq[l][:, :], start=True, stop=True).then_inc(S(f"blk_j1{l}"), 1)
            yield 8
            pe.wait_ge(S(f"blk_q2{l}"), n + 1)
            nc.tensor.matmul(psG(l), blk_j[:, :], b_sq[l][:, :], start=True, stop=True).then_inc(S(f"blk_j2{l}"), 1)
            yield from mlp_pe(pe, 10, l, n, 512, 128)

        def dense_act(act, l, n):
            yield 3
            act.wait_ge(S(f"blk_c1{l}"), n + 1)
            nc.scalar.activation(b_sq[l][:, :], psB[l][:, :], ACT.Square).then_inc(S(f"blk_q1{l}"), 1)
            yield 5
            act.wait_ge(S(f"blk_j1{l}"), n + 1)
            nc.scalar.activation(b_r[l][:, :], psG(l), ACT.Abs_reciprocal_sqrt, bias=col(EPSV)).then_inc(S(f"blk_r1{l}"), 1)
            yield 7
            act.wait_ge(S(f"blk_x1{l}"), n + 1)
            nc.scalar.activation(b_sq[l][:, :], b_x1[l][:, :], ACT.Square).then_inc(S(f"blk_q2{l}"), 1)
            yield 9
            act.wait_ge(S(f"blk_j2{l}"), n + 1)
            nc.scalar.activation(b_r[l][:, :], psG(l), ACT.Abs_reciprocal_sqrt, bias=col(EPSV)).then_inc(S(f"blk_r2{l}"), 1)
            yield from mlp_act(act, 10, l, n, 512, 16 * n)

        def dense_dve(dve, l, n):
            yield 1
            dve.wait_ge(S(f"blk_t1{l}"), n + 1)
            nc.vector.tensor_scalar(b_u[l][:, :], psA[l][:, :], col(B0), None, ALU.add).then_inc(S(f"blk_u{l}"), 1)
            yield 6
            dve.wait_ge(S(f"blk_r1{l}"), n + 1)
            nc.vector.tensor_tensor(b_x1[l][:, :], psB[l][:, :], b_r[l][:, :], ALU.mult).then_inc(S(f"blk_x1{l}"), 1)
            yield 10
            dve.wait_ge(S(f"blk_r2{l}"), n + 1)
            nc.vector.scalar_tensor_tensor(b_h[l][:, :], b_x1[l][:, :], col(G1), b_r[l][:, :], ALU.mult,
                                           ALU.mult).then_inc(S(f"mlp_h{l}"), 1)
            yield from mlp_dve(dve, 10, l, n, 512, b_x1[l][:, :])
            yield 25
            dve.wait_ge(S(f"mlp_t9{l}"), n + 1)
            dve.wait_ge(S(f"blk_st{l}"), 16 * n)
            nc.vector.tensor_copy(g_x[l], psA[l][:, :]).then_inc(S(f"blk_xo{l}"), 1)

        g_x = [b_gl[l][:, 512:1024] for l in LANES]

        def dense_load(sp, l, n, row):
            sp.wait_ge(S(f"blk_t1{l}"), n)
            sp.dma_start(xin[l][:, :], x[bass.ds(row, NB), :].rearrange("(p t) d -> p (t d)", p=128)).then_inc(
                S(f"blk_in{l}"), 16)

        def dense_store(sp, l, n, row):
            sp.wait_ge(S(f"blk_xo{l}"), n + 1)
            sp.dma_start(x2tab[bass.ds(row, NB), :].rearrange("(p t) d -> p (t d)", p=128), g_x[l]).then_inc(
                S(f"blk_st{l}"), 16)

        def first_blocks(steps, eng):
            with eng.Fori(0, PAIRS) as i:
                both(steps(eng, 0, i), steps(eng, 1, i))
            both(steps(eng, 1, PAIRS))

        def end_phase(eng, k):
            eng.drain().then_inc(S("phase"), 1)
            eng.wait_ge(S("phase"), 3 * k)

        def scores0_pe(pe, par, i, g):
            yield 0
            pe.wait_ge(S(f"gathered{par}"), 16 * 2 * GC * (i + 1))
            pe.wait_ge(S(f"ea_in{par}"), 16 * (i + 1))
            pe.wait_ge(S("s0_xs"), 2 * g)
            pe.wait_ge(S("s0_xd"), g)
            for q in range(Q):
                nc.tensor.transpose(psA[0][:, P * q:P * q + P], g_s[par][0:P, 128 * q:128 * q + 128], ident[0:P, 0:P])
                nc.tensor.transpose(psB[0][:, P * q:P * q + P], g_d[par][0:P, 128 * q:128 * q + 128], ident[0:P, 0:P])
            nc.tensor.transpose(psG(0)[:, 0:P], ea_s[par][0:P, :], ident[0:P, 0:P]).then_inc(S("s0_t"), 1)
            yield 2
            pe.wait_ge(S("s0_xs"), 2 * (g + 1))
            pe.wait_ge(S("s0_f"), g)
            nc.tensor.matmul(psH(0)[:, 0:EW], wt[:, W1X, :], xin[0][:, 0:EW], start=True, stop=False)
            for q in range(Q):
                last_f = nc.tensor.matmul(psH(0)[:, P * q:P * q + P], w_e[:, q, :], ea_t, start=False, stop=(q == Q - 1))
            last_f.then_inc(S("s0_f_ps"), 1)
            yield 5
            pe.wait_ge(S("s0_ed"), g + 1)
            pe.wait_ge(S("s0_es"), g + 1)
            for q in range(Q):
                o = psG(0)[0:P, 2 * q:2 * q + 2]
                nc.tensor.matmul(o, b_h[0][:, P * q:P * q + P], att[:, 0, :], start=True, stop=False)
                last_s = nc.tensor.matmul(o, b_x1[0][:, P * q:P * q + P], att[:, 1, :], start=False, stop=True)
            last_s.then_inc(S("s0_s_ps"), 1)

        def scores0_act(act, par, i, g):
            yield 1
            act.wait_ge(S("s0_t"), g + 1)
            nc.scalar.activation(xin[0][:, 0:EW], psA[0][:, 0:EW], ACT.Identity).then_inc(S("s0_xs"), 1)
            nc.scalar.activation(ea_t, psG(0)[:, 0:P], ACT.Identity).then_inc(S("s0_xs"), 1)
            yield 3
            act.wait_ge(S("s0_f_ps"), g + 1)
            nc.scalar.activation(b_u[0][:, 0:EW], psH(0)[:, 0:EW], ACT.Identity).then_inc(S("s0_fs"), 1)

        def scores0_dve(dve, par, i, g):
            yield 1
            dve.wait_ge(S("s0_t"), g + 1)
            nc.vector.tensor_copy(xg(g), psB[0][:, 0:EW]).then_inc(S("s0_xd"), 1)
            nc.vector.tensor_copy(xsg(g), g_s[par][0:P, :]).then_inc(S(f"rows0_used{par}"), 1)
            nc.vector.tensor_copy(ix_a[par][:, :], grp(src_i, g + 2))
            nc.vector.tensor_copy(ix_b[par][:, :], grp(dst_i, g + 2)).then_inc(S(f"idx{par}"), 1)
            yield 2
            dve.wait_ge(S("s0_xd"), g + 1)
            nc.vector.scalar_tensor_tensor(b_x1[0][:, 0:EW], xg(g), 0.01, xg(g), ALU.mult, ALU.max).then_inc(S("s0_ed"), 1)
            yield 4
            dve.wait_ge(S("s0_fs"), g + 1)
            nc.vector.scalar_tensor_tensor(b_h[0][:, 0:EW], b_u[0][:, 0:EW], 0.01, b_u[0][:, 0:EW], ALU.mult,
                                           ALU.max).then_inc(S("s0_es"), 1)
            yield 6
            dve.wait_ge(S("s0_s_ps"), g + 1)
            nc.vector.tensor_copy(grp(score, g), psG(0)[0:P, 0:GC]).then_inc(S("s0_f"), 1)

        def carries_pe(pe, k, n):
            pe.wait_ge(S("seg_ends"), k)
            nc.tensor.transpose(psA[0][0:n, 0:P], edge_col[:, 0:n], ident[0:P, 0:P]).then_inc(S("seg_rows_ps"), 1)
            pe.wait_ge(S("seg_rows"), k)
            src_rows = rows[0:n, 0:P] if k % 2 == 1 else rows[0:n, 1:P + 1]
            nc.tensor.transpose(psB[0][0:P, 0:n], src_rows, ident[0:n, 0:n]).then_inc(S("seg_carry_ps"), 1)

        def carries_dve(dve, k, n, flags, start, op0, op1):
            dve.wait_ge(S("seg_rows_ps"), k)
            if k % 2 == 1:
                nc.vector.memset(rows[0:n, 0:1], start)
                o, a, b = rows[0:n, 1:P + 1], row_flags[0:n, flags, :], psA[0][0:n, 0:P]
            else:
                nc.vector.memset(rows[0:n, P:P + 1], start)
                o, a, b = rows[0:n, 0:P][:, ::-1], row_flags[0:n, flags, ::-1], psA[0][0:n, 0:P][:, ::-1]
            nc.vector.tensor_tensor_scan(o, a, b, start, op0, op1).then_inc(S("seg_rows"), 1)
            dve.wait_ge(S("seg_carry_ps"), k)
            nc.vector.tensor_copy(carry[:, 0:n], psB[0][0:P, 0:n]).then_inc(S("seg_carry"), 1)
            dve.wait_ge(S("seg_carry"), k)

        def softmax_dve(dve, m, step):
            k = 6 * m

            def own(ins):
                step[0] += 1
                ins.then_inc(S("seg_step"), 1)
                dve.wait_ge(S("seg_step"), step[0])

            def scan(o, a, b, init, op0, op1, back):
                f = (lambda v: v[:, ::-1]) if back else (lambda v: v)
                own(nc.vector.tensor_tensor_scan(f(o), f(a), f(b), init, op0, op1))

            scan(sm1[:, :], pen_f[:, :], score[:, :], NEG, ALU.add, ALU.max, False)
            nc.vector.tensor_copy(edge_col[:, 0:1], sm1[:, TC - 1:TC]).then_inc(S("seg_ends"), 1)
            carries_dve(dve, k + 1, 1, 2, NEG, ALU.add, ALU.max)
            scan(sm2[:, :], pen_f[:, :], score[:, :], carry[:, 0:1], ALU.add, ALU.max, False)
            scan(sm1[:, :], pen_b[:, :], sm2[:, :], NEG, ALU.add, ALU.max, True)
            nc.vector.tensor_copy(edge_col[:, 0:1], sm1[:, 0:1]).then_inc(S("seg_ends"), 1)
            carries_dve(dve, k + 2, 1, 3, NEG, ALU.add, ALU.max)
            scan(sm1[:, :], pen_b[:, :], sm2[:, :], carry[:, 0:1], ALU.add, ALU.max, True)
            nc.vector.tensor_tensor(sm2[:, :], score[:, :], sm1[:, :], ALU.subtract).then_inc(S("seg_x"), 1)
            dve.wait_ge(S("seg_exp"), m + 1)
            scan(sm1[:, :], same[:, :], score[:, :], 0.0, ALU.mult, ALU.add, False)
            nc.vector.tensor_copy(edge_col[:, 0:1], sm1[:, TC - 1:TC]).then_inc(S("seg_ends"), 1)
            carries_dve(dve, k + 3, 1, 0, 0.0, ALU.mult, ALU.add)
            scan(sm1[:, :], same[:, :], score[:, :], carry[:, 0:1], ALU.mult, ALU.add, False)
            own(nc.vector.tensor_tensor(sm2[:, :], sm1[:, :], last[:, :], ALU.mult))
            scan(sm1[:, :], nxt[:, :], sm2[:, :], 0.0, ALU.mult, ALU.add, True)
            nc.vector.tensor_copy(edge_col[:, 0:1], sm1[:, 0:1]).then_inc(S("seg_ends"), 1)
            carries_dve(dve, k + 4, 1, 1, 0.0, ALU.mult, ALU.add)
            scan(sm1[:, :], nxt[:, :], sm2[:, :], carry[:, 0:1], ALU.mult, ALU.add, True)
            own(nc.vector.reciprocal(sm2[:, :], sm1[:, :]))
            own(nc.vector.tensor_tensor(sm1[:, :], score[:, :], sm2[:, :], ALU.mult))

        def softmax_act(act, m):
            act.wait_ge(S("seg_x"), m + 1)
            nc.scalar.activation(score[:, :], sm2[:, :], ACT.Exp).then_inc(S("seg_exp"), 1)

        def sums_dve(dve, m, step):
            k = 6 * m

            def own(ins):
                step[0] += 1
                ins.then_inc(S("seg_step"), 1)
                dve.wait_ge(S("seg_step"), step[0])

            own(nc.vector.tensor_tensor(ag[0:P, :, :], xsn[0:P, :, :].rearrange("p t d -> p d t"),
                                        sm1[:, :].unsqueeze(1).broadcast_to((P, D, TC)), ALU.mult))
            def scan_all(flags, back):
                def scan(a, f):
                    nc.vector.tensor_tensor_scan(a, f, a, 0.0, ALU.mult, ALU.add)
                if back:
                    for d in range(D):
                        scan(ag[0:P, d, ::-1], flags[:, ::-1])
                else:
                    U = 8
                    with dve.Fori(0, D // U) as i:
                        for u in range(U):
                            scan(ag[0:P, bass.ds(i * U + u, 1), :].rearrange("p o t -> p (o t)"), flags[:, :])
                own(dve.drain())

            def add_carry(run):
                U = 8
                with dve.Fori(0, D // U) as i:
                    for u in range(U):
                        a = ag[0:P, bass.ds(i * U + u, 1), :].rearrange("p o t -> p (o t)")
                        nc.vector.scalar_tensor_tensor(a, run[:, :], carry[:, bass.ds(i * U + u, 1)], a, ALU.mult, ALU.add)
                own(dve.drain())

            run_f, run_b = score, sm2
            nc.vector.tensor_tensor_scan(run_f[:, :], same[:, :], zero[0:P, 0:TC], 1.0, ALU.mult, ALU.add)
            own(nc.vector.tensor_tensor_scan(run_b[:, ::-1], nxt[:, ::-1], zero[0:P, 0:TC], 1.0, ALU.mult, ALU.add))
            scan_all(same, False)
            nc.vector.tensor_copy(edge_col[:, :], ag[0:P, :, TC - 1]).then_inc(S("seg_ends"), 1)
            carries_dve(dve, k + 5, D, 0, 0.0, ALU.mult, ALU.add)
            add_carry(run_f)
            own(nc.vector.tensor_tensor(ag[0:P, :, :], ag[0:P, :, :], last[:, :].unsqueeze(1).broadcast_to((P, D, TC)), ALU.mult))
            scan_all(nxt, True)
            nc.vector.tensor_copy(edge_col[:, :], ag[0:P, :, 0]).then_inc(S("seg_ends"), 1)
            carries_dve(dve, k + 6, D, 1, 0.0, ALU.mult, ALU.add)
            add_carry(run_b)

        def x1_pe(pe, n, xsrc, w):
            yield 3
            pe.wait_ge(S("ln_at"), n + 1)
            nc.tensor.matmul(psB[0][:, 0:EW], blk_c[:, :], xsrc, start=True, stop=False)
            nc.tensor.matmul(psB[0][:, 0:EW], w, b_u[0][:, 0:EW], start=False, stop=True).then_inc(S("ln_c"), 1)
            yield 5
            pe.wait_ge(S("ln_q"), n + 1)
            nc.tensor.matmul(psG(0)[:, 0:EW], blk_j[:, :], b_sq[0][:, 0:EW], start=True, stop=True).then_inc(S("ln_j"), 1)

        def x1_act(act, n, bias):
            yield 4
            act.wait_ge(S("ln_c"), n + 1)
            nc.scalar.activation(b_sq[0][:, 0:EW], psB[0][:, 0:EW], ACT.Square, bias=bias).then_inc(S("ln_q"), 1)
            yield 6
            act.wait_ge(S("ln_j"), n + 1)
            nc.scalar.activation(b_r[0][:, 0:EW], psG(0)[:, 0:EW], ACT.Abs_reciprocal_sqrt,
                                 bias=col(EPSV)).then_inc(S("ln_r"), 1)

        def dst1_pe(pe, par, i, g):
            yield 1
            pe.wait_ge(S("ln_rows"), g + 1)
            for q in range(Q):
                last_t = nc.tensor.transpose(psA[0][:, P * q:P * q + P], g_s[par][0:P, 128 * q:128 * q + 128], ident[0:P, 0:P])
            last_t.then_inc(S("ln_t"), 1)
            yield from x1_pe(pe, g, xg(g), wt[:, A2C, :])
            yield 8
            pe.wait_ge(S("d1_x1"), g + 1)
            pe.wait_ge(S("d1_s"), g)
            for q in range(Q):
                last_s = nc.tensor.matmul(psH(0)[0:P, 2 * q:2 * q + 2], b_h[0][:, P * q:P * q + P], att[:, 3, :],
                                          start=True, stop=True)
            last_s.then_inc(S("d1_s_ps"), 1)

        def dst1_act(act, par, i, g):
            yield 2
            act.wait_ge(S("ln_t"), g + 1)
            nc.scalar.activation(b_u[0][:, 0:EW], psA[0][:, 0:EW], ACT.Identity).then_inc(S("ln_at"), 1)
            yield from x1_act(act, g, col(CB0))
            yield 8
            act.wait_ge(S("d1_x1"), g + 1)
            nc.scalar.activation(xg(g), b_h[0][:, 0:EW], ACT.Identity).then_inc(S("d1_kept"), 1)

        def dst1_dve(dve, par, i, g):
            yield 0
            dve.wait_ge(S(f"agg0_sent{par}"), 16 * GC * i)
            dve.wait_ge(S("ln_t"), g)
            nc.vector.tensor_copy(t3(g_s[par][0:P, :]), ag[0:P, :, bass.ds(g * GC, GC)].rearrange("p d t -> p t d")).then_inc(
                S("ln_rows"), 1)
            nc.vector.tensor_copy(ix_a[par][:, :], grp(last_i, g)).then_inc(S("d1_idx"), 1)
            yield 7
            dve.wait_ge(S("ln_r"), g + 1)
            dve.wait_ge(S("d1_kept"), g)
            nc.vector.scalar_tensor_tensor(b_h[0][:, 0:EW], psB[0][:, 0:EW], col(CB0), b_r[0][:, 0:EW], ALU.add,
                                           ALU.mult).then_inc(S("d1_x1"), 1)
            yield 9
            dve.wait_ge(S("d1_s_ps"), g + 1)
            nc.vector.tensor_copy(grp(score, g), psH(0)[0:P, 0:GC]).then_inc(S("d1_s"), 1)

        def src1_pe(pe, par, i, g):
            yield 1
            pe.wait_ge(S(f"gathered{par}"), 16 * GC * (2 * of_parity(par) + i + 1))
            pe.wait_ge(S("ln_rows"), NGR + g + 1)
            pe.wait_ge(S("s1_msg"), g)
            for q in range(Q):
                nc.tensor.transpose(psA[0][:, P * q:P * q + P], xin[0][0:P, 128 * q:128 * q + 128], ident[0:P, 0:P])
                last_t = nc.tensor.transpose(psB[0][:, P * q:P * q + P], g_s[par][0:P, 128 * q:128 * q + 128], ident[0:P, 0:P])
            last_t.then_inc(S("ln_t"), 1)
            yield from x1_pe(pe, NGR + g, b_x1[0][:, 0:EW], wt[:, A2C, :])
            yield 8
            pe.wait_ge(S("s1_x1"), g + 1)
            pe.wait_ge(S("s1_s"), g)
            for q in range(Q):
                lhs = b_h[0][:, P * q:P * q + P]
                nc.tensor.matmul(psH(0)[0:P, 2 * q:2 * q + 2], lhs, att[:, 2, :], start=True, stop=True)
                nc.tensor.matmul(psA[0][0:P, 128 * q:128 * q + 128], lhs, wt[:, PHY, :], start=True, stop=True)
                last_m = nc.tensor.matmul(psG(0)[0:P, 128 * q:128 * q + 128], lhs, wt[:, NEU, :], start=True, stop=True)
            last_m.then_inc(S("s1_m_ps"), 1)

        def src1_act(act, par, i, g):
            yield 2
            act.wait_ge(S("ln_t"), NGR + g + 1)
            nc.scalar.activation(b_x1[0][:, 0:EW], psA[0][:, 0:EW], ACT.Identity)
            nc.scalar.activation(b_u[0][:, 0:EW], psB[0][:, 0:EW], ACT.Identity).then_inc(S("ln_at"), 1)
            yield from x1_act(act, NGR + g, col(CB0))

        def src1_dve(dve, par, i, g):
            yield 0
            dve.wait_ge(S("ln_t"), NGR + g)
            nc.vector.tensor_copy(xin[0][0:P, :], xsg(g)).then_inc(S("ln_rows"), 1)
            yield 2
            dve.wait_ge(S("ln_t"), NGR + g + 1)
            nc.vector.tensor_copy(ix_b[par][:, :], grp(src_i, g + 2)).then_inc(S(f"idx{par}"), 1)
            yield 7
            dve.wait_ge(S("ln_r"), NGR + g + 1)
            nc.vector.scalar_tensor_tensor(b_h[0][:, 0:EW], psB[0][:, 0:EW], col(CB0), b_r[0][:, 0:EW], ALU.add,
                                           ALU.mult).then_inc(S("s1_x1"), 1)
            yield 9
            dve.wait_ge(S("s1_m_ps"), g + 1)
            nc.vector.tensor_tensor(grp(score, g), psH(0)[0:P, 0:GC], grp(score, g), ALU.add).then_inc(S("s1_s"), 1)
            nc.vector.tensor_tensor(t3(b_gl[0][0:P, 0:512]), t3(psA[0][0:P, :]), bc(grp(ew, g), D), ALU.mult).then_inc(
                S("s1_phys"), 1)
            dve.wait_ge(S("s1_phys"), g + 1)
            nc.vector.tensor_tensor(xsg(g), psG(0)[0:P, :], b_gl[0][0:P, 0:512], ALU.add).then_inc(S("s1_msg"), 1)

        def unique_pe(pe, n):
            pe.wait_ge(S("msg_sf"), n + 1)
            for k in range(GC):
                o = psGH[0][0:P, 512 * (k // 4) + P * (k % 4):512 * (k // 4) + P * (k % 4) + P]
                last_b = nc.tensor.matmul(o, sf[:, k:k + 1].broadcast_to((P, P)), ident[0:P, 0:P], start=True, stop=True)
            last_b.then_inc(S("msg_src_ps"), 1)

        def summed_pe(pe, n, o):
            pe.wait_ge(S("msg_same"), n + 1)
            pe.wait_ge(S("msg_zs"), n + 1)
            for k in range(GC):
                last_z = nc.tensor.matmul(o[0:P, D * k:D * k + D], same_src[0:P, P * k:P * k + P], zs[0:P, D * k:D * k + D],
                                          start=True, stop=True)
            last_z.then_inc(S("msg_z_ps"), 1)

        def same_dve(dve, n):
            dve.wait_ge(S("msg_src_ps"), n + 1)
            for b in range(2):
                last_m = nc.vector.tensor_tensor(t3(same_src[0:P, 4 * P * b:4 * P * b + 4 * P], 4),
                                                 t3(psGH[0][0:P, 512 * b:512 * b + 4 * P], 4),
                                                 bc(sf[:, 4 * b:4 * b + 4], P), ALU.is_equal)
            last_m.then_inc(S("msg_same"), 1)

        def dst2_pe(pe, par, i, g):
            yield 1
            pe.wait_ge(S("ln_rows"), 2 * NGR + g + 1)
            for q in range(Q):
                last_t = nc.tensor.transpose(psA[0][:, P * q:P * q + P], g_s[par][0:P, 128 * q:128 * q + 128], ident[0:P, 0:P])
            last_t.then_inc(S("ln_t"), 1)
            yield from x1_pe(pe, 2 * NGR + g, xg(g), blk_c[:, :])
            yield from mlp_pe(pe, 7, 0, PAIRS + g, EW, P)
            yield 21
            for q in range(Q):
                last_z = nc.tensor.matmul(psB[0][0:P, 128 * q:128 * q + 128], b_h[0][:, P * q:P * q + P], wt[:, L2W, :],
                                          start=True, stop=True)
            last_z.then_inc(S("e2_msg_ps"), 1)
            unique_pe(pe, g)
            yield 24
            pe.wait_ge(S("e2_xrow"), g + 1)
            summed_pe(pe, g, psA[0])

        def dst2_act(act, par, i, g):
            yield 2
            act.wait_ge(S("ln_t"), 2 * NGR + g + 1)
            nc.scalar.activation(b_u[0][:, 0:EW], psA[0][:, 0:EW], ACT.Gelu).then_inc(S("ln_at"), 1)
            yield 4
            act.wait_ge(S("ln_c"), 2 * NGR + g + 1)
            nc.scalar.activation(b_sq[0][:, 0:EW], psB[0][:, 0:EW], ACT.Square).then_inc(S("ln_q"), 1)
            yield 6
            act.wait_ge(S("ln_j"), 2 * NGR + g + 1)
            nc.scalar.activation(b_r[0][:, 0:EW], psG(0)[:, 0:EW], ACT.Abs_reciprocal_sqrt,
                                 bias=col(EPSV)).then_inc(S("ln_r"), 1)
            yield from mlp_act(act, 7, 0, PAIRS + g, EW)
            yield 21
            act.wait_ge(S("mlp_x20"), PAIRS + g + 1)
            nc.scalar.activation(xg(g), b_h[0][:, 0:EW], ACT.Identity).then_inc(S("e2_kept"), 1)

        def dst2_dve(dve, par, i, g):
            yield 0
            dve.wait_ge(S("ln_t"), 2 * NGR + g)
            nc.vector.tensor_copy(t3(g_s[par][0:P, :]), ag[0:P, :, bass.ds(g * GC, GC)].rearrange("p d t -> p t d")).then_inc(
                S("ln_rows"), 1)
            dve.wait_ge(S("e2_idx"), 4 * g)
            nc.vector.tensor_copy(sf[:, :], grp(src_i, g)).then_inc(S("msg_sf"), 1)
            yield 7
            dve.wait_ge(S("ln_r"), 2 * NGR + g + 1)
            nc.vector.scalar_tensor_tensor(b_h[0][:, 0:EW], psB[0][:, 0:EW], col(G1), b_r[0][:, 0:EW], ALU.mult,
                                           ALU.mult).then_inc(S("mlp_h0"), 1)
            yield from mlp_dve(dve, 7, 0, PAIRS + g, EW, xg(g))
            yield 22
            dve.wait_ge(S("mlp_t90"), PAIRS + g + 1)
            dve.wait_ge(S(f"x2_sent{par}"), 16 * GC * i)
            nc.vector.tensor_copy(ix_a[par][:, :], grp(last_i, g))
            nc.vector.tensor_copy(xrow[par][0:P, :], psA[0][0:P, :]).then_inc(S("e2_xrow"), 1)
            dve.wait_ge(S("e2_msg_ps"), g + 1)
            nc.vector.tensor_tensor(t3(zs[0:P, :]), t3(psB[0][0:P, :]), bc(grp(dis, g), D), ALU.mult).then_inc(S("msg_zs"), 1)
            yield 23
            same_dve(dve, g)
            dve.wait_ge(S("msg_same"), g + 1)
            nc.vector.tensor_tensor(t3(dup[0:P, :]), t3(same_src[0:P, :]), low[0:P, 0:P].unsqueeze(1).broadcast_to((P, GC, P)),
                                    ALU.mult).then_inc(S("e2_idx"), 1)
            dve.wait_ge(S("e2_idx"), 4 * g + 1)
            nc.vector.tensor_reduce(cnt[:, :], t3(dup[0:P, :]), AX.X, ALU.add).then_inc(S("e2_idx"), 1)
            dve.wait_ge(S("e2_idx"), 4 * g + 2)
            nc.vector.tensor_scalar(cnt[:, :], cnt[:, :], 1.0, float(SKIP), ALU.min, ALU.mult)
            nc.vector.scalar_tensor_tensor(sf[:, :], sf[:, :], float(K), chain_of[:, :], ALU.mult, ALU.add).then_inc(
                S("e2_idx"), 1)
            dve.wait_ge(S("e2_idx"), 4 * g + 3)
            for c in range(K):
                dve.wait_ge(S(f"added{c}{par}"), 16 * (GC // K) * i)
            nc.vector.tensor_tensor(grp(acc_i, g), cnt[:, :], sf[:, :], ALU.add)
            nc.vector.tensor_tensor(ix_b[par][:, :], cnt[:, :], sf[:, :], ALU.add).then_inc(S("e2_idx"), 1)
            dve.wait_ge(S("msg_z_ps"), g + 1)
            nc.vector.tensor_copy(zrow[par][0:P, :], psA[0][0:P, :]).then_inc(S("msg_zrow"), 1)

        def dst3_pe(pe, par, i, g):
            yield 1
            pe.wait_ge(S("ln_rows"), 3 * NGR + g + 1)
            for q in range(Q):
                last_t = nc.tensor.transpose(psA[0][:, P * q:P * q + P], xin[0][0:P, 128 * q:128 * q + 128], ident[0:P, 0:P])
            last_t.then_inc(S("ln_t"), 1)
            yield from x1_pe(pe, 3 * NGR + g, xg(g), blk_c[:, :])
            yield 8
            pe.wait_ge(S("e3_x3"), g + 1)
            for q in range(Q):
                last_t = nc.tensor.transpose(psA[0][0:P, 128 * q:128 * q + 128], b_h[0][:, P * q:P * q + P], ident[:, :])
            last_t.then_inc(S("e3_t9"), 1)
            unique_pe(pe, NGR + g)
            yield 10
            summed_pe(pe, NGR + g, psB[0])

        def dst3_act(act, par, i, g):
            yield 2
            act.wait_ge(S("ln_t"), 3 * NGR + g + 1)
            nc.scalar.activation(b_u[0][:, 0:EW], psA[0][:, 0:EW], ACT.Identity).then_inc(S("ln_at"), 1)
            yield from x1_act(act, 3 * NGR + g, col(C2))

        def dst3_dve(dve, par, i, g):
            yield 0
            dve.wait_ge(S(f"gathered{par}"), 16 * GC * (3 * of_parity(par) + i + 1))
            a = g_a[par][0:P, :].rearrange("p (c k d) -> p c k d", c=GC, k=K)
            nc.vector.tensor_tensor(t3(b_gl[0][0:P, 0:512]), a[:, :, 0, :], a[:, :, 1, :], ALU.add).then_inc(S("e3_sum"), 1)
            nc.vector.tensor_copy(ix_a[par][:, :], grp(dst_i, g + 2)).then_inc(S(f"idx{par}"), 1)
            nc.vector.tensor_copy(sf[:, :], grp(src_i, g)).then_inc(S("msg_sf"), 1)
            dve.wait_ge(S("e3_sum"), g + 1)
            nc.vector.tensor_tensor(t3(xin[0][0:P, :]), t3(b_gl[0][0:P, 0:512]), bc(grp(dis, g), D), ALU.mult).then_inc(
                S("ln_rows"), 1)
            yield 7
            dve.wait_ge(S("ln_r"), 3 * NGR + g + 1)
            nc.vector.scalar_tensor_tensor(b_h[0][:, 0:EW], psB[0][:, 0:EW], col(C2), b_r[0][:, 0:EW], ALU.add,
                                           ALU.mult).then_inc(S("e3_x3"), 1)
            yield 9
            dve.wait_ge(S("e3_t9"), g + 1)
            nc.vector.tensor_tensor(t3(zs[0:P, :]), t3(psA[0][0:P, :]), bc(grp(ew, g), D), ALU.mult).then_inc(S("msg_zs"), 1)
            same_dve(dve, NGR + g)
            yield 11
            dve.wait_ge(S("msg_z_ps"), NGR + g + 1)
            for c in range(K):
                dve.wait_ge(S(f"added{c}{par}"), 16 * (GC // K) * (of_parity(par) + i))
            nc.vector.tensor_copy(ix_b[par][:, :], grp(acc_i, g))
            nc.vector.tensor_copy(zrow[par][0:P, :], psB[0][0:P, :]).then_inc(S("msg_zrow"), 1)

        at_[0] = 0
        l_x2 = [in_ag(R * D) for _ in LANES]
        l_a2 = [in_ag(R * K * D) for _ in LANES]
        l_a3 = [in_ag(R * K * D) for _ in LANES]
        xt_[0] = 0
        l_dis = [in_xsn(R) for _ in LANES]
        l_s2 = [in_xsn(R * D) for _ in LANES]
        l_s3 = [in_xsn(R * D) for _ in LANES]
        l_out = [in_xsn(R * D) for _ in LANES]
        l_u = in_xsn(R * D)
        l_st = in_xsn(R * 6)
        l_m, l_d, l_v, l_rs = (in_xsn(R) for _ in range(4))

        def tiles(eng, body):
            with eng.Fori(0, NTILE // 2) as i:
                body(eng, 0, i, 2 * i, 2 * i * NT)
                body(eng, 1, i, 2 * i + 1, (2 * i + 1) * NT)
            body(eng, 0, NTILE // 2, NTILE - 1, N - NT)

        def t3r(a):
            return a.rearrange("p (r d) -> p r d", r=R)

        def last_load(sp, par, i, n, row):
            sp.wait_ge(S(f"l_used{par}"), i)
            for t, a in ((x2tab, l_x2), (acc2, l_a2), (acc3, l_a3)):
                sp.dma_start(a[par], t[bass.ds(row, NT), :].rearrange("(p r) d -> p (r d)", p=128)).then_inc(S(f"l_in{par}"), 16)
            sp.dma_start(l_dis[par], distab[bass.ds(row, NT)].rearrange("(p r) -> p r", p=128)).then_inc(S(f"l_in{par}"), 16)

        def last_pool(pool, par, i, n, row):
            pool.wait_ge(S(f"l_in{par}"), 64 * (i + 1))
            pool.wait_ge(S(f"l_used{par}"), i)
            pool.sem_inc(S("pool_turn"))
            a2 = l_a2[par].rearrange("p (r k d) -> p r k d", r=R, k=K)
            a3 = l_a3[par].rearrange("p (r k d) -> p r k d", r=R, k=K)
            nc.gpsimd.tensor_tensor(t3r(l_s2[par]), a2[:, :, 0, :], a2[:, :, 1, :], ALU.add).then_inc(S(f"l_sums{par}"), 1)
            nc.gpsimd.tensor_tensor(t3r(l_s3[par]), a3[:, :, 0, :], a3[:, :, 1, :], ALU.add).then_inc(S(f"l_sums{par}"), 1)

        def last_act(act, par, i, n, row):
            for m in range(2):
                act.wait_ge(S("l_var"), 2 * n + m + 1)
                nc.scalar.activation(l_rs, l_v, ACT.Abs_reciprocal_sqrt, bias=col(EPSV)).then_inc(S("l_rstd"), 1)

        def last_dve(dve, par, i, n, row):
            C = 14
            k = [0]

            def own(ins):
                k[0] += 1
                ins.then_inc(S("l_step"), 1)
                dve.wait_ge(S("l_step"), C * n + k[0])

            def norm(m, o):
                for r in range(R):
                    st = nc.vector.bn_stats(l_st[:, 6 * r:6 * r + 6], l_u[:, D * r:D * r + D])
                own(st)
                s = l_st.rearrange("p (r c) -> p r c", c=6)
                me, ve, mo, vo = s[:, :, 1], s[:, :, 2], s[:, :, 4], s[:, :, 5]
                nc.vector.tensor_tensor(l_d, me, mo, ALU.subtract)
                nc.vector.tensor_tensor(l_m, me, mo, ALU.add)
                own(nc.vector.tensor_tensor(l_v, ve, vo, ALU.add))
                own(nc.vector.tensor_tensor(l_d, l_d, l_d, ALU.mult))
                own(nc.vector.tensor_scalar(l_d, l_d, 0.25, None, ALU.mult))
                nc.vector.scalar_tensor_tensor(l_v, l_v, 1.0 / D, l_d, ALU.mult, ALU.add).then_inc(S("l_var"), 1)
                own(nc.vector.tensor_scalar(l_m, l_m, -0.5, None, ALU.mult))
                dve.wait_ge(S("l_rstd"), 2 * n + m + 1)
                for r in range(R):
                    ap = nc.vector.tensor_scalar(o[:, D * r:D * r + D], l_u[:, D * r:D * r + D], l_m[:, r:r + 1],
                                                 l_rs[:, r:r + 1], ALU.add, ALU.mult)
                return ap

            dve.wait_ge(S(f"l_sums{par}"), 2 * (i + 1))
            own(nc.vector.tensor_tensor(t3r(l_u), t3r(l_s2[par]), bc(l_dis[par], D), ALU.mult))
            own(nc.vector.tensor_tensor(l_u, l_u, l_x2[par], ALU.add))
            own(nc.vector.tensor_tensor(t3r(l_u), t3r(l_u), b2_row[:, :].unsqueeze(1).broadcast_to((128, R, D)), ALU.add))
            own(norm(0, l_u))
            nc.vector.tensor_tensor(l_u, l_u, l_s3[par], ALU.add).then_inc(S(f"l_used{par}"), 1)
            dve.wait_ge(S(f"l_used{par}"), i + 1)
            dve.wait_ge(S(f"l_out{par}"), 16 * i)
            norm(1, l_out[par]).then_inc(S("l_done"), 1)
            dve.wait_ge(S("l_done"), n + 1)
            assert k[0] == C

        def last_store(sp, par, i, n, row):
            sp.wait_ge(S("l_done"), n + 1)
            if isinstance(n, int) and n == NTILE - 1:
                for l in LANES:
                    sp.wait_ge(S(f"l_out{l}"), 16 * (NTILE // 2))
            sp.dma_start(out[bass.ds(row, NT), :].rearrange("(p r) d -> p (r d)", p=128), l_out[par]).then_inc(
                S(f"l_out{par}"), 16)

        VECS = ((B0, bias0), (G1, ln1_g), (LB1, ln1_b), (G2, ln2_g), (LB2, ln2_b), (MB2, mlp_b2), (L2B, L2_b))
        MATS = ((0, W2), (1, W1[:, 0:D]), (2, W_phys), (3, W_neur), (4, L2_W))

        @block.sync
        def _(sp):
            sp.wait_ge(S("cleared"), 1)
            n = 0

            def get(o, a):
                nonlocal n
                sp.dma_start(o, a).then_inc(S("loaded"), 16)
                n += 16

            for v, a in VECS:
                for h in range(2):
                    get(vec[64 * h:64 * h + 64, v:v + 1], a.rearrange("(d o) -> d o", o=1))
            get(col(MB1), mlp_b1.rearrange("(d o) -> d o", o=1))
            get(col(FUS), fusion.rearrange("(a o) -> a o", o=1).broadcast_to((128, 1)))
            for m, a in MATS:
                for h in range(2):
                    get(wbd[64 * h:64 * h + 64, m, 64 * h:64 * h + 64], a)
            for h in range(2):
                get(w1d[:, 64 * h:64 * h + 64], mlp_w1)
                for m, a in ((0, attn[0:D]), (1, attn[D:2 * D]), (2, att_w[0:D]), (3, att_w[D:2 * D])):
                    get(att[64 * h:64 * h + 64, m, h:h + 1], a.rearrange("(d o) -> d o", o=1))
            get(w2s[0:D, :], mlp_w2)
            get(w1e_s[0:D, :], W1[:, D:D + DE])
            get(b2_row[:, :], L2_b.rearrange("(o d) -> o d", o=1).broadcast_to((128, D)))
            get(src_i[:, 0:TC], src.rearrange("(p t) -> p t", p=P))
            get(dst_i[:, 0:TC], dst.rearrange("(p t) -> p t", p=P))
            get(ew[:, :], edge_weight.rearrange("(p t) -> p t", p=P))
            prev_i, next_i = prev_f.bitcast(i32), next_f.bitcast(i32)
            get(prev_i[1:P, :], dst[TC - 1:E - 1].rearrange("(p t) -> p t", t=TC))
            get(prev_i[0:1, 1:TC], dst[0:TC - 1].rearrange("(o t) -> o t", o=1))
            get(next_i[0:P - 1, :], dst[1:E - TC + 1].rearrange("(p t) -> p t", t=TC))
            get(next_i[P - 1:P, 0:TC - 1], dst[E - TC + 1:E].rearrange("(o t) -> o t", o=1))
            assert n == LOADED

            def fill(table, cols):
                v = table.rearrange("n d -> (n d)").rearrange("(p r f) -> p r f", p=128, f=250)
                sp.dma_start(v, zero[:, :].unsqueeze(1).broadcast_to((128, N * cols // 128 // 250, 250))).then_inc(
                    S(f"zeroed_{cols}_{len(fills)}"), 16)
                fills.append(1)

            fills = []
            fill(agg0, D)
            sp.wait_ge(S("w1e_t"), 1)
            for c in range(GC):
                sp.dma_start(w_e[DE * c:DE * c + DE, c // 2, 64 * (c % 2):64 * (c % 2) + 64], w1e_t[0:DE, :]).then_inc(
                    S("w_e_in"), 16)
            sp.wait_ge(S("dis_made"), 1)
            sp.dma_start(distab.rearrange("(p h) -> p h", p=128), deg).then_inc(S("dis_out"), 16)

            dense_load(sp, 0, 0, 0)
            dense_load(sp, 1, 0, NB)
            with sp.Fori(0, PAIRS - 1) as i:
                for l in LANES:
                    dense_load(sp, l, i + 1, (2 * i + 2 + l) * NB)
                for l in LANES:
                    dense_store(sp, l, i, (2 * i + l) * NB)
            dense_load(sp, 1, PAIRS, 2 * PAIRS * NB)
            for l in LANES:
                dense_store(sp, l, PAIRS - 1, (2 * PAIRS - 2 + l) * NB)
            dense_store(sp, 1, PAIRS, 2 * PAIRS * NB)

            eav = edge_attr.rearrange("(p t) d -> p (t d)", p=P)
            for loop in range(LOOPS):
                def body(par, i, g, loop=loop):
                    dense_load(sp, 1, run1(loop, g), row1(loop, g))
                    if loop == 0:
                        sp.wait_ge(S(f"rows0_used{par}"), i)
                        sp.dma_start(ea_s[par][0:P, :], eav[:, bass.ds(g * (GC * DE), GC * DE)]).then_inc(S(f"ea_in{par}"), 16)
                    if loop == LOOPS - 1 and isinstance(g, int) and g == NGR - 1:
                        sp.wait_ge(S("blk_st1"), 16 * run1(loop, g))
                    dense_store(sp, 1, run1(loop, g), row1(loop, g))
                groups(sp, body)
                if loop < 2:
                    fill((acc2, acc3)[loop], K * D)

            for c in range(K):
                for par in LANES:
                    sp.wait_ge(S(f"added{c}{par}"), 2 * 16 * (GC // K) * of_parity(par))
            last_load(sp, 0, 0, 0, 0)
            last_load(sp, 1, 0, 1, NT)
            with sp.Fori(0, NTILE // 2 - 1) as i:
                for par in LANES:
                    last_store(sp, par, i, 2 * i + par, (2 * i + par) * NT)
                    last_load(sp, par, i + 1, 2 * i + 2 + par, (2 * i + 2 + par) * NT)
            i = NTILE // 2 - 1
            last_store(sp, 0, i, 2 * i, 2 * i * NT)
            last_load(sp, 0, i + 1, NTILE - 1, N - NT)
            last_store(sp, 1, i, 2 * i + 1, (2 * i + 1) * NT)
            last_store(sp, 0, i + 1, NTILE - 1, N - NT)
            sp.wait_ge(S("l_out0"), 16 * (NTILE // 2 + 1))
            sp.wait_ge(S("l_out1"), 16 * (NTILE // 2))

        @block.gpsimd
        def _(pool):
            nc.gpsimd.memset(ident[:, :], 1.0).then_inc(S("pool_c"), 1)
            nc.gpsimd.memset(low[:, :], 1.0).then_inc(S("pool_c"), 1)
            pool.wait_ge(S("pool_c"), 2)
            nc.gpsimd.affine_select(out=ident[:, :], in_=ident[:, :], pattern=[[-1, 128]], compare_op=ALU.is_equal, fill=0.0,
                                    base=0, channel_multiplier=1).then_inc(S("pool_c"), 1)
            nc.gpsimd.affine_select(out=low[:, :], in_=low[:, :], pattern=[[-1, 128]], compare_op=ALU.is_gt, fill=0.0,
                                    base=0, channel_multiplier=1).then_inc(S("pool_c"), 1)
            nc.gpsimd.iota(iota_lo, pattern=[[1, 128]], base=0, channel_multiplier=0,
                           allow_small_or_imprecise_dtypes=True).then_inc(S("pool_c"), 1)
            nc.gpsimd.iota(iota_hi, pattern=[[1, HB]], base=0, channel_multiplier=0,
                           allow_small_or_imprecise_dtypes=True).then_inc(S("pool_c"), 1)
            nc.gpsimd.iota(chain_of[:, :], pattern=[[0, GC // K], [1, K]], base=0, channel_multiplier=0,
                           allow_small_or_imprecise_dtypes=True).then_inc(S("pool_c"), 1)

            def at(ap):
                return bass.IndirectOffsetOnAxis(ap=ap, axis=0)

            def gather(o, table, ix, s):
                pool.indirect_dma_start(out=o, out_offset=None, in_=table, in_offset=at(ix)).then_inc(s, 16)

            def scatter(table, rows_n, ix, a, s, add=False):
                kw = dict(compute_op=ALU.add) if add else {}
                pool.indirect_dma_start(out=table, out_offset=at(ix), in_=a, in_offset=None, bounds_check=rows_n - 1,
                                        oob_is_err=False, **kw).then_inc(s, 16)

            def cols(a, k, w=D):
                return a[0:P, w * k:w * k + w]

            def g0(par, i, g):
                pool.wait_ge(S(f"idx{par}"), i + 1)
                pool.wait_ge(S(f"rows0_used{par}"), i)
                pool.sem_inc(S("pool_turn"))
                for k in range(GC):
                    gather(cols(g_s[par], k), x, ix_a[par][:, k:k + 1], S(f"gathered{par}"))
                    gather(cols(g_d[par], k), x, ix_b[par][:, k:k + 1], S(f"gathered{par}"))
            groups(pool, g0)

            pool.wait_ge(S("dis_out"), 16)
            pool.wait_ge(S("w_made"), 1)
            for t in range(TC):
                gather(dis[:, t:t + 1], distab.rearrange("(n o) -> n o", o=1), dst_i[:, t:t + 1], S("dis_in"))

            def s1(par, i, g):
                pool.wait_ge(S("d1_idx"), g + 1)
                pool.sem_inc(S("pool_turn"))
                for k in range(GC):
                    scatter(agg0, N, ix_a[par][:, k:k + 1], cols(g_s[par], k), S(f"agg0_sent{par}"))
            pool.wait_ge(S(f"zeroed_{D}_0"), 16)
            groups(pool, s1)

            for par in LANES:
                pool.wait_ge(S(f"agg0_sent{par}"), 16 * GC * of_parity(par))

            def g3(par, i, g):
                pool.wait_ge(S(f"idx{par}"), of_parity(par) + 1 + i + 1)
                pool.sem_inc(S("pool_turn"))
                for k in range(GC):
                    gather(cols(g_s[par], k), agg0, ix_b[par][:, k:k + 1], S(f"gathered{par}"))
            groups(pool, g3)

            for l in LANES:
                pool.wait_ge(S(f"blk_st{l}"), 16 * (PAIRS if l == 0 else run1(LOOPS, 0)))
            pool.wait_ge(S(f"zeroed_{K * D}_1"), 16)

            def chain_wait(layer, c, par, i, k):
                if k >= K:
                    pool.wait_ge(S(f"added{c}{par}"), 16 * ((GC // K) * (layer * of_parity(par) + i) + k // K))
                elif par == 0:
                    pool.wait_ge(S(f"added{c}1"), 16 * (GC // K) * (layer * of_parity(1) + i))
                else:
                    pool.wait_ge(S(f"added{c}0"), 16 * (GC // K) * (layer * of_parity(0) + i + 1))
                pool.sem_inc(S("pool_turn"))

            def s2(par, i, g):
                pool.wait_ge(S("e2_xrow"), g + 1)
                pool.sem_inc(S("pool_turn"))
                for k in range(GC // 2):
                    scatter(x2tab, N, ix_a[par][:, k:k + 1], cols(xrow[par], k), S(f"x2_sent{par}"))
                pool.wait_ge(S("msg_zrow"), g + 1)
                for k in range(GC):
                    chain_wait(0, k % K, par, i, k)
                    scatter(acc2_rows, N * K, ix_b[par][:, k:k + 1], cols(zrow[par], k), S(f"added{k % K}{par}"), add=True)
                    if k % 2:
                        j = GC // 2 + k // 2
                        scatter(x2tab, N, ix_a[par][:, j:j + 1], cols(xrow[par], j), S(f"x2_sent{par}"))
            groups(pool, s2)

            for c in range(K):
                for par in LANES:
                    pool.wait_ge(S(f"added{c}{par}"), 16 * (GC // K) * of_parity(par))
            for par in LANES:
                pool.wait_ge(S(f"x2_sent{par}"), 16 * GC * of_parity(par))
            pool.wait_ge(S(f"zeroed_{K * D}_2"), 16)

            def g6(par, i, g):
                pool.wait_ge(S(f"idx{par}"), 2 * (of_parity(par) + 1) + i + 1)
                pool.sem_inc(S("pool_turn"))
                for k in range(GC):
                    gather(cols(g_a[par], k, K * D), acc2, ix_a[par][:, k:k + 1], S(f"gathered{par}"))

            def s3(par, i, g):
                pool.wait_ge(S("msg_zrow"), NGR + g + 1)
                for k in range(GC):
                    chain_wait(1, k % K, par, i, k)
                    scatter(acc3_rows, N * K, ix_b[par][:, k:k + 1], cols(zrow[par], k), S(f"added{k % K}{par}"), add=True)

            g6(0, 0, 0)
            with pool.Fori(0, NGR // 2) as i:
                g6(1, i, 2 * i + 1)
                s3(0, i, 2 * i)
                g6(0, i + 1, 2 * i + 2)
                s3(1, i, 2 * i + 1)
            s3(0, NGR // 2, NGR - 1)

            tiles(pool, last_pool)

        @block.tensor
        def _(pe):
            pe.wait_ge(S("pool_c"), 7)
            pe.wait_ge(S("consts"), 1)
            z = oh_hi[0][0:P, 0:HH]
            pe.wait_ge(S("hist_ready"), 1)
            for h in range(2):
                last_h = nc.tensor.matmul(psGH[0][:, 512 * h:512 * h + HH], oh_lo[0][0:P, :], z, start=True, stop=False)
            last_h.then_inc(S("hist_pe"), 1)
            with pe.Fori(0, TC // 2) as i:
                for l in LANES:
                    pe.wait_ge(S(f"onehot{l}"), i + 1)
                    for h in range(2):
                        last_h = nc.tensor.matmul(psGH[0][:, 512 * h:512 * h + HH], oh_lo[l][0:P, :],
                                                  oh_hi[l][0:P, HH * h:HH * h + HH], start=False, stop=False)
                    last_h.then_inc(S(f"onehot_used{l}"), 1)
            pe.wait_ge(S("hist_ready"), 2)
            for h in range(2):
                last_h = nc.tensor.matmul(psGH[0][:, 512 * h:512 * h + HH], oh_lo[0][0:P, :], z, start=False, stop=True)
            last_h.then_inc(S("hist_pe"), 1)
            pe.wait_ge(S("loaded"), LOADED)
            nc.tensor.matmul(psA[0][:, 0:128], wbd[:, 0, :], blk_c[:, :], start=True, stop=True)
            for m in range(1, 4):
                nc.tensor.matmul(psA[0][:, 128 * m:128 * m + 128], wbd[:, m, :], ident[:, :], start=True, stop=True)
            nc.tensor.matmul(psB[0][:, 0:128], wbd[:, 4, :], ident[:, :], start=True, stop=True)
            nc.tensor.transpose(psB[0][:, 128:256], w1d, ident[:, :])
            nc.tensor.matmul(psB[0][:, 256:320], w2s[0:D, :], blk_c[0:D, 0:D], start=True, stop=True)
            nc.tensor.transpose(psB[0][0:DE, 384:384 + D], w1e_s[0:D, :], ident[0:D, 0:D]).then_inc(S("setup_ps"), 1)
            pe.wait_ge(S("w_made"), 1)
            for j, v in enumerate((B0, CR, LB2, L2B)):
                nc.tensor.matmul(psA[1][:, j:j + 1], blk_c[:, :], col(v), start=True, stop=True)
            nc.tensor.matmul(psA[1][:, 4:5], wt[0:D, W1T, :], vec[0:D, LB1:LB1 + 1], start=True, stop=True)
            for f in range(4):
                last_f = nc.tensor.matmul(psB[1][0:D, P * f:P * f + P], ends[:, f:f + 1].broadcast_to((P, D)),
                                          ident[0:P, 0:P], start=True, stop=True)
            last_f.then_inc(S("setup_ps"), 1)
            end_phase(pe, 1)

            first_blocks(dense_pe, pe)
            end_phase(pe, 2)
            groups(pe, lambda par, i, g: both(scores0_pe(pe, par, i, g), dense_pe(pe, 1, run1(0, g))))
            end_phase(pe, 3)
            for k, n in enumerate((1, 1, 1, 1, D, D)):
                carries_pe(pe, k + 1, n)
            end_phase(pe, 4)
            groups(pe, lambda par, i, g: both(dst1_pe(pe, par, i, g), dense_pe(pe, 1, run1(1, g))))
            end_phase(pe, 5)
            groups(pe, lambda par, i, g: both(src1_pe(pe, par, i, g), dense_pe(pe, 1, run1(2, g))))
            end_phase(pe, 6)
            for k, n in enumerate((1, 1, 1, 1, D, D)):
                carries_pe(pe, 6 + k + 1, n)
            end_phase(pe, 7)
            groups(pe, lambda par, i, g: both(dst2_pe(pe, par, i, g)))
            end_phase(pe, 8)
            groups(pe, lambda par, i, g: both(dst3_pe(pe, par, i, g)))

        @block.scalar
        def _(act):
            act.wait_ge(S("loaded"), LOADED)
            nc.scalar.activation(col(FUN), col(FUS), ACT.Sigmoid).then_inc(S("fusion"), 1)
            act.wait_ge(S("deg_max"), 1)
            nc.scalar.activation(deg, deg, ACT.Abs_reciprocal_sqrt).then_inc(S("deg_rs"), 1)
            end_phase(act, 1)
            first_blocks(dense_act, act)
            end_phase(act, 2)
            groups(act, lambda par, i, g: both(scores0_act(act, par, i, g), dense_act(act, 1, run1(0, g))))
            end_phase(act, 3)
            softmax_act(act, 0)
            end_phase(act, 4)
            groups(act, lambda par, i, g: both(dst1_act(act, par, i, g), dense_act(act, 1, run1(1, g))))
            end_phase(act, 5)
            groups(act, lambda par, i, g: both(src1_act(act, par, i, g), dense_act(act, 1, run1(2, g))))
            end_phase(act, 6)
            softmax_act(act, 1)
            end_phase(act, 7)
            groups(act, lambda par, i, g: both(dst2_act(act, par, i, g)))
            end_phase(act, 8)
            groups(act, lambda par, i, g: both(dst3_act(act, par, i, g)))
            tiles(act, last_act)

        @block.vector
        def _(dve):
            step = [0]

            def own(ins):
                step[0] += 1
                ins.then_inc(S("seg_step"), 1)
                dve.wait_ge(S("seg_step"), step[0])

            nc.vector.memset(wbd, 0.0)
            nc.vector.memset(w_e, 0.0)
            nc.vector.memset(att[:, :, :], 0.0)
            nc.vector.memset(zero[:, :], 0.0)
            nc.vector.memset(src_i[:, :], 0)
            nc.vector.memset(dst_i[:, :], 0)
            nc.vector.memset(last_i[:, :], 0)
            nc.vector.memset(acc_i[:, :], 0)
            nc.vector.memset(prev_f.bitcast(i32)[0:P, :], -1)
            nc.vector.memset(next_f.bitcast(i32)[0:P, :], -1)
            nc.vector.memset(col(EPSV), EPS)
            own(nc.vector.memset(w2p[:, :, :], 0.0))
            dve.drain().then_inc(S("cleared"), 1)
            own(nc.vector.memset(blk_j[:, :], 0.0))
            nc.vector.memset(blk_j[0:64, 0:64], 1.0 / D)
            own(nc.vector.memset(blk_j[64:128, 64:128], 1.0 / D))
            dve.wait_ge(S("pool_c"), 7)
            nc.vector.tensor_tensor(blk_c[:, :], ident[:, :], blk_j[:, :], ALU.subtract).then_inc(S("consts"), 1)
            dve.wait_ge(S("loaded"), LOADED)

            own(nc.vector.tensor_copy(dst_f[0:P, :], src_i[:, 0:TC]))
            own(nc.vector.tensor_scalar(src_hi[0:P, :], dst_f[0:P, :], 1.0 / HB, None, ALU.mult))
            own(nc.vector.tensor_copy(tmp_i[0:P, :], src_hi[0:P, :]))
            own(nc.vector.tensor_copy(src_lo[0:P, :], tmp_i[0:P, :]))
            own(nc.vector.scalar_tensor_tensor(src_hi[0:P, :], src_lo[0:P, :], -float(HB), dst_f[0:P, :], ALU.mult, ALU.add))
            for op, bound, sign in ((ALU.is_lt, 0.0, 1.0), (ALU.is_ge, float(HB), -1.0)):
                own(nc.vector.tensor_scalar(tmp_f[0:P, :], src_hi[0:P, :], bound, sign, op, ALU.mult))
                own(nc.vector.tensor_tensor(src_lo[0:P, :], src_lo[0:P, :], tmp_f[0:P, :], ALU.subtract))
                own(nc.vector.scalar_tensor_tensor(src_hi[0:P, :], tmp_f[0:P, :], float(HB), src_hi[0:P, :], ALU.mult, ALU.add))
            nc.vector.memset(oh_lo[0][0:P, :], 0.0)
            own(nc.vector.memset(oh_hi[0][0:P, :], 0.0))
            dve.drain().then_inc(S("hist_ready"), 1)
            dve.wait_ge(S("hist_pe"), 1)
            with dve.Fori(0, TC // 2) as i:
                for l in LANES:
                    dve.wait_ge(S(f"onehot_used{l}"), i)
                    nc.vector.tensor_scalar(oh_lo[l][0:P, :], iota_lo[0:P, :], src_lo[0:P, bass.ds(2 * i + l, 1)], None,
                                            ALU.is_equal)
                    nc.vector.tensor_scalar(oh_hi[l][0:P, :], iota_hi[0:P, :], src_hi[0:P, bass.ds(2 * i + l, 1)], None,
                                            ALU.is_equal).then_inc(S(f"onehot{l}"), 1)
            dve.wait_ge(S("onehot_used0"), TC // 2)
            nc.vector.memset(oh_lo[0][0:P, :], 0.0)
            nc.vector.memset(oh_hi[0][0:P, :], 0.0).then_inc(S("hist_ready"), 1)
            dve.wait_ge(S("hist_pe"), 2)
            d_ps = psGH[0][:, :].rearrange("p (h c) -> p h c", h=2)[:, :, 0:HH]
            nc.vector.tensor_scalar(deg_on.rearrange("p (h c) -> p h c", h=2), d_ps, 0.0, None, ALU.is_gt)
            nc.vector.tensor_scalar(deg.rearrange("p (h c) -> p h c", h=2), d_ps, 1.0, None, ALU.max).then_inc(S("deg_max"), 1)

            dve.wait_ge(S("setup_ps"), 1)
            nc.vector.tensor_copy(w1e_t[0:DE, :], psB[0][0:DE, 384:384 + D]).then_inc(S("w1e_t"), 1)
            dve.wait_ge(S("fusion"), 1)
            own(nc.vector.tensor_scalar(col(T0), col(FUN), -1.0, 1.0, ALU.mult, ALU.add))
            nc.vector.tensor_copy(wt[:, 0:2, :].rearrange("p w c -> p (w c)"), psA[0][:, 0:256])
            nc.vector.tensor_scalar(wt[:, PHY, :], psA[0][:, 256:384], col(FUN), None, ALU.mult)
            nc.vector.tensor_scalar(wt[:, NEU, :], psA[0][:, 384:512], col(T0), None, ALU.mult)
            nc.vector.tensor_copy(wt[:, L2W:L2W + 2, :].rearrange("p w c -> p (w c)"), psB[0][:, 0:256])
            nc.vector.tensor_scalar(wt[:, DG2, :], blk_c[:, :], col(G2), None, ALU.mult)
            nc.vector.tensor_copy(w2p[:, 0, 0:64], psB[0][:, 256:320])
            nc.vector.tensor_copy(w2p[:, 1, 64:128], psB[0][:, 256:320])
            nc.vector.tensor_tensor(col(CR), col(LB1), col(MB2), ALU.add)

            own(nc.vector.tensor_copy(tmp_f[0:P, :], prev_f.bitcast(i32)[0:P, :]))
            own(nc.vector.tensor_copy(src_lo[0:P, :], next_f.bitcast(i32)[0:P, :]))
            own(nc.vector.tensor_copy(dst_f[0:P, :], dst_i[:, 0:TC]))
            nc.vector.tensor_tensor(same[:, :], dst_f[0:P, :], tmp_f[0:P, :], ALU.is_equal)
            own(nc.vector.tensor_tensor(nxt[:, :], dst_f[0:P, :], src_lo[0:P, :], ALU.is_equal))
            nc.vector.tensor_scalar(last[:, :], nxt[:, :], -1.0, 1.0, ALU.mult, ALU.add)
            nc.vector.tensor_scalar(pen_f[:, :], same[:, :], 1.0, -NEG, ALU.subtract, ALU.mult)
            nc.vector.tensor_scalar(pen_b[:, :], nxt[:, :], 1.0, -NEG, ALU.subtract, ALU.mult)
            own(nc.vector.scalar_tensor_tensor(tmp_f[0:P, :], nxt[:, :], float(SKIP), dst_f[0:P, :], ALU.mult, ALU.add))
            nc.vector.tensor_copy(last_i[:, 0:TC], tmp_f[0:P, :])
            for f, a in enumerate((same, nxt, pen_f, pen_b)):
                nc.vector.tensor_reduce(ends[:, f:f + 1], a[:, :], AX.X, ALU.min)
            for l in LANES:
                nc.vector.tensor_copy(ix_a[l][:, :], src_i[:, GC * l:GC * l + GC])
                nc.vector.tensor_copy(ix_b[l][:, :], dst_i[:, GC * l:GC * l + GC])
            dve.drain().then_inc(S("w_made"), 1)
            nc.vector.nop().then_inc(S("idx0"), 1)
            nc.vector.nop().then_inc(S("idx1"), 1)
            dve.wait_ge(S("deg_rs"), 1)
            nc.vector.tensor_tensor(deg, deg, deg_on, ALU.mult).then_inc(S("dis_made"), 1)
            dve.wait_ge(S("setup_ps"), 2)
            nc.vector.tensor_copy(vec[:, CB0:CB0 + 4], psA[1][:, 0:4])
            nc.vector.tensor_tensor(col(HB1), psA[1][:, 4:5], col(MB1), ALU.add)
            nc.vector.tensor_copy(row_flags[:, :, :].rearrange("d f p -> d (f p)"), psB[1][0:D, 0:4 * P])
            end_phase(dve, 1)

            first_blocks(dense_dve, dve)
            end_phase(dve, 2)
            groups(dve, lambda par, i, g: both(scores0_dve(dve, par, i, g), dense_dve(dve, 1, run1(0, g))))
            end_phase(dve, 3)
            softmax_dve(dve, 0, step)
            sums_dve(dve, 0, step)
            end_phase(dve, 4)
            groups(dve, lambda par, i, g: both(dst1_dve(dve, par, i, g), dense_dve(dve, 1, run1(1, g))))
            for l in LANES:
                nc.vector.tensor_copy(ix_b[l][:, :], src_i[:, GC * l:GC * l + GC]).then_inc(S(f"idx{l}"), 1)
            end_phase(dve, 5)
            groups(dve, lambda par, i, g: both(src1_dve(dve, par, i, g), dense_dve(dve, 1, run1(2, g))))
            end_phase(dve, 6)
            softmax_dve(dve, 1, step)
            sums_dve(dve, 1, step)
            dve.wait_ge(S("dis_in"), 16 * TC)
            end_phase(dve, 7)
            groups(dve, lambda par, i, g: both(dst2_dve(dve, par, i, g)))
            for par in LANES:
                dve.wait_ge(S(f"x2_sent{par}"), 16 * GC * of_parity(par))
                for c in range(K):
                    dve.wait_ge(S(f"added{c}{par}"), 16 * (GC // K) * of_parity(par))
            for l in LANES:
                nc.vector.tensor_copy(ix_a[l][:, :], dst_i[:, GC * l:GC * l + GC]).then_inc(S(f"idx{l}"), 1)
            end_phase(dve, 8)
            groups(dve, lambda par, i, g: both(dst3_dve(dve, par, i, g)))
            tiles(dve, last_dve)


_INS = ['x', 'src', 'dst', 'edge_attr_16', 'edge_weight', 'L0_gnn_W1', 'L0_gnn_W2', 'L0_gnn_attn', 'L0_gnn_bias',
        'L1_gnn_W_phys', 'L1_gnn_W_neur', 'L1_gnn_att_w', 'L1_gnn_channel_fusion', 'L1_gnn_mlp_w1', 'L1_gnn_mlp_b1',
        'L1_gnn_mlp_w2', 'L1_gnn_mlp_b2', 'L1_gnn_ln1_g', 'L1_gnn_ln1_b', 'L1_gnn_ln2_g', 'L1_gnn_ln2_b', 'L2_gnn_W',
        'L2_gnn_b']


def kernel(**inputs):
    import numpy as _np
    import concourse.bacc as _bacc
    from concourse import mybir as _mybir
    from concourse.bass_utils import run_bass_kernel_spmd as _run

    nc = _bacc.Bacc("TRN2", target_bir_lowering=False, num_devices=1)
    arrays, args = {}, []
    for name in _INS:
        a = _np.ascontiguousarray(inputs[name])
        if a.ndim == 0:
            a = a.reshape(1)
        arrays[f"in_{name}_dram"] = a
        args.append(nc.dram_tensor(f"in_{name}_dram", a.shape, _mybir.dt.from_np(a.dtype), kind="ExternalInput").ap())
    shape = inputs["x"].shape
    args.append(nc.dram_tensor("out_0_dram", shape, _mybir.dt.float32, kind="ExternalOutput").ap())
    gnn_resnorm_kernel(nc, *args)
    r = _run(nc, [arrays], core_ids=[0])
    return r.results[0]["out_0_dram"]
```

```python
import concourse.bass as bass
from concourse import mybir
from contextlib import ExitStack

fp32 = mybir.dt.float32
bf16 = mybir.dt.bfloat16
i32 = mybir.dt.int32
ALU = mybir.AluOpType
ACT = mybir.ActivationFunctionType
AX = mybir.AxisListType


def gnn_resnorm_kernel(nc, x, src, dst, edge_attr, edge_weight, W1, W2, attn, bias0, W_phys, W_neur, att_w,
                       fusion, mlp_w1, mlp_b1, mlp_w2, mlp_b2, ln1_g, ln1_b, ln2_g, ln2_b, L2_W, L2_b, out):
    N, D = x.shape
    E, DE = edge_attr.shape
    HID = mlp_w1.shape[0]
    P = 125
    TC = E // P
    GC = 8
    NGR = TC // GC
    Q = GC // 2
    EW = Q * P
    NB = 1024
    NBLK = -(-N // NB)
    R = 16
    NT = 128 * R
    NTILE = -(-N // NT)
    K = 2
    HB = 782
    HH = HB // 2
    EPS = 1e-5
    NEG = -1e30
    SKIP = 1 << 22

    agg0 = nc.dram_tensor("agg0", (N, D), fp32).ap()
    x2tab = nc.dram_tensor("x2tab", (N, D), fp32).ap()
    acc2 = nc.dram_tensor("acc2", (N, K * D), fp32).ap()
    acc3 = nc.dram_tensor("acc3", (N, K * D), fp32).ap()
    distab = nc.dram_tensor("distab", (128 * HB,), fp32).ap()
    acc2_rows = acc2.rearrange("n (k d) -> (n k) d", k=K)
    acc3_rows = acc3.rearrange("n (k d) -> (n k) d", k=K)

    ctx = ExitStack()
    with ctx:
        def sb(name, shape, dt=fp32):
            return ctx.enter_context(nc.sbuf_tensor(name, shape, dt))

        xsn = sb("xsn", [128, TC, D])
        xdt = sb("xdt", [128, TC // 2 * P])
        ag = sb("ag", [128, D, TC])
        src_i, dst_i, last_i, acc_i = (sb(n, [P, TC + 2 * GC], i32) for n in ("src_i", "dst_i", "last_i", "acc_i"))
        ew, same, nxt, last, pen_f, pen_b, score, sm1, sm2, dis = (
            sb(n, [P, TC]) for n in ("ew", "same", "nxt", "last", "pen_f", "pen_b", "score", "sm1", "sm2", "dis"))
        edge_col, carry = (sb(n, [P, D]) for n in ("edge_col", "carry"))
        rows = sb("rows", [D, P + 1])
        ends = sb("ends", [P, 4])
        row_flags = sb("row_flags", [D, 4, P])
        ident, blk_j, blk_c, low = (sb(n, [128, 128]) for n in ("ident", "blk_j", "blk_c", "low"))
        wt = sb("wt", [128, 7, 128])
        A2C, W1X, PHY, NEU, L2W, W1T, DG2 = range(7)
        w2p = sb("w2p", [128, 2, 128])
        att = sb("att", [128, 4, 2])
        vec = sb("vec", [128, 17])
        B0, G1, LB1, G2, LB2, MB2, MB1, L2B, FUS, EPSV, CB0, CR, CT, C2, HB1, FUN, T0 = range(17)
        b2_row = sb("b2_row", [128, D])
        zero = sb("zero", [128, 250])
        LANES = range(2)

        def lane(name, cols):
            return [sb(f"{name}{l}", [128, cols]) for l in LANES]

        xin, b_x1, b_h, b_s = (lane(n, 512) for n in ("xin", "b_x1", "b_h", "b_s"))
        b_gl = lane("b_gl", 1024)
        e_a, e_b, e_c = (sb(n, [128, 512]) for n in ("e_a", "e_b", "e_c"))
        g_s = lane("g_s", GC * D)
        ix_a = [sb(f"ix_a{l}", [P, GC], i32) for l in LANES]
        ix_b = [sb(f"ix_b{l}", [P, GC], i32) for l in LANES]
        sf, cnt = ([sb(f"{n}{l}", [P, GC]) for l in LANES] for n in ("sf", "cnt"))
        chain_of = sb("chain_of", [P, GC])

        ps = ctx.enter_context(nc.psum_tensor("ps", [128, 8 * 512], fp32))

        def bank(j, n=1):
            return ps[:, 512 * j:512 * (j + n)]

        psD = [[bank(3 * l + j) for j in range(3)] for l in LANES]
        psE = [bank(6), bank(7)]
        psL = [[bank(4 * l + j) for j in range(4)] for l in LANES]
        psD_BG = [bank(3 * l + 1, 2) for l in LANES]
        psL_BG = [bank(4 * l + 1, 2) for l in LANES]
        psL_GH = [bank(4 * l + 2, 2) for l in LANES]
        psA, psB, psGH = [bank(0), bank(1)], [bank(2), bank(3)], [bank(4, 2)]

        agf = ag[:, :, :].rearrange("p d t -> p (d t)")
        at_ = [0]

        def in_ag(cols):
            at_[0] += cols
            return agf[:, at_[0] - cols:at_[0]]

        wbd = in_ag(6 * 128).rearrange("p (w c) -> p w c", w=6)
        w_e = in_ag(Q * 128).rearrange("p (w c) -> p w c", w=Q)
        w1e_s, w1e_t, w1d, w2s = in_ag(DE), in_ag(D), in_ag(128), in_ag(HID)
        g_d = [in_ag(GC * D) for _ in LANES]
        ea_s = [in_ag(GC * DE) for _ in LANES]
        iota_lo, iota_hi = in_ag(128), in_ag(HB)
        oh_lo = [in_ag(64).bitcast(bf16) for _ in LANES]
        oh_hi = [in_ag(HH).bitcast(bf16) for _ in LANES]
        deg, deg_on = in_ag(HB), in_ag(HB)
        src_lo, src_hi, dst_f, prev_f, next_f, tmp_f = (in_ag(TC) for _ in range(6))
        tmp_i = in_ag(TC).bitcast(i32)

        xsf = xsn[:, :, :].rearrange("p t d -> p (t d)")
        xt_ = [0]

        def in_xsn(cols):
            xt_[0] += cols
            return xsf[:, xt_[0] - cols:xt_[0]]

        xrow = [in_xsn(GC * D) for _ in LANES]
        zrow = [in_xsn(GC * D) for _ in LANES]
        g_a = [in_xsn(GC * K * D) for _ in LANES]
        zs = [in_xsn(GC * D) for _ in LANES]
        same_src = [in_xsn(GC * P) for _ in LANES]
        dup = [in_xsn(GC * P) for _ in LANES]

        LOADED = 16 * (2 * 7 + 2 + 2 * 5 + 2 * 5 + 3 + 3 + 4)
        names = {}

        HEAD = 1
        LANED = ("blk_xo", "blk_st", "blk_t1",  "s1_msg", "ln_t", "e2_idx", "e2_kept",  "rows0_used",
                 "onehot_used", "l_sums", "l_added", "l_act", "l_out")
        HEADED = ("scores_out", "d1_kept", *(f"{name}{l}" for name in LANED for l in LANES))

        def S(name):
            if name not in names:
                names[name] = ctx.enter_context(nc.semaphore(name))
            return names[name]

        def col(v):
            return vec[:, v:v + 1]

        def grp(a, g):
            return a[:, bass.ds(g * GC, GC)]

        def xg(g):
            return xdt[:, bass.ds(g * EW, EW)]

        def xsg(g):
            return xsf[0:P, bass.ds(g * (GC * D), GC * D)]

        def bc(a, d):
            return a.unsqueeze(2).broadcast_to((a.shape[0], a.shape[1], d))

        def t3(a, c=GC):
            return a.rearrange("p (c d) -> p c d", c=c)

        block = ctx.enter_context(nc.Block())

        def groups(eng, body):
            with eng.Fori(0, NGR // 2) as i:
                body(0, i, 2 * i)
                body(1, i, 2 * i + 1)
            body(0, NGR // 2, NGR - 1)

        def group_pairs(eng, steps):
            with eng.Fori(0, NGR // 2) as i:
                both(steps(eng, 0, i, 2 * i), steps(eng, 1, i, 2 * i + 1))
            both(steps(eng, 0, NGR // 2, NGR - 1))

        def of_parity(par):
            return (NGR + 1 - par) // 2

        def moved(loop, par, i):
            return 16 * GC * ((0, 2, 3, 4, 5)[loop - 1] * of_parity(par) + (2 if loop == 1 else 1) * i)

        def added(loop, par, i):
            return 16 * (TC // (2 * K) + (GC // K) * ((loop - 4) * of_parity(par) + i))

        def both(*programs):
            at = [next(p) for p in programs]
            while any(a is not None for a in at):
                j = min((j for j in range(len(at)) if at[j] is not None), key=lambda j: at[j])
                at[j] = next(programs[j], None)

        assert NBLK == 2 * (2 * NGR - 1)

        def turn(loop, g):
            return loop * (NGR - 1) + g

        def row(loop, g, l):
            if loop == 1 and isinstance(g, int) and g == NGR - 1 and l == 1:
                return N - NB
            return (2 * turn(loop, g) + l) * NB

        def groups_and_blocks(eng, loop, edges, dense):
            def body(par, i, g):
                if loop == 0 and isinstance(g, int):
                    both(edges(eng, par, i, g))
                else:
                    both(*(dense(eng, l, turn(loop, g)) for l in LANES), edges(eng, par, i, g))
            groups(eng, body)

        def mlp_pe(pe, h, l, n, c, w, w4, pl, bg):
            yield h + 1
            pe.wait_ge(S(f"mlp_h{l}"), n + 1)
            nc.tensor.matmul(bg[:, 0:w], wt[0:64, W1T, :], b_h[l][0:64, 0:w], start=True, stop=True)
            nc.tensor.matmul(bg[:, 512:512 + w], wt[64:128, W1T, :], b_h[l][64:128, 0:w], start=True,
                             stop=True).then_inc(S(f"mlp_m1{l}"), 1)
            nc.tensor.matmul(pl[0][:, 0:w], blk_c[:, :], b_h[l][:, 0:w], start=True, stop=False)
            yield h + 3
            pe.wait_ge(S(f"mlp_gelu{l}"), n + 1)
            nc.tensor.matmul(pl[0][:, 0:w], w2p[:, 0, :], b_gl[l][:, 0:w], start=False, stop=False)
            nc.tensor.matmul(pl[0][:, 0:w], w2p[:, 1, :], b_gl[l][:, 512:512 + w], start=False,
                             stop=True).then_inc(S(f"mlp_m2{l}"), 1)
            yield h + 5
            pe.wait_ge(S(f"squares{l}"), c + 1)
            nc.tensor.matmul(pl[2][:, 0:w], blk_j[:, :], b_s[l][:, 0:w], start=True,
                             stop=True).then_inc(S(f"means{l}"), 1)
            yield h + 8
            pe.wait_ge(S(f"mlp_t{l}"), n + 1)
            nc.tensor.matmul(pl[1][:, 0:w], wt[:, DG2, :], b_h[l][:, 0:w], start=True,
                             stop=True).then_inc(S(f"mlp_d{l}"), 1)
            yield h + 11
            pe.wait_ge(S(f"squares{l}"), c + 2)
            nc.tensor.matmul(pl[2][:, 0:w], blk_j[:, :], b_s[l][:, 0:w], start=True,
                             stop=True).then_inc(S(f"means{l}"), 1)
            yield h + 14
            pe.wait_ge(S(f"mlp_x2{l}"), n + 1)
            for q in range(4):
                last_t = nc.tensor.transpose(pl[0][0:w4, 128 * q:128 * q + 128], b_h[l][:, w4 * q:w4 * q + w4], ident[:, :])
            last_t.then_inc(S(f"mlp_t9{l}"), 1)

        def mlp_act(act, h, l, n, c, w, pl, bg, stored=None):
            yield h + 2
            act.wait_ge(S(f"mlp_m1{l}"), n + 1)
            if stored is not None:
                act.wait_ge(S(f"blk_st{l}"), HEAD + stored)
            nc.scalar.activation(b_gl[l][:, :].rearrange("p (b f) -> p b f", b=2)[:, :, 0:w],
                                 bg.rearrange("p (b f) -> p b f", b=2)[:, :, 0:w], ACT.Gelu,
                                 bias=col(HB1)).then_inc(S(f"mlp_gelu{l}"), 1)
            yield h + 4
            act.wait_ge(S(f"mlp_m2{l}"), n + 1)
            nc.scalar.activation(b_s[l][:, 0:w], pl[0][:, 0:w], ACT.Square, bias=col(CR)).then_inc(S(f"squares{l}"), 1)
            yield h + 6
            act.wait_ge(S(f"means{l}"), c + 1)
            nc.scalar.activation(b_s[l][:, 0:w], pl[2][:, 0:w], ACT.Abs_reciprocal_sqrt,
                                 bias=col(EPSV)).then_inc(S(f"rstds{l}"), 1)
            yield h + 10
            act.wait_ge(S(f"mlp_v{l}"), n + 1)
            nc.scalar.activation(b_s[l][:, 0:w], b_h[l][:, 0:w], ACT.Square).then_inc(S(f"squares{l}"), 1)
            yield h + 12
            act.wait_ge(S(f"means{l}"), c + 2)
            nc.scalar.activation(b_s[l][:, 0:w], pl[2][:, 0:w], ACT.Abs_reciprocal_sqrt,
                                 bias=col(EPSV)).then_inc(S(f"rstds{l}"), 1)

        def mlp_dve(dve, h, l, n, c, w, pl, x1):
            yield h + 7
            dve.wait_ge(S(f"rstds{l}"), c + 1)
            nc.vector.scalar_tensor_tensor(b_h[l][:, 0:w], pl[0][:, 0:w], col(CR), b_s[l][:, 0:w], ALU.add,
                                           ALU.mult).then_inc(S(f"mlp_t{l}"), 1)
            yield h + 9
            dve.wait_ge(S(f"mlp_d{l}"), n + 1)
            nc.vector.scalar_tensor_tensor(b_h[l][:, 0:w], pl[1][:, 0:w], col(CT), x1, ALU.add,
                                           ALU.add).then_inc(S(f"mlp_v{l}"), 1)
            yield h + 13
            dve.wait_ge(S(f"rstds{l}"), c + 2)
            nc.vector.tensor_tensor(b_h[l][:, 0:w], b_h[l][:, 0:w], b_s[l][:, 0:w], ALU.mult).then_inc(S(f"mlp_x2{l}"), 1)

        def dense_pe(pe, l, n):
            yield 0
            pe.wait_ge(S(f"blk_in{l}"), 16 * (n + 1))
            pe.wait_ge(S(f"blk_xo{l}"), HEAD + n)
            for q in range(4):
                last_t = nc.tensor.transpose(psD[l][0][:, 128 * q:128 * q + 128], xin[l][:, 128 * q:128 * q + 128], ident[:, :])
            last_t.then_inc(S(f"blk_t1{l}"), 1)
            yield 2
            pe.wait_ge(S(f"blk_u{l}"), n + 1)
            nc.tensor.matmul(psD[l][1][:, :], blk_c[:, :], b_h[l][:, :], start=True, stop=True).then_inc(S(f"blk_c1{l}"), 1)
            yield 4
            pe.wait_ge(S(f"squares{l}"), 4 * n + 1)
            nc.tensor.matmul(psD[l][2], blk_j[:, :], b_s[l][:, :], start=True, stop=True).then_inc(S(f"means{l}"), 1)
            yield 8
            pe.wait_ge(S(f"squares{l}"), 4 * n + 2)
            nc.tensor.matmul(psD[l][2], blk_j[:, :], b_s[l][:, :], start=True, stop=True).then_inc(S(f"means{l}"), 1)
            yield from mlp_pe(pe, 10, l, n, 4 * n + 2, 512, 128, psD[l], psD_BG[l])

        def dense_act(act, l, n):
            yield 3
            act.wait_ge(S(f"blk_c1{l}"), n + 1)
            nc.scalar.activation(b_s[l][:, :], psD[l][1][:, :], ACT.Square).then_inc(S(f"squares{l}"), 1)
            yield 5
            act.wait_ge(S(f"means{l}"), 4 * n + 1)
            nc.scalar.activation(b_s[l][:, :], psD[l][2], ACT.Abs_reciprocal_sqrt, bias=col(EPSV)).then_inc(S(f"rstds{l}"), 1)
            yield 7
            act.wait_ge(S(f"blk_x1{l}"), n + 1)
            nc.scalar.activation(b_s[l][:, :], b_x1[l][:, :], ACT.Square).then_inc(S(f"squares{l}"), 1)
            yield 9
            act.wait_ge(S(f"means{l}"), 4 * n + 2)
            nc.scalar.activation(b_s[l][:, :], psD[l][2], ACT.Abs_reciprocal_sqrt, bias=col(EPSV)).then_inc(S(f"rstds{l}"), 1)
            yield from mlp_act(act, 10, l, n, 4 * n + 2, 512, psD[l], psD_BG[l], 16 * n)

        def dense_dve(dve, l, n):
            yield 1
            dve.wait_ge(S(f"blk_t1{l}"), HEAD + n + 1)
            nc.vector.tensor_scalar(b_h[l][:, :], psD[l][0][:, :], col(B0), None, ALU.add).then_inc(S(f"blk_u{l}"), 1)
            yield 6
            dve.wait_ge(S(f"rstds{l}"), 4 * n + 1)
            nc.vector.tensor_tensor(b_x1[l][:, :], psD[l][1][:, :], b_s[l][:, :], ALU.mult).then_inc(S(f"blk_x1{l}"), 1)
            yield 10
            dve.wait_ge(S(f"rstds{l}"), 4 * n + 2)
            nc.vector.scalar_tensor_tensor(b_h[l][:, :], b_x1[l][:, :], col(G1), b_s[l][:, :], ALU.mult,
                                           ALU.mult).then_inc(S(f"mlp_h{l}"), 1)
            yield from mlp_dve(dve, 10, l, n, 4 * n + 2, 512, psD[l], b_x1[l][:, :])
            yield 25
            dve.wait_ge(S(f"mlp_t9{l}"), n + 1)
            dve.wait_ge(S(f"blk_st{l}"), HEAD + 16 * n)
            nc.vector.tensor_tensor(g_x[l].rearrange("p (t d) -> p t d", d=D), psD[l][0].rearrange("p (t d) -> p t d", d=D),
                                    b2_row[:, :].unsqueeze(1).broadcast_to((128, 8, D)), ALU.add).then_inc(S(f"blk_xo{l}"), 1)

        g_x = [b_gl[l][:, 512:1024] for l in LANES]

        def dense_load(sp, l, n, row):
            sp.wait_ge(S(f"blk_t1{l}"), HEAD + n)
            sp.dma_start(xin[l][:, :], x[bass.ds(row, NB), :].rearrange("(p t) d -> p (t d)", p=128)).then_inc(
                S(f"blk_in{l}"), 16)

        def dense_store(sp, l, n, row):
            sp.wait_ge(S(f"blk_xo{l}"), HEAD + n + 1)
            sp.dma_start(x2tab[bass.ds(row, NB), :].rearrange("(p t) d -> p (t d)", p=128), g_x[l]).then_inc(
                S(f"blk_st{l}"), 16)

        def end_phase(eng, k):
            eng.drain().then_inc(S("phase"), 1)
            eng.wait_ge(S("phase"), 3 * k)

        def scores0_pe(pe, par, i, g):
            yield 0
            pe.wait_ge(S(f"moved{par}"), moved(1, par, i + 1))
            pe.wait_ge(S(f"ea_in{par}"), 16 * (i + 1))
            pe.wait_ge(S("scores_out"), HEAD + g)
            for q in range(Q):
                nc.tensor.transpose(psE[0][:, P * q:P * q + P], g_s[par][0:P, 128 * q:128 * q + 128], ident[0:P, 0:P])
                last_t = nc.tensor.transpose(psE[1][:, P * q:P * q + P], g_d[par][0:P, 128 * q:128 * q + 128], ident[0:P, 0:P])
            last_t.then_inc(S("edge_t"), 1)
            yield 3
            pe.wait_ge(S("edge_a"), g + 1)
            nc.tensor.transpose(psE[0][:, 0:P], ea_s[par][0:P, :], ident[0:P, 0:P]).then_inc(S("s0_ea_ps"), 1)
            yield 6
            pe.wait_ge(S("s0_xd"), g + 1)
            pe.wait_ge(S("s0_ea"), g + 1)
            nc.tensor.matmul(psE[1][:, 0:EW], wt[:, W1X, :], e_a[:, 0:EW], start=True, stop=False)
            for q in range(Q):
                last_f = nc.tensor.matmul(psE[1][:, P * q:P * q + P], w_e[:, q, :], e_b[:, 0:P], start=False, stop=(q == Q - 1))
            last_f.then_inc(S("s0_f_ps"), 1)
            yield 12
            pe.wait_ge(S("s0_ed"), g + 1)
            pe.wait_ge(S("edge_x"), g + 1)
            for q in range(Q):
                o = psE[0][0:P, 2 * q:2 * q + 2]
                nc.tensor.matmul(o, e_b[:, P * q:P * q + P], att[:, 0, :], start=True, stop=False)
                last_s = nc.tensor.matmul(o, e_c[:, P * q:P * q + P], att[:, 1, :], start=False, stop=True)
            last_s.then_inc(S("scores_ps"), 1)

        def scores0_act(act, par, i, g):
            yield 2
            act.wait_ge(S("edge_t"), g + 1)
            nc.scalar.activation(e_a[:, 0:EW], psE[0][:, 0:EW], ACT.Identity).then_inc(S("edge_a"), 1)
            yield 5
            act.wait_ge(S("s0_ea_ps"), g + 1)
            nc.scalar.activation(e_b[:, 0:P], psE[0][:, 0:P], ACT.Identity).then_inc(S("s0_ea"), 1)
            yield 8
            act.wait_ge(S("s0_f_ps"), g + 1)
            nc.scalar.activation(e_a[:, 0:EW], psE[1][:, 0:EW], ACT.Identity).then_inc(S("s0_fs"), 1)

        def scores0_dve(dve, par, i, g):
            yield 2
            dve.wait_ge(S("edge_t"), g + 1)
            nc.vector.tensor_copy(xg(g), psE[1][:, 0:EW]).then_inc(S("s0_xd"), 1)
            nc.vector.tensor_copy(xsg(g), g_s[par][0:P, :]).then_inc(S(f"rows0_used{par}"), 1)
            nc.vector.tensor_copy(ix_a[par][:, :], grp(src_i, g + 2))
            nc.vector.tensor_copy(ix_b[par][:, :], grp(dst_i, g + 2)).then_inc(S(f"idx{par}"), 1)
            yield 5
            dve.wait_ge(S("s0_xd"), g + 1)
            nc.vector.scalar_tensor_tensor(e_c[:, 0:EW], xg(g), 0.01, xg(g), ALU.mult, ALU.max).then_inc(S("s0_ed"), 1)
            yield 10
            dve.wait_ge(S("s0_fs"), g + 1)
            nc.vector.scalar_tensor_tensor(e_b[:, 0:EW], e_a[:, 0:EW], 0.01, e_a[:, 0:EW], ALU.mult,
                                           ALU.max).then_inc(S("edge_x"), 1)
            yield 14
            dve.wait_ge(S("scores_ps"), g + 1)
            nc.vector.tensor_copy(grp(score, g), psE[0][0:P, 0:GC]).then_inc(S("scores_out"), 1)

        def carries_pe(pe, k, n):
            pe.wait_ge(S("seg_ends"), k)
            nc.tensor.transpose(psA[0][0:n, 0:P], edge_col[:, 0:n], ident[0:P, 0:P]).then_inc(S("seg_rows_ps"), 1)
            pe.wait_ge(S("seg_rows"), k)
            src_rows = rows[0:n, 0:P] if k % 2 == 1 else rows[0:n, 1:P + 1]
            nc.tensor.transpose(psB[0][0:P, 0:n], src_rows, ident[0:n, 0:n]).then_inc(S("seg_carry_ps"), 1)

        def carries_dve(dve, k, n, flags, start, op0, op1):
            dve.wait_ge(S("seg_rows_ps"), k)
            if k % 2 == 1:
                nc.vector.memset(rows[0:n, 0:1], start)
                o, a, b = rows[0:n, 1:P + 1], row_flags[0:n, flags, :], psA[0][0:n, 0:P]
            else:
                nc.vector.memset(rows[0:n, P:P + 1], start)
                o, a, b = rows[0:n, 0:P][:, ::-1], row_flags[0:n, flags, ::-1], psA[0][0:n, 0:P][:, ::-1]
            nc.vector.tensor_tensor_scan(o, a, b, start, op0, op1).then_inc(S("seg_rows"), 1)
            dve.wait_ge(S("seg_carry_ps"), k)
            nc.vector.tensor_copy(carry[:, 0:n], psB[0][0:P, 0:n]).then_inc(S("seg_carry"), 1)
            dve.wait_ge(S("seg_carry"), k)

        def softmax_dve(dve, m, step):
            k = 6 * m

            def own(ins):
                step[0] += 1
                ins.then_inc(S("seg_step"), 1)
                dve.wait_ge(S("seg_step"), step[0])

            def scan(o, a, b, init, op0, op1, back):
                f = (lambda v: v[:, ::-1]) if back else (lambda v: v)
                own(nc.vector.tensor_tensor_scan(f(o), f(a), f(b), init, op0, op1))

            scan(sm1[:, :], pen_f[:, :], score[:, :], NEG, ALU.add, ALU.max, False)
            nc.vector.tensor_copy(edge_col[:, 0:1], sm1[:, TC - 1:TC]).then_inc(S("seg_ends"), 1)
            carries_dve(dve, k + 1, 1, 2, NEG, ALU.add, ALU.max)
            scan(sm2[:, :], pen_f[:, :], score[:, :], carry[:, 0:1], ALU.add, ALU.max, False)
            scan(sm1[:, :], pen_b[:, :], sm2[:, :], NEG, ALU.add, ALU.max, True)
            nc.vector.tensor_copy(edge_col[:, 0:1], sm1[:, 0:1]).then_inc(S("seg_ends"), 1)
            carries_dve(dve, k + 2, 1, 3, NEG, ALU.add, ALU.max)
            scan(sm1[:, :], pen_b[:, :], sm2[:, :], carry[:, 0:1], ALU.add, ALU.max, True)
            nc.vector.tensor_tensor(sm2[:, :], score[:, :], sm1[:, :], ALU.subtract).then_inc(S("seg_x"), 1)
            dve.wait_ge(S("seg_exp"), m + 1)
            scan(sm1[:, :], same[:, :], score[:, :], 0.0, ALU.mult, ALU.add, False)
            nc.vector.tensor_copy(edge_col[:, 0:1], sm1[:, TC - 1:TC]).then_inc(S("seg_ends"), 1)
            carries_dve(dve, k + 3, 1, 0, 0.0, ALU.mult, ALU.add)
            scan(sm1[:, :], same[:, :], score[:, :], carry[:, 0:1], ALU.mult, ALU.add, False)
            own(nc.vector.tensor_tensor(sm2[:, :], sm1[:, :], last[:, :], ALU.mult))
            scan(sm1[:, :], nxt[:, :], sm2[:, :], 0.0, ALU.mult, ALU.add, True)
            nc.vector.tensor_copy(edge_col[:, 0:1], sm1[:, 0:1]).then_inc(S("seg_ends"), 1)
            carries_dve(dve, k + 4, 1, 1, 0.0, ALU.mult, ALU.add)
            scan(sm1[:, :], nxt[:, :], sm2[:, :], carry[:, 0:1], ALU.mult, ALU.add, True)
            own(nc.vector.reciprocal(sm2[:, :], sm1[:, :]))
            own(nc.vector.tensor_tensor(sm1[:, :], score[:, :], sm2[:, :], ALU.mult))

        def softmax_act(act, m):
            act.wait_ge(S("seg_x"), m + 1)
            nc.scalar.activation(score[:, :], sm2[:, :], ACT.Exp).then_inc(S("seg_exp"), 1)

        def sums_dve(dve, m, step):
            k = 6 * m

            def own(ins):
                step[0] += 1
                ins.then_inc(S("seg_step"), 1)
                dve.wait_ge(S("seg_step"), step[0])

            own(nc.vector.tensor_tensor(ag[0:P, :, :], xsn[0:P, :, :].rearrange("p t d -> p d t"),
                                        sm1[:, :].unsqueeze(1).broadcast_to((P, D, TC)), ALU.mult))
            def scan_all(flags, back):
                def scan(a, f):
                    nc.vector.tensor_tensor_scan(a, f, a, 0.0, ALU.mult, ALU.add)
                if back:
                    for d in range(D):
                        scan(ag[0:P, d, ::-1], flags[:, ::-1])
                else:
                    U = 8
                    with dve.Fori(0, D // U) as i:
                        for u in range(U):
                            scan(ag[0:P, bass.ds(i * U + u, 1), :].rearrange("p o t -> p (o t)"), flags[:, :])
                own(dve.drain())

            def add_carry(run):
                U = 8
                with dve.Fori(0, D // U) as i:
                    for u in range(U):
                        a = ag[0:P, bass.ds(i * U + u, 1), :].rearrange("p o t -> p (o t)")
                        nc.vector.scalar_tensor_tensor(a, run[:, :], carry[:, bass.ds(i * U + u, 1)], a, ALU.mult, ALU.add)
                own(dve.drain())

            run_f, run_b = score, sm2
            nc.vector.tensor_tensor_scan(run_f[:, :], same[:, :], zero[0:P, 0:TC], 1.0, ALU.mult, ALU.add)
            own(nc.vector.tensor_tensor_scan(run_b[:, ::-1], nxt[:, ::-1], zero[0:P, 0:TC], 1.0, ALU.mult, ALU.add))
            scan_all(same, False)
            nc.vector.tensor_copy(edge_col[:, :], ag[0:P, :, TC - 1]).then_inc(S("seg_ends"), 1)
            carries_dve(dve, k + 5, D, 0, 0.0, ALU.mult, ALU.add)
            add_carry(run_f)
            own(nc.vector.tensor_tensor(ag[0:P, :, :], ag[0:P, :, :], last[:, :].unsqueeze(1).broadcast_to((P, D, TC)), ALU.mult))
            scan_all(nxt, True)
            nc.vector.tensor_copy(edge_col[:, :], ag[0:P, :, 0]).then_inc(S("seg_ends"), 1)
            carries_dve(dve, k + 6, D, 1, 0.0, ALU.mult, ALU.add)
            add_carry(run_b)

        def x1_pe(pe, at, s, a_ready, n, c, xsrc, w, agg, sq, c_ps, j_ps):
            yield at[0]
            pe.wait_ge(*a_ready)
            nc.tensor.matmul(c_ps[:, 0:EW], blk_c[:, :], xsrc, start=True, stop=False)
            nc.tensor.matmul(c_ps[:, 0:EW], w, agg, start=False, stop=True).then_inc(S(f"ln_c{s}"), 1)
            yield at[2]
            pe.wait_ge(S(f"squares{s}"), c + 1)
            nc.tensor.matmul(j_ps[:, 0:EW], blk_j[:, :], sq, start=True, stop=True).then_inc(S(f"means{s}"), 1)

        def x1_act(act, at, s, n, c, bias, sq, c_ps, j_ps):
            yield at[1]
            act.wait_ge(S(f"ln_c{s}"), n + 1)
            nc.scalar.activation(sq, c_ps[:, 0:EW], ACT.Square, bias=bias).then_inc(S(f"squares{s}"), 1)
            yield at[3]
            act.wait_ge(S(f"means{s}"), c + 1)
            nc.scalar.activation(sq, j_ps[:, 0:EW], ACT.Abs_reciprocal_sqrt, bias=col(EPSV)).then_inc(S(f"rstds{s}"), 1)

        AT2 = (6, 8, 10, 12)
        ATL = (3, 4, 5, 6)

        def dst1_pe(pe, par, i, g):
            yield 2
            pe.wait_ge(S("ln_rows_e"), g + 1)
            pe.wait_ge(S("scores_out"), HEAD + NGR + g)
            for q in range(Q):
                last_t = nc.tensor.transpose(psE[0][:, P * q:P * q + P], g_s[par][0:P, 128 * q:128 * q + 128], ident[0:P, 0:P])
            last_t.then_inc(S("edge_t"), 1)
            yield from x1_pe(pe, AT2, "_e", (S("edge_a"), NGR + g + 1), g, g, xg(g), wt[:, A2C, :], e_a[:, 0:EW], e_b[:, 0:EW], psE[1], psE[0])
            yield 16
            pe.wait_ge(S("edge_x"), NGR + g + 1)
            for q in range(Q):
                last_s = nc.tensor.matmul(psE[0][0:P, 2 * q:2 * q + 2], e_c[:, P * q:P * q + P], att[:, 3, :],
                                          start=True, stop=True)
            last_s.then_inc(S("scores_ps"), 1)

        def dst1_act(act, par, i, g):
            yield 4
            act.wait_ge(S("edge_t"), NGR + g + 1)
            nc.scalar.activation(e_a[:, 0:EW], psE[0][:, 0:EW], ACT.Identity).then_inc(S("edge_a"), 1)
            yield from x1_act(act, AT2, "_e", g, g, col(CB0), e_b[:, 0:EW], psE[1], psE[0])
            yield 16
            act.wait_ge(S("edge_x"), NGR + g + 1)
            nc.scalar.activation(xg(g), e_c[:, 0:EW], ACT.Identity).then_inc(S("d1_kept"), 1)

        def dst1_dve(dve, par, i, g):
            yield 0
            dve.wait_ge(S(f"moved{par}"), moved(2, par, i))
            dve.wait_ge(S("edge_t"), NGR + g)
            nc.vector.tensor_copy(t3(g_s[par][0:P, :]), ag[0:P, :, bass.ds(g * GC, GC)].rearrange("p d t -> p t d")).then_inc(
                S("ln_rows_e"), 1)
            nc.vector.tensor_copy(ix_a[par][:, :], grp(last_i, g)).then_inc(S("d1_idx"), 1)
            yield 14
            dve.wait_ge(S("rstds_e"), g + 1)
            dve.wait_ge(S("d1_kept"), HEAD + g)
            nc.vector.scalar_tensor_tensor(e_c[:, 0:EW], psE[1][:, 0:EW], col(CB0), e_b[:, 0:EW], ALU.add,
                                           ALU.mult).then_inc(S("edge_x"), 1)
            yield 18
            dve.wait_ge(S("scores_ps"), NGR + g + 1)
            nc.vector.tensor_copy(grp(score, g), psE[0][0:P, 0:GC]).then_inc(S("scores_out"), 1)

        NDENSE = 2 * NGR - 1

        def lane_count(l, loop, i):
            return 4 * NDENSE + {3: i, 4: of_parity(l) + 3 * i, 5: 4 * of_parity(l) + i}[loop]

        def src1_pe(pe, l, i, g):
            A, B, G, H = psL[l]
            yield 1
            pe.wait_ge(S(f"moved{l}"), moved(3, l, i + 1))
            pe.wait_ge(S(f"ln_rows{l}"), i + 1)
            pe.wait_ge(S(f"s1_msg{l}"), HEAD + i)
            for q in range(Q):
                nc.tensor.transpose(A[:, P * q:P * q + P], xin[l][0:P, 128 * q:128 * q + 128], ident[0:P, 0:P])
                last_t = nc.tensor.transpose(B[:, P * q:P * q + P], g_s[l][0:P, 128 * q:128 * q + 128], ident[0:P, 0:P])
            last_t.then_inc(S(f"ln_t{l}"), 1)
            yield from x1_pe(pe, ATL, l, (S(f"ln_at{l}"), i + 1), i, lane_count(l, 3, i), b_x1[l][:, 0:EW], wt[:, A2C, :], b_gl[l][:, 0:EW], b_s[l][:, 0:EW], B, G)
            yield 8
            pe.wait_ge(S(f"ln_x{l}"), i + 1)
            for q in range(Q):
                lhs = b_h[l][:, P * q:P * q + P]
                nc.tensor.matmul(H[0:P, 2 * q:2 * q + 2], lhs, att[:, 2, :], start=True, stop=True)
                nc.tensor.matmul(A[0:P, 128 * q:128 * q + 128], lhs, wt[:, PHY, :], start=True, stop=True)
                last_m = nc.tensor.matmul(G[0:P, 128 * q:128 * q + 128], lhs, wt[:, NEU, :], start=True, stop=True)
            last_m.then_inc(S(f"rows_ps{l}"), 1)

        def src1_act(act, l, i, g):
            A, B, G, H = psL[l]
            yield 2
            act.wait_ge(S(f"ln_t{l}"), HEAD + i + 1)
            nc.scalar.activation(b_x1[l][:, 0:EW], A[:, 0:EW], ACT.Identity)
            nc.scalar.activation(b_gl[l][:, 0:EW], B[:, 0:EW], ACT.Identity).then_inc(S(f"ln_at{l}"), 1)
            yield from x1_act(act, ATL, l, i, lane_count(l, 3, i), col(CB0), b_s[l][:, 0:EW], B, G)

        def src1_dve(dve, l, i, g):
            A, B, G, H = psL[l]
            yield 0
            dve.wait_ge(S(f"ln_t{l}"), HEAD + i)
            nc.vector.tensor_copy(xin[l][0:P, :], xsg(g)).then_inc(S(f"ln_rows{l}"), 1)
            yield 2
            dve.wait_ge(S(f"ln_t{l}"), HEAD + i + 1)
            nc.vector.tensor_copy(ix_b[l][:, :], grp(src_i, g + 2)).then_inc(S(f"idx{l}"), 1)
            yield 7
            dve.wait_ge(S(f"rstds{l}"), lane_count(l, 3, i) + 1)
            nc.vector.scalar_tensor_tensor(b_h[l][:, 0:EW], B[:, 0:EW], col(CB0), b_s[l][:, 0:EW], ALU.add,
                                           ALU.mult).then_inc(S(f"ln_x{l}"), 1)
            yield 9
            dve.wait_ge(S(f"rows_ps{l}"), i + 1)
            nc.vector.tensor_tensor(grp(score, g), H[0:P, 0:GC], grp(score, g), ALU.add)
            nc.vector.tensor_tensor(t3(b_gl[l][0:P, 512:1024]), t3(A[0:P, :]), bc(grp(ew, g), D), ALU.mult).then_inc(
                S(f"part{l}"), 1)
            dve.wait_ge(S(f"part{l}"), i + 1)
            nc.vector.tensor_tensor(xsg(g), G[0:P, :], b_gl[l][0:P, 512:1024], ALU.add).then_inc(S(f"s1_msg{l}"), 1)

        def unique_pe(pe, l, n):
            pe.wait_ge(S(f"msg_sf{l}"), n + 1)
            for k in range(GC):
                o = psL_GH[l][0:P, 512 * (k // 4) + P * (k % 4):512 * (k // 4) + P * (k % 4) + P]
                last_b = nc.tensor.matmul(o, sf[l][:, k:k + 1].broadcast_to((P, P)), ident[0:P, 0:P], start=True, stop=True)
            last_b.then_inc(S(f"msg_src_ps{l}"), 1)

        def summed_pe(pe, l, n, o):
            pe.wait_ge(S(f"msg_same{l}"), n + 1)
            pe.wait_ge(S(f"msg_zs{l}"), n + 1)
            for k in range(GC):
                last_z = nc.tensor.matmul(o[0:P, D * k:D * k + D], same_src[l][0:P, P * k:P * k + P],
                                          zs[l][0:P, D * k:D * k + D], start=True, stop=True)
            last_z.then_inc(S(f"msg_z_ps{l}"), 1)

        def same_dve(dve, l, n):
            dve.wait_ge(S(f"msg_src_ps{l}"), n + 1)
            for b in range(2):
                last_m = nc.vector.tensor_tensor(t3(same_src[l][0:P, 4 * P * b:4 * P * b + 4 * P], 4),
                                                 t3(psL_GH[l][0:P, 512 * b:512 * b + 4 * P], 4),
                                                 bc(sf[l][:, 4 * b:4 * b + 4], P), ALU.is_equal)
            last_m.then_inc(S(f"msg_same{l}"), 1)

        def dst2_pe(pe, l, i, g):
            A, B, G, H = psL[l]
            n, c = of_parity(l) + i, lane_count(l, 4, i)
            yield 1
            pe.wait_ge(S(f"ln_rows{l}"), n + 1)
            for q in range(Q):
                last_t = nc.tensor.transpose(A[:, P * q:P * q + P], g_s[l][0:P, 128 * q:128 * q + 128], ident[0:P, 0:P])
            last_t.then_inc(S(f"ln_t{l}"), 1)
            yield from x1_pe(pe, ATL, l, (S(f"ln_at{l}"), n + 1), n, c, xg(g), blk_c[:, :], b_gl[l][:, 0:EW], b_s[l][:, 0:EW], B, G)
            yield from mlp_pe(pe, 7, l, NDENSE + i, c + 1, EW, P, psL[l], psL_BG[l])
            yield 21
            for q in range(Q):
                last_z = nc.tensor.matmul(B[0:P, 128 * q:128 * q + 128], b_h[l][:, P * q:P * q + P], wt[:, L2W, :],
                                          start=True, stop=True)
            last_z.then_inc(S(f"rows_ps{l}"), 1)
            unique_pe(pe, l, i)
            yield 24
            pe.wait_ge(S(f"e2_xrow{l}"), i + 1)
            summed_pe(pe, l, i, A)

        def dst2_act(act, l, i, g):
            A, B, G, H = psL[l]
            n, c = of_parity(l) + i, lane_count(l, 4, i)
            yield 2
            act.wait_ge(S(f"ln_t{l}"), HEAD + n + 1)
            nc.scalar.activation(b_gl[l][:, 0:EW], A[:, 0:EW], ACT.Gelu).then_inc(S(f"ln_at{l}"), 1)
            yield 4
            act.wait_ge(S(f"ln_c{l}"), n + 1)
            nc.scalar.activation(b_s[l][:, 0:EW], B[:, 0:EW], ACT.Square).then_inc(S(f"squares{l}"), 1)
            yield 6
            act.wait_ge(S(f"means{l}"), c + 1)
            nc.scalar.activation(b_s[l][:, 0:EW], G[:, 0:EW], ACT.Abs_reciprocal_sqrt,
                                 bias=col(EPSV)).then_inc(S(f"rstds{l}"), 1)
            yield from mlp_act(act, 7, l, NDENSE + i, c + 1, EW, psL[l], psL_BG[l])
            yield 21
            act.wait_ge(S(f"mlp_x2{l}"), NDENSE + i + 1)
            nc.scalar.activation(xg(g), b_h[l][:, 0:EW], ACT.Identity).then_inc(S(f"e2_kept{l}"), 1)

        def dst2_dve(dve, l, i, g):
            A, B, G, H = psL[l]
            n, c = of_parity(l) + i, lane_count(l, 4, i)
            yield 0
            dve.wait_ge(S(f"ln_t{l}"), HEAD + n)
            nc.vector.tensor_copy(t3(g_s[l][0:P, :]), ag[0:P, :, bass.ds(g * GC, GC)].rearrange("p d t -> p t d")).then_inc(
                S(f"ln_rows{l}"), 1)
            dve.wait_ge(S(f"e2_idx{l}"), HEAD + 4 * i)
            nc.vector.tensor_copy(sf[l][:, :], grp(src_i, g)).then_inc(S(f"msg_sf{l}"), 1)
            yield 7
            dve.wait_ge(S(f"rstds{l}"), c + 1)
            dve.wait_ge(S(f"e2_kept{l}"), HEAD + i)
            nc.vector.scalar_tensor_tensor(b_h[l][:, 0:EW], B[:, 0:EW], col(G1), b_s[l][:, 0:EW], ALU.mult,
                                           ALU.mult).then_inc(S(f"mlp_h{l}"), 1)
            yield from mlp_dve(dve, 7, l, NDENSE + i, c + 1, EW, psL[l], xg(g))
            yield 22
            dve.wait_ge(S(f"mlp_t9{l}"), NDENSE + i + 1)
            dve.wait_ge(S(f"moved{l}"), moved(4, l, i))
            nc.vector.tensor_copy(ix_a[l][:, :], grp(last_i, g))
            nc.vector.tensor_tensor(t3(xrow[l][0:P, :]), t3(A[0:P, :]), b2_row[0:P, :].unsqueeze(1).broadcast_to((P, GC, D)),
                                    ALU.add).then_inc(S(f"e2_xrow{l}"), 1)
            dve.wait_ge(S(f"rows_ps{l}"), n + 1)
            nc.vector.tensor_tensor(t3(zs[l][0:P, :]), t3(B[0:P, :]), bc(grp(dis, g), D), ALU.mult).then_inc(S(f"msg_zs{l}"), 1)
            yield 23
            same_dve(dve, l, i)
            dve.wait_ge(S(f"msg_same{l}"), i + 1)
            nc.vector.tensor_tensor(t3(dup[l][0:P, :]), t3(same_src[l][0:P, :]),
                                    low[0:P, 0:P].unsqueeze(1).broadcast_to((P, GC, P)), ALU.mult).then_inc(S(f"e2_idx{l}"), 1)
            dve.wait_ge(S(f"e2_idx{l}"), HEAD + 4 * i + 1)
            nc.vector.tensor_reduce(cnt[l][:, :], t3(dup[l][0:P, :]), AX.X, ALU.add).then_inc(S(f"e2_idx{l}"), 1)
            dve.wait_ge(S(f"e2_idx{l}"), HEAD + 4 * i + 2)
            nc.vector.tensor_scalar(cnt[l][:, :], cnt[l][:, :], 1.0, float(SKIP), ALU.min, ALU.mult)
            nc.vector.scalar_tensor_tensor(sf[l][:, :], sf[l][:, :], float(K), chain_of[:, :], ALU.mult, ALU.add).then_inc(
                S(f"e2_idx{l}"), 1)
            dve.wait_ge(S(f"e2_idx{l}"), HEAD + 4 * i + 3)
            for c in range(K):
                dve.wait_ge(S(f"added{c}{l}"), added(4, l, i))
            nc.vector.tensor_tensor(grp(acc_i, g), cnt[l][:, :], sf[l][:, :], ALU.add)
            nc.vector.tensor_tensor(ix_b[l][:, :], cnt[l][:, :], sf[l][:, :], ALU.add).then_inc(S(f"e2_idx{l}"), 1)
            yield 25
            dve.wait_ge(S(f"msg_z_ps{l}"), i + 1)
            nc.vector.tensor_copy(zrow[l][0:P, :], A[0:P, :]).then_inc(S(f"msg_zrow{l}"), 1)

        def dst3_pe(pe, l, i, g):
            A, B, G, H = psL[l]
            n, c = 2 * of_parity(l) + i, lane_count(l, 5, i)
            yield 1
            pe.wait_ge(S(f"ln_rows{l}"), n + 1)
            for q in range(Q):
                last_t = nc.tensor.transpose(A[:, P * q:P * q + P], xin[l][0:P, 128 * q:128 * q + 128], ident[0:P, 0:P])
            last_t.then_inc(S(f"ln_t{l}"), 1)
            yield from x1_pe(pe, ATL, l, (S(f"ln_at{l}"), n + 1), n, c, xg(g), blk_c[:, :], b_x1[l][:, 0:EW], b_s[l][:, 0:EW], B, G)
            yield 8
            pe.wait_ge(S(f"ln_x{l}"), of_parity(l) + i + 1)
            for q in range(Q):
                last_t = nc.tensor.transpose(A[0:P, 128 * q:128 * q + 128], b_h[l][:, P * q:P * q + P], ident[:, :])
            last_t.then_inc(S(f"rows_ps{l}"), 1)
            unique_pe(pe, l, of_parity(l) + i)
            yield 10
            summed_pe(pe, l, of_parity(l) + i, B)

        def dst3_act(act, l, i, g):
            A, B, G, H = psL[l]
            n, c = 2 * of_parity(l) + i, lane_count(l, 5, i)
            yield 2
            act.wait_ge(S(f"ln_t{l}"), HEAD + n + 1)
            nc.scalar.activation(b_x1[l][:, 0:EW], A[:, 0:EW], ACT.Identity).then_inc(S(f"ln_at{l}"), 1)
            yield from x1_act(act, ATL, l, n, c, col(C2), b_s[l][:, 0:EW], B, G)

        def dst3_dve(dve, l, i, g):
            A, B, G, H = psL[l]
            n, m, c = 2 * of_parity(l) + i, of_parity(l) + i, lane_count(l, 5, i)
            yield 0
            dve.wait_ge(S(f"moved{l}"), moved(5, l, i + 1))
            a = g_a[l][0:P, :].rearrange("p (c k d) -> p c k d", c=GC, k=K)
            nc.vector.tensor_tensor(t3(b_gl[l][0:P, 0:512]), a[:, :, 0, :], a[:, :, 1, :], ALU.add).then_inc(S(f"part{l}"), 1)
            nc.vector.tensor_copy(ix_a[l][:, :], grp(dst_i, g + 2)).then_inc(S(f"idx{l}"), 1)
            nc.vector.tensor_copy(sf[l][:, :], grp(src_i, g)).then_inc(S(f"msg_sf{l}"), 1)
            dve.wait_ge(S(f"part{l}"), of_parity(l) + i + 1)
            nc.vector.tensor_tensor(t3(xin[l][0:P, :]), t3(b_gl[l][0:P, 0:512]), bc(grp(dis, g), D), ALU.mult).then_inc(
                S(f"ln_rows{l}"), 1)
            yield 7
            dve.wait_ge(S(f"rstds{l}"), c + 1)
            nc.vector.scalar_tensor_tensor(b_h[l][:, 0:EW], B[:, 0:EW], col(C2), b_s[l][:, 0:EW], ALU.add,
                                           ALU.mult).then_inc(S(f"ln_x{l}"), 1)
            yield 9
            dve.wait_ge(S(f"rows_ps{l}"), n + 1)
            nc.vector.tensor_tensor(t3(zs[l][0:P, :]), t3(A[0:P, :]), bc(grp(ew, g), D), ALU.mult).then_inc(S(f"msg_zs{l}"), 1)
            same_dve(dve, l, m)
            yield 11
            dve.wait_ge(S(f"msg_z_ps{l}"), m + 1)
            for c in range(K):
                dve.wait_ge(S(f"added{c}{l}"), added(5, l, i))
            nc.vector.tensor_copy(ix_b[l][:, :], grp(acc_i, g))
            nc.vector.tensor_copy(zrow[l][0:P, :], B[0:P, :]).then_inc(S(f"msg_zrow{l}"), 1)

        at_[0] = 0
        l_x2 = [in_ag(R * D) for _ in LANES]
        l_a2 = [in_ag(R * K * D) for _ in LANES]
        l_a3 = [in_ag(R * K * D) for _ in LANES]
        xt_[0] = 0
        l_s2, l_s3, l_u, l_out = ([in_xsn(R * D) for _ in LANES] for _ in range(4))
        l_st = [in_xsn(R * 6) for _ in LANES]
        l_dis, l_m, l_d, l_v, l_rs, l_nb = ([in_xsn(R) for _ in LANES] for _ in range(6))

        def tiles(eng, steps):
            with eng.Fori(0, NTILE // 2) as i:
                both(steps(eng, 0, i), steps(eng, 1, i))
            both(steps(eng, 0, NTILE // 2))

        def t3r(a):
            return a.rearrange("p (r d) -> p r d", r=R)

        LAG = 4

        def last_load(sp, l, i, row):
            sp.wait_ge(S(f"l_sums{l}"), HEAD + 4 * i)
            for t, a in ((x2tab, l_x2), (acc2, l_a2), (acc3, l_a3)):
                sp.dma_start(a[l], t[bass.ds(row, NT), :].rearrange("(p r) d -> p (r d)", p=128)).then_inc(S(f"l_in{l}"), 16)
            sp.dma_start(l_dis[l], distab[bass.ds(row, NT)].rearrange("(p r) -> p r", p=128)).then_inc(S(f"l_in{l}"), 16)

        def last_pool(pool, l, i):
            yield 0
            pool.wait_ge(S(f"l_in{l}"), 64 * (i + 1))
            pool.wait_ge(S(f"l_added{l}"), HEAD + i)
            pool.sem_inc(S("pool_turn"))
            a2 = l_a2[l].rearrange("p (r k d) -> p r k d", r=R, k=K)
            a3 = l_a3[l].rearrange("p (r k d) -> p r k d", r=R, k=K)
            nc.gpsimd.tensor_tensor(t3r(l_s2[l]), a2[:, :, 0, :], a2[:, :, 1, :], ALU.add).then_inc(S(f"l_sums{l}"), 1)
            pool.wait_ge(S(f"l_sums{l}"), HEAD + 4 * i + 1)
            nc.gpsimd.tensor_tensor(t3r(l_s2[l]), t3r(l_s2[l]), bc(l_dis[l], D), ALU.mult).then_inc(S(f"l_sums{l}"), 1)
            pool.wait_ge(S(f"l_sums{l}"), HEAD + 4 * i + 2)
            nc.gpsimd.tensor_tensor(l_s2[l], l_s2[l], l_x2[l], ALU.add).then_inc(S(f"l_sums{l}"), 1)
            nc.gpsimd.tensor_tensor(t3r(l_s3[l]), a3[:, :, 0, :], a3[:, :, 1, :], ALU.add).then_inc(S(f"l_sums{l}"), 1)

        def last_act(act, l, i):
            for m in range(2):
                yield LAG * l + 2 + 3 * m
                act.wait_ge(S(f"l_stats{l}"), 3 * i + m + 1)
                act.wait_ge(S(f"l_act{l}"), HEAD + 3 * i + m)
                nc.scalar.activation(l_rs[l], l_v[l], ACT.Abs_reciprocal_sqrt, bias=col(EPSV)).then_inc(S(f"l_act{l}"), 1)
            yield LAG * l + 7
            act.wait_ge(S(f"l_stats{l}"), 3 * i + 3)
            act.wait_ge(S(f"l_out{l}"), HEAD + 16 * i)
            for r in range(R):
                last_n = nc.scalar.activation(l_out[l][:, D * r:D * r + D], l_u[l][:, D * r:D * r + D], ACT.Identity,
                                              bias=l_nb[l][:, r:r + 1], scale=l_rs[l][:, r:r + 1])
            last_n.then_inc(S(f"l_act{l}"), 1)
            last_tile = isinstance(i, int)
            act.wait_ge(S(f"l_act{l}"), HEAD + 3 * i + 3)
            if last_tile:
                act.wait_ge(S("l_out1"), HEAD + 16 * (NTILE // 2))
            row = N - NT if last_tile else (2 * i + l) * NT
            act.dma_start(out[bass.ds(row, NT), :].rearrange("(p r) d -> p (r d)", p=128), l_out[l]).then_inc(
                S(f"l_out{l}"), 16)

        def last_dve(dve, l, i):
            C = 6
            k = [0]

            def own(ins):
                k[0] += 1
                ins.then_inc(S(f"l_step{l}"), 1)
                dve.wait_ge(S(f"l_step{l}"), C * i + k[0])

            def variance(u):
                for r in range(R):
                    st = nc.vector.bn_stats(l_st[l][:, 6 * r:6 * r + 6], u[:, D * r:D * r + D])
                own(st)
                s = l_st[l].rearrange("p (r c) -> p r c", c=6)
                me, ve, mo, vo = s[:, :, 1], s[:, :, 2], s[:, :, 4], s[:, :, 5]
                nc.vector.tensor_tensor(l_m[l], me, mo, ALU.add)
                nc.vector.tensor_tensor(l_v[l], ve, vo, ALU.add)
                own(nc.vector.tensor_tensor(l_d[l], me, mo, ALU.subtract))
                own(nc.vector.scalar_tensor_tensor(l_d[l], l_d[l], 0.25, l_d[l], ALU.mult, ALU.mult))
                nc.vector.scalar_tensor_tensor(l_v[l], l_v[l], 1.0 / D, l_d[l], ALU.mult, ALU.add).then_inc(S(f"l_stats{l}"), 1)

            yield LAG * l + 1
            dve.wait_ge(S(f"l_sums{l}"), HEAD + 4 * i + 3)
            variance(l_s2[l])
            yield LAG * l + 3
            dve.wait_ge(S(f"l_act{l}"), HEAD + 3 * i + 1)
            dve.wait_ge(S(f"l_sums{l}"), HEAD + 4 * i + 4)
            for r in range(R):
                c = slice(D * r, D * r + D)
                last_x = nc.vector.scalar_tensor_tensor(l_u[l][:, c], l_s2[l][:, c], l_rs[l][:, r:r + 1], l_s3[l][:, c],
                                                        ALU.mult, ALU.add)
            last_x.then_inc(S(f"l_added{l}"), 1)
            dve.wait_ge(S(f"l_added{l}"), HEAD + i + 1)
            yield LAG * l + 4
            variance(l_u[l])
            yield LAG * l + 6
            dve.wait_ge(S(f"l_act{l}"), HEAD + 3 * i + 2)
            nc.vector.scalar_tensor_tensor(l_nb[l], l_m[l], -0.5, l_rs[l], ALU.mult, ALU.mult).then_inc(S(f"l_stats{l}"), 1)
            assert k[0] == C

        VECS = ((B0, bias0), (G1, ln1_g), (LB1, ln1_b), (G2, ln2_g), (LB2, ln2_b), (MB2, mlp_b2), (L2B, L2_b))
        MATS = ((0, W2), (1, W1[:, 0:D]), (2, W_phys), (3, W_neur), (4, L2_W))

        @block.sync
        def _(sp):
            for name in HEADED:
                sp.sem_inc(S(name), HEAD)
            sp.wait_ge(S("cleared"), 1)
            n = 0

            def get(o, a):
                nonlocal n
                sp.dma_start(o, a).then_inc(S("loaded"), 16)
                n += 16

            for v, a in VECS:
                for h in range(2):
                    get(vec[64 * h:64 * h + 64, v:v + 1], a.rearrange("(d o) -> d o", o=1))
            get(col(MB1), mlp_b1.rearrange("(d o) -> d o", o=1))
            get(col(FUS), fusion.rearrange("(a o) -> a o", o=1).broadcast_to((128, 1)))
            for m, a in MATS:
                for h in range(2):
                    get(wbd[64 * h:64 * h + 64, m, 64 * h:64 * h + 64], a)
            for h in range(2):
                get(w1d[:, 64 * h:64 * h + 64], mlp_w1)
                for m, a in ((0, attn[0:D]), (1, attn[D:2 * D]), (2, att_w[0:D]), (3, att_w[D:2 * D])):
                    get(att[64 * h:64 * h + 64, m, h:h + 1], a.rearrange("(d o) -> d o", o=1))
            get(w2s[0:D, :], mlp_w2)
            get(w1e_s[0:D, :], W1[:, D:D + DE])
            get(b2_row[:, :], L2_b.rearrange("(o d) -> o d", o=1).broadcast_to((128, D)))
            get(src_i[:, 0:TC], src.rearrange("(p t) -> p t", p=P))
            get(dst_i[:, 0:TC], dst.rearrange("(p t) -> p t", p=P))
            get(ew[:, :], edge_weight.rearrange("(p t) -> p t", p=P))
            prev_i, next_i = prev_f.bitcast(i32), next_f.bitcast(i32)
            get(prev_i[1:P, :], dst[TC - 1:E - 1].rearrange("(p t) -> p t", t=TC))
            get(prev_i[0:1, 1:TC], dst[0:TC - 1].rearrange("(o t) -> o t", o=1))
            get(next_i[0:P - 1, :], dst[1:E - TC + 1].rearrange("(p t) -> p t", t=TC))
            get(next_i[P - 1:P, 0:TC - 1], dst[E - TC + 1:E].rearrange("(o t) -> o t", o=1))
            assert n == LOADED

            def fill(table, part, parts, s):
                v = table.rearrange("n d -> (n d)").rearrange("(p r f) -> p r f", p=128, f=zero.shape[1])
                n = v.shape[1] // parts
                sp.dma_start(v[:, bass.ds(part * n, n), :], zero[:, :].unsqueeze(1).broadcast_to((128, n, v.shape[2]))).then_inc(
                    S(s), 16)

            fill(agg0, 0, 1, "zeroed0")
            sp.wait_ge(S("w1e_t"), 1)
            for c in range(GC):
                sp.dma_start(w_e[DE * c:DE * c + DE, c // 2, 64 * (c % 2):64 * (c % 2) + 64], w1e_t[0:DE, :]).then_inc(
                    S("w_e_in"), 16)
            sp.wait_ge(S("dis_made"), 1)
            sp.dma_start(distab.rearrange("(p h) -> p h", p=128), deg).then_inc(S("dis_out"), 16)

            eav = edge_attr.rearrange("(p t) d -> p (t d)", p=P)

            def edge_load(par, i, g):
                sp.dma_start(ea_s[par][0:P, :], eav[:, bass.ds(g * (GC * DE), GC * DE)]).then_inc(S(f"ea_in{par}"), 16)

            def feed(loop, par, i, g):
                peeled = isinstance(g, int)
                n = turn(loop, g)
                ends = (loop == 0 and peeled and g == NGR - 1, loop == 1 and peeled and g == NGR - 1)
                if not (ends[0] or ends[1]):
                    for l in LANES:
                        dense_load(sp, l, n + 1, row(loop, g + 1, l))
                if not ends[0]:
                    for l in LANES:
                        if ends[1] and l == 1:
                            sp.wait_ge(S("blk_st0"), HEAD + 16 * NDENSE)
                            sp.wait_ge(S("blk_st1"), HEAD + 16 * (NDENSE - 1))
                        dense_store(sp, l, n, row(loop, g, l))
                fill((acc2, acc3)[loop], g, NGR, f"zeroed{2 + loop}")
                if loop == 0 and not (peeled and g + 2 >= NGR):
                    sp.wait_ge(S(f"rows0_used{par}"), HEAD + i + 1)
                    edge_load(par, i + 1, g + 2)

            edge_load(0, 0, 0)
            edge_load(1, 0, 1)
            for l in LANES:
                dense_load(sp, l, 0, l * NB)
            for loop in range(2):
                with sp.Fori(0, NGR // 2 - 1) as i:
                    for par in LANES:
                        feed(loop, par, i, 2 * i + par)
                for g in range(NGR - 3, NGR):
                    feed(loop, g % 2, g // 2, g)

            for c in range(K):
                for par in LANES:
                    sp.wait_ge(S(f"added{c}{par}"), added(6, par, 0))
            for l in LANES:
                last_load(sp, l, 0, l * NT)
            with sp.Fori(0, NTILE // 2 - 1) as i:
                for l in LANES:
                    last_load(sp, l, i + 1, (2 * i + 2 + l) * NT)
            last_load(sp, 0, NTILE // 2, N - NT)
            sp.wait_ge(S("l_out0"), HEAD + 16 * (NTILE // 2 + 1))
            sp.wait_ge(S("l_out1"), HEAD + 16 * (NTILE // 2))

        @block.gpsimd
        def _(pool):
            nc.gpsimd.memset(ident[:, :], 1.0).then_inc(S("pool_c"), 1)
            nc.gpsimd.memset(low[:, :], 1.0).then_inc(S("pool_c"), 1)
            pool.wait_ge(S("pool_c"), 2)
            nc.gpsimd.affine_select(out=ident[:, :], in_=ident[:, :], pattern=[[-1, 128]], compare_op=ALU.is_equal, fill=0.0,
                                    base=0, channel_multiplier=1).then_inc(S("pool_c"), 1)
            nc.gpsimd.affine_select(out=low[:, :], in_=low[:, :], pattern=[[-1, 128]], compare_op=ALU.is_gt, fill=0.0,
                                    base=0, channel_multiplier=1).then_inc(S("pool_c"), 1)
            nc.gpsimd.iota(iota_lo, pattern=[[1, 128]], base=0, channel_multiplier=0,
                           allow_small_or_imprecise_dtypes=True).then_inc(S("pool_c"), 1)
            nc.gpsimd.iota(iota_hi, pattern=[[1, HB]], base=0, channel_multiplier=0,
                           allow_small_or_imprecise_dtypes=True).then_inc(S("pool_c"), 1)
            nc.gpsimd.iota(chain_of[:, :], pattern=[[0, GC // K], [1, K]], base=0, channel_multiplier=0,
                           allow_small_or_imprecise_dtypes=True).then_inc(S("pool_c"), 1)

            def at(ap):
                return bass.IndirectOffsetOnAxis(ap=ap, axis=0)

            def gather(o, table, ix, s):
                pool.indirect_dma_start(out=o, out_offset=None, in_=table, in_offset=at(ix)).then_inc(s, 16)

            def scatter(table, rows_n, ix, a, s, add=False):
                kw = dict(compute_op=ALU.add) if add else {}
                pool.indirect_dma_start(out=table, out_offset=at(ix), in_=a, in_offset=None, bounds_check=rows_n - 1,
                                        oob_is_err=False, **kw).then_inc(s, 16)

            def cols(a, k, w=D):
                return a[0:P, w * k:w * k + w]

            def g0(par, i, g):
                pool.wait_ge(S(f"idx{par}"), i + 1)
                pool.wait_ge(S(f"rows0_used{par}"), HEAD + i)
                pool.sem_inc(S("pool_turn"))
                for k in range(GC):
                    gather(cols(g_s[par], k), x, ix_a[par][:, k:k + 1], S(f"moved{par}"))
                    gather(cols(g_d[par], k), x, ix_b[par][:, k:k + 1], S(f"moved{par}"))
            groups(pool, g0)

            pool.wait_ge(S("dis_out"), 16)
            pool.wait_ge(S("w_made"), 1)
            for t in range(TC):
                gather(dis[:, t:t + 1], distab.rearrange("(n o) -> n o", o=1), dst_i[:, t:t + 1], S(f"added{t % K}{t // K % 2}"))

            def s1(par, i, g):
                pool.wait_ge(S("d1_idx"), g + 1)
                pool.sem_inc(S("pool_turn"))
                for k in range(GC):
                    scatter(agg0, N, ix_a[par][:, k:k + 1], cols(g_s[par], k), S(f"moved{par}"))
            pool.wait_ge(S("zeroed0"), 16)
            groups(pool, s1)

            for par in LANES:
                pool.wait_ge(S(f"moved{par}"), moved(3, par, 0))

            def g3(par, i, g):
                pool.wait_ge(S(f"idx{par}"), of_parity(par) + 1 + i + 1)
                pool.sem_inc(S("pool_turn"))
                for k in range(GC):
                    gather(cols(g_s[par], k), agg0, ix_b[par][:, k:k + 1], S(f"moved{par}"))
            groups(pool, g3)

            for l in LANES:
                pool.wait_ge(S(f"blk_st{l}"), HEAD + 16 * NDENSE)
            pool.wait_ge(S("zeroed2"), 16 * NGR)

            def chain_wait(loop, c, par, i, k):
                if k >= K:
                    pool.wait_ge(S(f"added{c}{par}"), added(loop, par, i) + 16 * (k // K))
                elif par == 0:
                    pool.wait_ge(S(f"added{c}1"), added(loop, 1, i))
                else:
                    pool.wait_ge(S(f"added{c}0"), added(loop, 0, i + 1))
                pool.sem_inc(S("pool_turn"))

            def s2(par, i, g):
                pool.wait_ge(S(f"e2_xrow{par}"), i + 1)
                pool.sem_inc(S("pool_turn"))
                for k in range(GC // 2):
                    scatter(x2tab, N, ix_a[par][:, k:k + 1], cols(xrow[par], k), S(f"moved{par}"))
                pool.wait_ge(S(f"msg_zrow{par}"), i + 1)
                for k in range(GC):
                    chain_wait(4, k % K, par, i, k)
                    scatter(acc2_rows, N * K, ix_b[par][:, k:k + 1], cols(zrow[par], k), S(f"added{k % K}{par}"), add=True)
                    if k % 2:
                        j = GC // 2 + k // 2
                        scatter(x2tab, N, ix_a[par][:, j:j + 1], cols(xrow[par], j), S(f"moved{par}"))
            groups(pool, s2)

            for c in range(K):
                for par in LANES:
                    pool.wait_ge(S(f"added{c}{par}"), added(5, par, 0))
            for par in LANES:
                pool.wait_ge(S(f"moved{par}"), moved(5, par, 0))
            pool.wait_ge(S("zeroed3"), 16 * NGR)

            def g6(par, i, g):
                pool.wait_ge(S(f"idx{par}"), 2 * (of_parity(par) + 1) + i + 1)
                pool.sem_inc(S("pool_turn"))
                for k in range(GC):
                    gather(cols(g_a[par], k, K * D), acc2, ix_a[par][:, k:k + 1], S(f"moved{par}"))

            def s3(par, i, g):
                pool.wait_ge(S(f"msg_zrow{par}"), of_parity(par) + i + 1)
                for k in range(GC):
                    chain_wait(5, k % K, par, i, k)
                    scatter(acc3_rows, N * K, ix_b[par][:, k:k + 1], cols(zrow[par], k), S(f"added{k % K}{par}"), add=True)

            g6(0, 0, 0)
            with pool.Fori(0, NGR // 2) as i:
                g6(1, i, 2 * i + 1)
                s3(0, i, 2 * i)
                g6(0, i + 1, 2 * i + 2)
                s3(1, i, 2 * i + 1)
            s3(0, NGR // 2, NGR - 1)

            tiles(pool, last_pool)

        @block.tensor
        def _(pe):
            pe.wait_ge(S("pool_c"), 7)
            pe.wait_ge(S("consts"), 1)
            z = oh_hi[0][0:P, 0:HH]
            pe.wait_ge(S("hist_ready"), 1)
            for h in range(2):
                last_h = nc.tensor.matmul(psGH[0][:, 512 * h:512 * h + HH], oh_lo[0][0:P, :], z, start=True, stop=False)
            last_h.then_inc(S("hist_pe"), 1)
            with pe.Fori(0, TC // 2) as i:
                for l in LANES:
                    pe.wait_ge(S(f"onehot{l}"), i + 1)
                    for h in range(2):
                        last_h = nc.tensor.matmul(psGH[0][:, 512 * h:512 * h + HH], oh_lo[l][0:P, :],
                                                  oh_hi[l][0:P, HH * h:HH * h + HH], start=False, stop=False)
                    last_h.then_inc(S(f"onehot_used{l}"), 1)
            pe.wait_ge(S("hist_ready"), 2)
            for h in range(2):
                last_h = nc.tensor.matmul(psGH[0][:, 512 * h:512 * h + HH], oh_lo[0][0:P, :], z, start=False, stop=True)
            last_h.then_inc(S("hist_pe"), 1)
            pe.wait_ge(S("loaded"), LOADED)
            nc.tensor.matmul(psA[0][:, 0:128], wbd[:, 0, :], blk_c[:, :], start=True, stop=True)
            for m in range(1, 4):
                nc.tensor.matmul(psA[0][:, 128 * m:128 * m + 128], wbd[:, m, :], ident[:, :], start=True, stop=True)
            nc.tensor.matmul(psB[0][:, 0:128], wbd[:, 4, :], ident[:, :], start=True, stop=True)
            nc.tensor.transpose(psB[0][:, 128:256], w1d, ident[:, :])
            nc.tensor.matmul(psB[0][:, 256:320], w2s[0:D, :], blk_c[0:D, 0:D], start=True, stop=True)
            nc.tensor.transpose(psB[0][0:DE, 384:384 + D], w1e_s[0:D, :], ident[0:D, 0:D]).then_inc(S("setup_ps"), 1)
            pe.wait_ge(S("w_made"), 1)
            for j, v in enumerate((B0, CR, LB2, L2B)):
                nc.tensor.matmul(psA[1][:, j:j + 1], blk_c[:, :], col(v), start=True, stop=True)
            nc.tensor.matmul(psA[1][:, 4:5], wt[0:D, W1T, :], vec[0:D, LB1:LB1 + 1], start=True, stop=True)
            for f in range(4):
                last_f = nc.tensor.matmul(psB[1][0:D, P * f:P * f + P], ends[:, f:f + 1].broadcast_to((P, D)),
                                          ident[0:P, 0:P], start=True, stop=True)
            last_f.then_inc(S("setup_ps"), 1)
            end_phase(pe, 1)

            groups_and_blocks(pe, 0, scores0_pe, dense_pe)
            end_phase(pe, 2)
            for k, n in enumerate((1, 1, 1, 1, D, D)):
                carries_pe(pe, k + 1, n)
            end_phase(pe, 3)
            groups_and_blocks(pe, 1, dst1_pe, dense_pe)
            end_phase(pe, 4)
            group_pairs(pe, src1_pe)
            end_phase(pe, 5)
            for k, n in enumerate((1, 1, 1, 1, D, D)):
                carries_pe(pe, 6 + k + 1, n)
            end_phase(pe, 6)
            group_pairs(pe, dst2_pe)
            end_phase(pe, 7)
            group_pairs(pe, dst3_pe)

        @block.scalar
        def _(act):
            act.wait_ge(S("loaded"), LOADED)
            nc.scalar.activation(col(FUN), col(FUS), ACT.Sigmoid).then_inc(S("fusion"), 1)
            act.wait_ge(S("deg_max"), 1)
            nc.scalar.activation(deg, deg, ACT.Abs_reciprocal_sqrt).then_inc(S("deg_rs"), 1)
            end_phase(act, 1)
            groups_and_blocks(act, 0, scores0_act, dense_act)
            end_phase(act, 2)
            softmax_act(act, 0)
            end_phase(act, 3)
            groups_and_blocks(act, 1, dst1_act, dense_act)
            end_phase(act, 4)
            group_pairs(act, src1_act)
            end_phase(act, 5)
            softmax_act(act, 1)
            end_phase(act, 6)
            group_pairs(act, dst2_act)
            end_phase(act, 7)
            group_pairs(act, dst3_act)
            tiles(act, last_act)

        @block.vector
        def _(dve):
            step = [0]

            def own(ins):
                step[0] += 1
                ins.then_inc(S("seg_step"), 1)
                dve.wait_ge(S("seg_step"), step[0])

            nc.vector.memset(wbd, 0.0)
            nc.vector.memset(w_e, 0.0)
            nc.vector.memset(att[:, :, :], 0.0)
            nc.vector.memset(zero[:, :], 0.0)
            nc.vector.memset(src_i[:, :], 0)
            nc.vector.memset(dst_i[:, :], 0)
            nc.vector.memset(last_i[:, :], 0)
            nc.vector.memset(acc_i[:, :], 0)
            nc.vector.memset(prev_f.bitcast(i32)[0:P, :], -1)
            nc.vector.memset(next_f.bitcast(i32)[0:P, :], -1)
            nc.vector.memset(col(EPSV), EPS)
            own(nc.vector.memset(w2p[:, :, :], 0.0))
            dve.drain().then_inc(S("cleared"), 1)
            own(nc.vector.memset(blk_j[:, :], 0.0))
            nc.vector.memset(blk_j[0:64, 0:64], 1.0 / D)
            own(nc.vector.memset(blk_j[64:128, 64:128], 1.0 / D))
            dve.wait_ge(S("pool_c"), 7)
            nc.vector.tensor_tensor(blk_c[:, :], ident[:, :], blk_j[:, :], ALU.subtract).then_inc(S("consts"), 1)
            dve.wait_ge(S("loaded"), LOADED)

            own(nc.vector.tensor_copy(dst_f[0:P, :], src_i[:, 0:TC]))
            own(nc.vector.tensor_scalar(src_hi[0:P, :], dst_f[0:P, :], 1.0 / HB, None, ALU.mult))
            own(nc.vector.tensor_copy(tmp_i[0:P, :], src_hi[0:P, :]))
            own(nc.vector.tensor_copy(src_lo[0:P, :], tmp_i[0:P, :]))
            own(nc.vector.scalar_tensor_tensor(src_hi[0:P, :], src_lo[0:P, :], -float(HB), dst_f[0:P, :], ALU.mult, ALU.add))
            for op, bound, sign in ((ALU.is_lt, 0.0, 1.0), (ALU.is_ge, float(HB), -1.0)):
                own(nc.vector.tensor_scalar(tmp_f[0:P, :], src_hi[0:P, :], bound, sign, op, ALU.mult))
                own(nc.vector.tensor_tensor(src_lo[0:P, :], src_lo[0:P, :], tmp_f[0:P, :], ALU.subtract))
                own(nc.vector.scalar_tensor_tensor(src_hi[0:P, :], tmp_f[0:P, :], float(HB), src_hi[0:P, :], ALU.mult, ALU.add))
            nc.vector.memset(oh_lo[0][0:P, :], 0.0)
            own(nc.vector.memset(oh_hi[0][0:P, :], 0.0))
            dve.drain().then_inc(S("hist_ready"), 1)
            dve.wait_ge(S("hist_pe"), 1)
            with dve.Fori(0, TC // 2) as i:
                for l in LANES:
                    dve.wait_ge(S(f"onehot_used{l}"), HEAD + i)
                    nc.vector.tensor_scalar(oh_lo[l][0:P, :], iota_lo[0:P, :], src_lo[0:P, bass.ds(2 * i + l, 1)], None,
                                            ALU.is_equal)
                    nc.vector.tensor_scalar(oh_hi[l][0:P, :], iota_hi[0:P, :], src_hi[0:P, bass.ds(2 * i + l, 1)], None,
                                            ALU.is_equal).then_inc(S(f"onehot{l}"), 1)
            dve.wait_ge(S("onehot_used0"), HEAD + TC // 2)
            nc.vector.memset(oh_lo[0][0:P, :], 0.0)
            nc.vector.memset(oh_hi[0][0:P, :], 0.0).then_inc(S("hist_ready"), 1)
            dve.wait_ge(S("hist_pe"), 2)
            d_ps = psGH[0][:, :].rearrange("p (h c) -> p h c", h=2)[:, :, 0:HH]
            nc.vector.tensor_scalar(deg_on.rearrange("p (h c) -> p h c", h=2), d_ps, 0.0, None, ALU.is_gt)
            nc.vector.tensor_scalar(deg.rearrange("p (h c) -> p h c", h=2), d_ps, 1.0, None, ALU.max).then_inc(S("deg_max"), 1)

            dve.wait_ge(S("setup_ps"), 1)
            nc.vector.tensor_copy(w1e_t[0:DE, :], psB[0][0:DE, 384:384 + D]).then_inc(S("w1e_t"), 1)
            dve.wait_ge(S("fusion"), 1)
            own(nc.vector.tensor_scalar(col(T0), col(FUN), -1.0, 1.0, ALU.mult, ALU.add))
            nc.vector.tensor_copy(wt[:, 0:2, :].rearrange("p w c -> p (w c)"), psA[0][:, 0:256])
            nc.vector.tensor_scalar(wt[:, PHY, :], psA[0][:, 256:384], col(FUN), None, ALU.mult)
            nc.vector.tensor_scalar(wt[:, NEU, :], psA[0][:, 384:512], col(T0), None, ALU.mult)
            nc.vector.tensor_copy(wt[:, L2W:L2W + 2, :].rearrange("p w c -> p (w c)"), psB[0][:, 0:256])
            nc.vector.tensor_scalar(wt[:, DG2, :], blk_c[:, :], col(G2), None, ALU.mult)
            nc.vector.tensor_copy(w2p[:, 0, 0:64], psB[0][:, 256:320])
            nc.vector.tensor_copy(w2p[:, 1, 64:128], psB[0][:, 256:320])
            nc.vector.tensor_tensor(col(CR), col(LB1), col(MB2), ALU.add)

            own(nc.vector.tensor_copy(tmp_f[0:P, :], prev_f.bitcast(i32)[0:P, :]))
            own(nc.vector.tensor_copy(src_lo[0:P, :], next_f.bitcast(i32)[0:P, :]))
            own(nc.vector.tensor_copy(dst_f[0:P, :], dst_i[:, 0:TC]))
            nc.vector.tensor_tensor(same[:, :], dst_f[0:P, :], tmp_f[0:P, :], ALU.is_equal)
            own(nc.vector.tensor_tensor(nxt[:, :], dst_f[0:P, :], src_lo[0:P, :], ALU.is_equal))
            nc.vector.tensor_scalar(last[:, :], nxt[:, :], -1.0, 1.0, ALU.mult, ALU.add)
            nc.vector.tensor_scalar(pen_f[:, :], same[:, :], 1.0, -NEG, ALU.subtract, ALU.mult)
            nc.vector.tensor_scalar(pen_b[:, :], nxt[:, :], 1.0, -NEG, ALU.subtract, ALU.mult)
            own(nc.vector.scalar_tensor_tensor(tmp_f[0:P, :], nxt[:, :], float(SKIP), dst_f[0:P, :], ALU.mult, ALU.add))
            nc.vector.tensor_copy(last_i[:, 0:TC], tmp_f[0:P, :])
            for f, a in enumerate((same, nxt, pen_f, pen_b)):
                nc.vector.tensor_reduce(ends[:, f:f + 1], a[:, :], AX.X, ALU.min)
            for l in LANES:
                nc.vector.tensor_copy(ix_a[l][:, :], src_i[:, GC * l:GC * l + GC])
                nc.vector.tensor_copy(ix_b[l][:, :], dst_i[:, GC * l:GC * l + GC])
            dve.drain().then_inc(S("w_made"), 1)
            nc.vector.nop().then_inc(S("idx0"), 1)
            nc.vector.nop().then_inc(S("idx1"), 1)
            dve.wait_ge(S("deg_rs"), 1)
            nc.vector.tensor_tensor(deg, deg, deg_on, ALU.mult).then_inc(S("dis_made"), 1)
            dve.wait_ge(S("setup_ps"), 2)
            nc.vector.tensor_copy(vec[:, CB0:CB0 + 4], psA[1][:, 0:4])
            nc.vector.tensor_tensor(col(HB1), psA[1][:, 4:5], col(MB1), ALU.add)
            nc.vector.tensor_copy(row_flags[:, :, :].rearrange("d f p -> d (f p)"), psB[1][0:D, 0:4 * P])
            end_phase(dve, 1)

            groups_and_blocks(dve, 0, scores0_dve, dense_dve)
            end_phase(dve, 2)
            softmax_dve(dve, 0, step)
            sums_dve(dve, 0, step)
            end_phase(dve, 3)
            groups_and_blocks(dve, 1, dst1_dve, dense_dve)
            for l in LANES:
                nc.vector.tensor_copy(ix_b[l][:, :], src_i[:, GC * l:GC * l + GC]).then_inc(S(f"idx{l}"), 1)
            for l in LANES:
                dve.wait_ge(S(f"blk_st{l}"), HEAD + 16 * NDENSE)
            end_phase(dve, 4)
            group_pairs(dve, src1_dve)
            end_phase(dve, 5)
            softmax_dve(dve, 1, step)
            sums_dve(dve, 1, step)
            for par in LANES:
                for c in range(K):
                    dve.wait_ge(S(f"added{c}{par}"), added(4, par, 0))
            end_phase(dve, 6)
            group_pairs(dve, dst2_dve)
            for par in LANES:
                dve.wait_ge(S(f"moved{par}"), moved(5, par, 0))
                for c in range(K):
                    dve.wait_ge(S(f"added{c}{par}"), added(5, par, 0))
            for l in LANES:
                nc.vector.tensor_copy(ix_a[l][:, :], dst_i[:, GC * l:GC * l + GC]).then_inc(S(f"idx{l}"), 1)
            end_phase(dve, 7)
            group_pairs(dve, dst3_dve)
            tiles(dve, last_dve)


_INS = ['x', 'src', 'dst', 'edge_attr_16', 'edge_weight', 'L0_gnn_W1', 'L0_gnn_W2', 'L0_gnn_attn', 'L0_gnn_bias',
        'L1_gnn_W_phys', 'L1_gnn_W_neur', 'L1_gnn_att_w', 'L1_gnn_channel_fusion', 'L1_gnn_mlp_w1', 'L1_gnn_mlp_b1',
        'L1_gnn_mlp_w2', 'L1_gnn_mlp_b2', 'L1_gnn_ln1_g', 'L1_gnn_ln1_b', 'L1_gnn_ln2_g', 'L1_gnn_ln2_b', 'L2_gnn_W',
        'L2_gnn_b']


def kernel(**inputs):
    import numpy as _np
    import concourse.bacc as _bacc
    from concourse import mybir as _mybir
    from concourse.bass_utils import run_bass_kernel_spmd as _run

    nc = _bacc.Bacc("TRN2", target_bir_lowering=False, num_devices=1)
    arrays, args = {}, []
    for name in _INS:
        a = _np.ascontiguousarray(inputs[name])
        if a.ndim == 0:
            a = a.reshape(1)
        arrays[f"in_{name}_dram"] = a
        args.append(nc.dram_tensor(f"in_{name}_dram", a.shape, _mybir.dt.from_np(a.dtype), kind="ExternalInput").ap())
    shape = inputs["x"].shape
    args.append(nc.dram_tensor("out_0_dram", shape, _mybir.dt.float32, kind="ExternalOutput").ap())
    gnn_resnorm_kernel(nc, *args)
    r = _run(nc, [arrays], core_ids=[0])
    return r.results[0]["out_0_dram"]
```

```python
import concourse.bass as bass
from concourse import mybir
from contextlib import ExitStack

fp32 = mybir.dt.float32
fp16 = mybir.dt.float16
i32 = mybir.dt.int32
ALU = mybir.AluOpType
ACT = mybir.ActivationFunctionType
AX = mybir.AxisListType


def gnn_resnorm_kernel(nc, x, src, dst, edge_attr, edge_weight, W1, W2, attn, bias0, W_phys, W_neur, att_w,
                       fusion, mlp_w1, mlp_b1, mlp_w2, mlp_b2, ln1_g, ln1_b, ln2_g, ln2_b, L2_W, L2_b, out):
    N, D = x.shape
    E, DE = edge_attr.shape
    HID = mlp_w1.shape[0]
    P = 125
    TC = E // P
    GC = 8
    NGR = TC // GC
    Q = GC // 2
    EW = Q * P
    NB = 1024
    NBLK = -(-N // NB)
    R = 16
    NT = P * R
    NTILE = N // NT
    K = 2
    HB = 782
    HH = HB // 2
    EPS = 1e-5
    NEG = -1e30
    SKIP = 1 << 22

    agg0 = nc.dram_tensor("agg0", (N, D), fp32).ap()
    x2tab = nc.dram_tensor("x2tab", (N, D), fp32).ap()
    acc2 = nc.dram_tensor("acc2", (N, K * D), fp32).ap()
    acc3 = nc.dram_tensor("acc3", (N, K * D), fp32).ap()
    distab = nc.dram_tensor("distab", (128 * HB,), fp32).ap()
    acc2_rows = acc2.rearrange("n (k d) -> (n k) d", k=K)
    acc3_rows = acc3.rearrange("n (k d) -> (n k) d", k=K)

    ctx = ExitStack()
    with ctx:
        def sb(name, shape, dt=fp32):
            return ctx.enter_context(nc.sbuf_tensor(name, shape, dt))

        xsn = sb("xsn", [128, TC, D])
        xdt = sb("xdt", [128, TC // 2 * P])
        ag = sb("ag", [128, D, TC])
        src_i, dst_i, last_i, acc_i = (sb(n, [P, TC + 2 * GC], i32) for n in ("src_i", "dst_i", "last_i", "acc_i"))
        ew, same, nxt, last, pen_f, pen_b, score, sm1, sm2, dis = (
            sb(n, [P, TC]) for n in ("ew", "same", "nxt", "last", "pen_f", "pen_b", "score", "sm1", "sm2", "dis"))
        edge_col, carry = (sb(n, [P, D]) for n in ("edge_col", "carry"))
        rows = sb("rows", [D, P + 1])
        ends = sb("ends", [P, 4])
        row_flags = sb("row_flags", [D, 4, P])
        ident, blk_j, blk_c, low = (sb(n, [128, 128]) for n in ("ident", "blk_j", "blk_c", "low"))
        wt = sb("wt", [128, 7, 128])
        A2C, W1X, PHY, NEU, L2W, W1T, DG2 = range(7)
        w2p = sb("w2p", [128, 2, 128])
        att = sb("att", [128, 4, 2])
        vec = sb("vec", [128, 17])
        B0, G1, LB1, G2, LB2, MB2, MB1, L2B, FUS, EPSV, CB0, CR, CT, C2, HB1, FUN, T0 = range(17)
        b2_row = sb("b2_row", [128, D])
        zero = sb("zero", [128, 250])
        LANES = range(2)

        def lane(name, cols):
            return [sb(f"{name}{l}", [128, cols]) for l in LANES]

        xin, b_x1, b_h, b_s = (lane(n, 512) for n in ("xin", "b_x1", "b_h", "b_s"))
        b_gl = lane("b_gl", 1024)
        e_a, e_b, e_c = (sb(n, [128, 512]) for n in ("e_a", "e_b", "e_c"))
        g_s = lane("g_s", GC * D)
        ix_a = [sb(f"ix_a{l}", [P, GC], i32) for l in LANES]
        ix_b = [sb(f"ix_b{l}", [P, GC], i32) for l in LANES]
        sf, cnt = ([sb(f"{n}{l}", [P, GC]) for l in LANES] for n in ("sf", "cnt"))
        chain_of = sb("chain_of", [P, GC])

        ps = ctx.enter_context(nc.psum_tensor("ps", [128, 8 * 512], fp32))

        def bank(j, n=1):
            return ps[:, 512 * j:512 * (j + n)]

        psD = [[bank(3 * l + j) for j in range(3)] for l in LANES]
        psE = [bank(6), bank(7)]
        psL = [[bank(4 * l + j) for j in range(4)] for l in LANES]
        psD_BG = [bank(3 * l + 1, 2) for l in LANES]
        psL_BG = [bank(4 * l + 1, 2) for l in LANES]
        psL_GH = [bank(4 * l + 2, 2) for l in LANES]
        psA, psB, psGH = [bank(0), bank(1)], [bank(2), bank(3)], [bank(4, 2)]

        agf = ag[:, :, :].rearrange("p d t -> p (d t)")
        at_ = [0]

        def in_ag(cols):
            at_[0] += cols
            return agf[:, at_[0] - cols:at_[0]]

        wbd = in_ag(6 * 128).rearrange("p (w c) -> p w c", w=6)
        w_e = in_ag(Q * 128).rearrange("p (w c) -> p w c", w=Q)
        w1e_s, w1e_t, w1d, w2s = in_ag(DE), in_ag(D), in_ag(128), in_ag(HID)
        g_d = [in_ag(GC * D) for _ in LANES]
        ea_s = [in_ag(GC * DE) for _ in LANES]
        iota_lo32, iota_hi32 = in_ag(128), in_ag(HB)
        iota_lo, iota_hi = in_ag(64).bitcast(fp16), in_ag(HH).bitcast(fp16)
        oh_lo = [in_ag(64).bitcast(fp16) for _ in LANES]
        oh_hi = [in_ag(HH).bitcast(fp16) for _ in LANES]
        deg, deg_on = in_ag(HB), in_ag(HB)
        src_lo, src_hi, dst_f, prev_f, next_f, tmp_f = (in_ag(TC) for _ in range(6))
        tmp_i = in_ag(TC).bitcast(i32)

        xsf = xsn[:, :, :].rearrange("p t d -> p (t d)")
        xt_ = [0]

        def in_xsn(cols):
            xt_[0] += cols
            return xsf[:, xt_[0] - cols:xt_[0]]

        xrow = [in_xsn(GC * D) for _ in LANES]
        zrow = [in_xsn(GC * D) for _ in LANES]
        g_a = [in_xsn(GC * K * D) for _ in LANES]
        zs = [in_xsn(GC * D) for _ in LANES]
        same_src = [in_xsn(GC * P) for _ in LANES]
        dup = [in_xsn(GC * P) for _ in LANES]

        LOADED = 16 * (2 * 7 + 2 + 2 * 5 + 2 * 5 + 3 + 3 + 4)
        names = {}

        HEAD = 1
        LANED = ("blk_xo", "blk_st", "blk_t1", "s1_msg", "ln_t", "e2_idx", "e2_kept", "rows0_used",
                 "onehot_used", "l_act", "l_outa", "l_outb")
        HEADED = ("scores_out", "d1_kept", *(f"{name}{l}" for name in LANED for l in LANES))

        def S(name):
            if name not in names:
                names[name] = ctx.enter_context(nc.semaphore(name))
            return names[name]

        def col(v):
            return vec[:, v:v + 1]

        def grp(a, g):
            return a[:, bass.ds(g * GC, GC)]

        def xg(g):
            return xdt[:, bass.ds(g * EW, EW)]

        def xsg(g):
            return xsf[0:P, bass.ds(g * (GC * D), GC * D)]

        def bc(a, d):
            return a.unsqueeze(2).broadcast_to((a.shape[0], a.shape[1], d))

        def t3(a, c=GC):
            return a.rearrange("p (c d) -> p c d", c=c)

        block = ctx.enter_context(nc.Block())

        def groups(eng, body):
            with eng.Fori(0, NGR // 2) as i:
                body(0, i, 2 * i)
                body(1, i, 2 * i + 1)
            body(0, NGR // 2, NGR - 1)

        def group_pairs(eng, *steps):
            with eng.Fori(0, NGR // 2) as i:
                both(*(s(eng, l, i, 2 * i + l) for s in steps for l in LANES))
            both(*(s(eng, 0, NGR // 2, NGR - 1) for s in steps))

        def of_parity(par):
            return (NGR + 1 - par) // 2

        def moved(loop, par, i):
            return 16 * GC * ((0, 2, 3, 4, 5)[loop - 1] * of_parity(par) + (2 if loop == 1 else 1) * i)

        def added(loop, par, i):
            return 16 * (TC // (2 * K) + (GC // K) * ((loop - 4) * of_parity(par) + i))

        def both(*programs, lags=()):
            at = [next(p) for p in programs]
            while any(a is not None for a in at):
                j = min((j for j in range(len(at)) if at[j] is not None), key=lambda j: at[j] + (lags[j] if lags else 0))
                at[j] = next(programs[j], None)

        assert NBLK == 2 * (2 * NGR - 1)

        def turn(loop, g):
            return loop * (NGR - 1) + g

        def row(loop, g, l):
            if loop == 1 and isinstance(g, int) and g == NGR - 1 and l == 1:
                return N - NB
            return (2 * turn(loop, g) + l) * NB

        EDGE_LAG = (10, 0.5)

        def groups_and_blocks(eng, loop, edges, dense):
            def body(par, i, g):
                if loop == 0 and isinstance(g, int):
                    both(edges(eng, par, i, g))
                else:
                    both(*(dense(eng, l, turn(loop, g)) for l in LANES), edges(eng, par, i, g), lags=(0, 0, EDGE_LAG[loop]))
            groups(eng, body)

        def mlp_pe(pe, h, l, n, c, w, w4, pl, bg):
            yield h + 1
            pe.wait_ge(S(f"mlp_h{l}"), n + 1)
            nc.tensor.matmul(bg[:, 0:w], wt[0:64, W1T, :], b_h[l][0:64, 0:w], start=True, stop=True)
            nc.tensor.matmul(bg[:, 512:512 + w], wt[64:128, W1T, :], b_h[l][64:128, 0:w], start=True,
                             stop=True).then_inc(S(f"mlp_m1{l}"), 1)
            nc.tensor.matmul(pl[0][:, 0:w], blk_c[:, :], b_h[l][:, 0:w], start=True, stop=False)
            yield h + 3
            pe.wait_ge(S(f"mlp_gelu{l}"), n + 1)
            nc.tensor.matmul(pl[0][:, 0:w], w2p[:, 0, :], b_gl[l][:, 0:w], start=False, stop=False)
            nc.tensor.matmul(pl[0][:, 0:w], w2p[:, 1, :], b_gl[l][:, 512:512 + w], start=False,
                             stop=True).then_inc(S(f"mlp_m2{l}"), 1)
            yield h + 5
            pe.wait_ge(S(f"squares{l}"), c + 1)
            nc.tensor.matmul(pl[2][:, 0:w], blk_j[:, :], b_s[l][:, 0:w], start=True,
                             stop=True).then_inc(S(f"means{l}"), 1)
            yield h + 8
            pe.wait_ge(S(f"mlp_t{l}"), n + 1)
            nc.tensor.matmul(pl[1][:, 0:w], wt[:, DG2, :], b_h[l][:, 0:w], start=True,
                             stop=True).then_inc(S(f"mlp_d{l}"), 1)
            yield h + 11
            pe.wait_ge(S(f"squares{l}"), c + 2)
            nc.tensor.matmul(pl[2][:, 0:w], blk_j[:, :], b_s[l][:, 0:w], start=True,
                             stop=True).then_inc(S(f"means{l}"), 1)
            yield h + 14
            pe.wait_ge(S(f"mlp_x2{l}"), n + 1)
            for q in range(4):
                last_t = nc.tensor.transpose(pl[0][0:w4, 128 * q:128 * q + 128], b_h[l][:, w4 * q:w4 * q + w4], ident[:, :])
            last_t.then_inc(S(f"mlp_t9{l}"), 1)

        def mlp_act(act, h, l, n, c, w, pl, bg, stored=None):
            yield h + 2
            act.wait_ge(S(f"mlp_m1{l}"), n + 1)
            if stored is not None:
                act.wait_ge(S(f"blk_st{l}"), HEAD + stored)
            nc.scalar.activation(b_gl[l][:, :].rearrange("p (b f) -> p b f", b=2)[:, :, 0:w],
                                 bg.rearrange("p (b f) -> p b f", b=2)[:, :, 0:w], ACT.Gelu,
                                 bias=col(HB1)).then_inc(S(f"mlp_gelu{l}"), 1)
            yield h + 4
            act.wait_ge(S(f"mlp_m2{l}"), n + 1)
            nc.scalar.activation(b_s[l][:, 0:w], pl[0][:, 0:w], ACT.Square, bias=col(CR)).then_inc(S(f"squares{l}"), 1)
            yield h + 6
            act.wait_ge(S(f"means{l}"), c + 1)
            nc.scalar.activation(b_s[l][:, 0:w], pl[2][:, 0:w], ACT.Abs_reciprocal_sqrt,
                                 bias=col(EPSV)).then_inc(S(f"rstds{l}"), 1)
            yield h + 10
            act.wait_ge(S(f"mlp_v{l}"), n + 1)
            nc.scalar.activation(b_s[l][:, 0:w], b_h[l][:, 0:w], ACT.Square).then_inc(S(f"squares{l}"), 1)
            yield h + 12
            act.wait_ge(S(f"means{l}"), c + 2)
            nc.scalar.activation(b_s[l][:, 0:w], pl[2][:, 0:w], ACT.Abs_reciprocal_sqrt,
                                 bias=col(EPSV)).then_inc(S(f"rstds{l}"), 1)

        def mlp_dve(dve, h, l, n, c, w, pl, x1):
            yield h + 7
            dve.wait_ge(S(f"rstds{l}"), c + 1)
            nc.vector.scalar_tensor_tensor(b_h[l][:, 0:w], pl[0][:, 0:w], col(CR), b_s[l][:, 0:w], ALU.add,
                                           ALU.mult).then_inc(S(f"mlp_t{l}"), 1)
            yield h + 9
            dve.wait_ge(S(f"mlp_d{l}"), n + 1)
            nc.vector.scalar_tensor_tensor(b_h[l][:, 0:w], pl[1][:, 0:w], col(CT), x1, ALU.add,
                                           ALU.add).then_inc(S(f"mlp_v{l}"), 1)
            yield h + 13
            dve.wait_ge(S(f"rstds{l}"), c + 2)
            nc.vector.tensor_tensor(b_h[l][:, 0:w], b_h[l][:, 0:w], b_s[l][:, 0:w], ALU.mult).then_inc(S(f"mlp_x2{l}"), 1)

        def dense_pe(pe, l, n):
            yield 0
            pe.wait_ge(S(f"blk_in{l}"), 16 * (n + 1))
            pe.wait_ge(S(f"blk_xo{l}"), HEAD + n)
            for q in range(4):
                last_t = nc.tensor.transpose(psD[l][0][:, 128 * q:128 * q + 128], xin[l][:, 128 * q:128 * q + 128], ident[:, :])
            last_t.then_inc(S(f"blk_t1{l}"), 1)
            yield 2
            pe.wait_ge(S(f"blk_u{l}"), n + 1)
            nc.tensor.matmul(psD[l][1][:, :], blk_c[:, :], b_h[l][:, :], start=True, stop=True).then_inc(S(f"blk_c1{l}"), 1)
            yield 4
            pe.wait_ge(S(f"squares{l}"), 4 * n + 1)
            nc.tensor.matmul(psD[l][2], blk_j[:, :], b_s[l][:, :], start=True, stop=True).then_inc(S(f"means{l}"), 1)
            yield 8
            pe.wait_ge(S(f"squares{l}"), 4 * n + 2)
            nc.tensor.matmul(psD[l][2], blk_j[:, :], b_s[l][:, :], start=True, stop=True).then_inc(S(f"means{l}"), 1)
            yield from mlp_pe(pe, 10, l, n, 4 * n + 2, 512, 128, psD[l], psD_BG[l])

        def dense_act(act, l, n):
            yield 3
            act.wait_ge(S(f"blk_c1{l}"), n + 1)
            nc.scalar.activation(b_s[l][:, :], psD[l][1][:, :], ACT.Square).then_inc(S(f"squares{l}"), 1)
            yield 5
            act.wait_ge(S(f"means{l}"), 4 * n + 1)
            nc.scalar.activation(b_s[l][:, :], psD[l][2], ACT.Abs_reciprocal_sqrt, bias=col(EPSV)).then_inc(S(f"rstds{l}"), 1)
            yield 7
            act.wait_ge(S(f"blk_x1{l}"), n + 1)
            nc.scalar.activation(b_s[l][:, :], b_x1[l][:, :], ACT.Square).then_inc(S(f"squares{l}"), 1)
            yield 9
            act.wait_ge(S(f"means{l}"), 4 * n + 2)
            nc.scalar.activation(b_s[l][:, :], psD[l][2], ACT.Abs_reciprocal_sqrt, bias=col(EPSV)).then_inc(S(f"rstds{l}"), 1)
            yield from mlp_act(act, 10, l, n, 4 * n + 2, 512, psD[l], psD_BG[l], 16 * n)

        def dense_dve(dve, l, n):
            yield 1
            dve.wait_ge(S(f"blk_t1{l}"), HEAD + n + 1)
            nc.vector.tensor_scalar(b_h[l][:, :], psD[l][0][:, :], col(B0), None, ALU.add).then_inc(S(f"blk_u{l}"), 1)
            yield 6
            dve.wait_ge(S(f"rstds{l}"), 4 * n + 1)
            nc.vector.tensor_tensor(b_x1[l][:, :], psD[l][1][:, :], b_s[l][:, :], ALU.mult).then_inc(S(f"blk_x1{l}"), 1)
            yield 10
            dve.wait_ge(S(f"rstds{l}"), 4 * n + 2)
            nc.vector.scalar_tensor_tensor(b_h[l][:, :], b_x1[l][:, :], col(G1), b_s[l][:, :], ALU.mult,
                                           ALU.mult).then_inc(S(f"mlp_h{l}"), 1)
            yield from mlp_dve(dve, 10, l, n, 4 * n + 2, 512, psD[l], b_x1[l][:, :])
            yield 25
            dve.wait_ge(S(f"mlp_t9{l}"), n + 1)
            dve.wait_ge(S(f"blk_st{l}"), HEAD + 16 * n)
            nc.vector.tensor_tensor(g_x[l].rearrange("p (t d) -> p t d", d=D), psD[l][0].rearrange("p (t d) -> p t d", d=D),
                                    b2_row[:, :].unsqueeze(1).broadcast_to((128, 8, D)), ALU.add).then_inc(S(f"blk_xo{l}"), 1)

        g_x = [b_gl[l][:, 512:1024] for l in LANES]

        def dense_load(sp, l, n, row):
            sp.wait_ge(S(f"blk_t1{l}"), HEAD + n)
            sp.dma_start(xin[l][:, :], x[bass.ds(row, NB), :].rearrange("(p t) d -> p (t d)", p=128)).then_inc(
                S(f"blk_in{l}"), 16)

        def dense_store(sp, l, n, row):
            sp.wait_ge(S(f"blk_xo{l}"), HEAD + n + 1)
            sp.dma_start(x2tab[bass.ds(row, NB), :].rearrange("(p t) d -> p (t d)", p=128), g_x[l]).then_inc(
                S(f"blk_st{l}"), 16)

        def end_phase(eng, k):
            eng.drain().then_inc(S("phase"), 1)
            eng.wait_ge(S("phase"), 3 * k)

        def scores0_pe(pe, par, i, g):
            yield 0
            pe.wait_ge(S(f"moved{par}"), moved(1, par, i + 1))
            pe.wait_ge(S(f"ea_in{par}"), 16 * (i + 1))
            pe.wait_ge(S("scores_out"), HEAD + g)
            for q in range(Q):
                nc.tensor.transpose(psE[0][:, P * q:P * q + P], g_s[par][0:P, 128 * q:128 * q + 128], ident[0:P, 0:P])
                last_t = nc.tensor.transpose(psE[1][:, P * q:P * q + P], g_d[par][0:P, 128 * q:128 * q + 128], ident[0:P, 0:P])
            last_t.then_inc(S("edge_t"), 1)
            yield 3
            pe.wait_ge(S("edge_a"), g + 1)
            nc.tensor.transpose(psE[0][:, 0:P], ea_s[par][0:P, :], ident[0:P, 0:P]).then_inc(S("s0_ea_ps"), 1)
            yield 6
            pe.wait_ge(S("s0_xd"), g + 1)
            pe.wait_ge(S("s0_ea"), g + 1)
            nc.tensor.matmul(psE[1][:, 0:EW], wt[:, W1X, :], e_a[:, 0:EW], start=True, stop=False)
            for q in range(Q):
                last_f = nc.tensor.matmul(psE[1][:, P * q:P * q + P], w_e[:, q, :], e_b[:, 0:P], start=False, stop=(q == Q - 1))
            last_f.then_inc(S("s0_f_ps"), 1)
            yield 12
            pe.wait_ge(S("s0_ed"), g + 1)
            pe.wait_ge(S("edge_x"), g + 1)
            for q in range(Q):
                o = psE[0][0:P, 2 * q:2 * q + 2]
                nc.tensor.matmul(o, e_b[:, P * q:P * q + P], att[:, 0, :], start=True, stop=False)
                last_s = nc.tensor.matmul(o, e_c[:, P * q:P * q + P], att[:, 1, :], start=False, stop=True)
            last_s.then_inc(S("scores_ps"), 1)

        def scores0_act(act, par, i, g):
            yield 2
            act.wait_ge(S("edge_t"), g + 1)
            nc.scalar.activation(e_a[:, 0:EW], psE[0][:, 0:EW], ACT.Identity).then_inc(S("edge_a"), 1)
            yield 5
            act.wait_ge(S("s0_ea_ps"), g + 1)
            nc.scalar.activation(e_b[:, 0:P], psE[0][:, 0:P], ACT.Identity).then_inc(S("s0_ea"), 1)
            yield 8
            act.wait_ge(S("s0_f_ps"), g + 1)
            nc.scalar.activation(e_a[:, 0:EW], psE[1][:, 0:EW], ACT.Identity).then_inc(S("s0_fs"), 1)

        def scores0_dve(dve, par, i, g):
            yield 2
            dve.wait_ge(S("edge_t"), g + 1)
            nc.vector.tensor_copy(xg(g), psE[1][:, 0:EW]).then_inc(S("s0_xd"), 1)
            nc.vector.tensor_copy(xsg(g), g_s[par][0:P, :]).then_inc(S(f"rows0_used{par}"), 1)
            nc.vector.tensor_copy(ix_a[par][:, :], grp(src_i, g + 2))
            nc.vector.tensor_copy(ix_b[par][:, :], grp(dst_i, g + 2)).then_inc(S(f"idx{par}"), 1)
            yield 5
            dve.wait_ge(S("s0_xd"), g + 1)
            nc.vector.scalar_tensor_tensor(e_c[:, 0:EW], xg(g), 0.01, xg(g), ALU.mult, ALU.max).then_inc(S("s0_ed"), 1)
            yield 10
            dve.wait_ge(S("s0_fs"), g + 1)
            nc.vector.scalar_tensor_tensor(e_b[:, 0:EW], e_a[:, 0:EW], 0.01, e_a[:, 0:EW], ALU.mult,
                                           ALU.max).then_inc(S("edge_x"), 1)
            yield 14
            dve.wait_ge(S("scores_ps"), g + 1)
            nc.vector.tensor_copy(grp(score, g), psE[0][0:P, 0:GC]).then_inc(S("scores_out"), 1)

        def carries_pe(pe, k, n):
            pe.wait_ge(S("seg_ends"), k)
            nc.tensor.transpose(psA[0][0:n, 0:P], edge_col[:, 0:n], ident[0:P, 0:P]).then_inc(S("seg_rows_ps"), 1)
            pe.wait_ge(S("seg_rows"), k)
            src_rows = rows[0:n, 0:P] if k % 2 == 1 else rows[0:n, 1:P + 1]
            nc.tensor.transpose(psB[0][0:P, 0:n], src_rows, ident[0:n, 0:n]).then_inc(S("seg_carry_ps"), 1)

        def carries_dve(dve, k, n, flags, start, op0, op1):
            dve.wait_ge(S("seg_rows_ps"), k)
            if k % 2 == 1:
                nc.vector.memset(rows[0:n, 0:1], start)
                o, a, b = rows[0:n, 1:P + 1], row_flags[0:n, flags, :], psA[0][0:n, 0:P]
            else:
                nc.vector.memset(rows[0:n, P:P + 1], start)
                o, a, b = rows[0:n, 0:P][:, ::-1], row_flags[0:n, flags, ::-1], psA[0][0:n, 0:P][:, ::-1]
            nc.vector.tensor_tensor_scan(o, a, b, start, op0, op1).then_inc(S("seg_rows"), 1)
            dve.wait_ge(S("seg_carry_ps"), k)
            nc.vector.tensor_copy(carry[:, 0:n], psB[0][0:P, 0:n]).then_inc(S("seg_carry"), 1)
            dve.wait_ge(S("seg_carry"), k)

        def softmax_dve(dve, m, step):
            k = 6 * m

            def own(ins):
                step[0] += 1
                ins.then_inc(S("seg_step"), 1)
                dve.wait_ge(S("seg_step"), step[0])

            def scan(o, a, b, init, op0, op1, back):
                f = (lambda v: v[:, ::-1]) if back else (lambda v: v)
                own(nc.vector.tensor_tensor_scan(f(o), f(a), f(b), init, op0, op1))

            scan(sm1[:, :], pen_f[:, :], score[:, :], NEG, ALU.add, ALU.max, False)
            nc.vector.tensor_copy(edge_col[:, 0:1], sm1[:, TC - 1:TC]).then_inc(S("seg_ends"), 1)
            carries_dve(dve, k + 1, 1, 2, NEG, ALU.add, ALU.max)
            scan(sm2[:, :], pen_f[:, :], score[:, :], carry[:, 0:1], ALU.add, ALU.max, False)
            scan(sm1[:, :], pen_b[:, :], sm2[:, :], NEG, ALU.add, ALU.max, True)
            nc.vector.tensor_copy(edge_col[:, 0:1], sm1[:, 0:1]).then_inc(S("seg_ends"), 1)
            carries_dve(dve, k + 2, 1, 3, NEG, ALU.add, ALU.max)
            scan(sm1[:, :], pen_b[:, :], sm2[:, :], carry[:, 0:1], ALU.add, ALU.max, True)
            nc.vector.tensor_tensor(sm2[:, :], score[:, :], sm1[:, :], ALU.subtract).then_inc(S("seg_x"), 1)
            dve.wait_ge(S("seg_exp"), m + 1)
            scan(sm1[:, :], same[:, :], score[:, :], 0.0, ALU.mult, ALU.add, False)
            nc.vector.tensor_copy(edge_col[:, 0:1], sm1[:, TC - 1:TC]).then_inc(S("seg_ends"), 1)
            carries_dve(dve, k + 3, 1, 0, 0.0, ALU.mult, ALU.add)
            scan(sm1[:, :], same[:, :], score[:, :], carry[:, 0:1], ALU.mult, ALU.add, False)
            own(nc.vector.tensor_tensor(sm2[:, :], sm1[:, :], last[:, :], ALU.mult))
            scan(sm1[:, :], nxt[:, :], sm2[:, :], 0.0, ALU.mult, ALU.add, True)
            nc.vector.tensor_copy(edge_col[:, 0:1], sm1[:, 0:1]).then_inc(S("seg_ends"), 1)
            carries_dve(dve, k + 4, 1, 1, 0.0, ALU.mult, ALU.add)
            scan(sm1[:, :], nxt[:, :], sm2[:, :], carry[:, 0:1], ALU.mult, ALU.add, True)
            own(nc.vector.reciprocal(sm2[:, :], sm1[:, :]))
            own(nc.vector.tensor_tensor(sm1[:, :], score[:, :], sm2[:, :], ALU.mult))

        def softmax_act(act, m):
            act.wait_ge(S("seg_x"), m + 1)
            nc.scalar.activation(score[:, :], sm2[:, :], ACT.Exp).then_inc(S("seg_exp"), 1)

        def sums_dve(dve, m, step):
            k = 6 * m

            def own(ins):
                step[0] += 1
                ins.then_inc(S("seg_step"), 1)
                dve.wait_ge(S("seg_step"), step[0])

            own(nc.vector.tensor_tensor(ag[0:P, :, :], xsn[0:P, :, :].rearrange("p t d -> p d t"),
                                        sm1[:, :].unsqueeze(1).broadcast_to((P, D, TC)), ALU.mult))
            def scan_all(flags, back):
                def scan(a, f):
                    nc.vector.tensor_tensor_scan(a, f, a, 0.0, ALU.mult, ALU.add)
                if back:
                    for d in range(D):
                        scan(ag[0:P, d, ::-1], flags[:, ::-1])
                else:
                    U = 8
                    with dve.Fori(0, D // U) as i:
                        for u in range(U):
                            scan(ag[0:P, bass.ds(i * U + u, 1), :].rearrange("p o t -> p (o t)"), flags[:, :])
                own(dve.drain())

            def add_carry(run):
                U = 8
                with dve.Fori(0, D // U) as i:
                    for u in range(U):
                        a = ag[0:P, bass.ds(i * U + u, 1), :].rearrange("p o t -> p (o t)")
                        nc.vector.scalar_tensor_tensor(a, run[:, :], carry[:, bass.ds(i * U + u, 1)], a, ALU.mult, ALU.add)
                own(dve.drain())

            run_f, run_b = score, sm2
            nc.vector.tensor_tensor_scan(run_f[:, :], same[:, :], zero[0:P, 0:TC], 1.0, ALU.mult, ALU.add)
            own(nc.vector.tensor_tensor_scan(run_b[:, ::-1], nxt[:, ::-1], zero[0:P, 0:TC], 1.0, ALU.mult, ALU.add))
            scan_all(same, False)
            nc.vector.tensor_copy(edge_col[:, :], ag[0:P, :, TC - 1]).then_inc(S("seg_ends"), 1)
            carries_dve(dve, k + 5, D, 0, 0.0, ALU.mult, ALU.add)
            add_carry(run_f)
            own(nc.vector.tensor_tensor(ag[0:P, :, :], ag[0:P, :, :], last[:, :].unsqueeze(1).broadcast_to((P, D, TC)), ALU.mult))
            scan_all(nxt, True)
            nc.vector.tensor_copy(edge_col[:, :], ag[0:P, :, 0]).then_inc(S("seg_ends"), 1)
            carries_dve(dve, k + 6, D, 1, 0.0, ALU.mult, ALU.add)
            add_carry(run_b)

        def x1_pe(pe, at, s, a_ready, n, c, xsrc, w, agg, sq, c_ps, j_ps, j_free=None):
            yield at[0]
            pe.wait_ge(*a_ready)
            nc.tensor.matmul(c_ps[:, 0:EW], blk_c[:, :], xsrc, start=True, stop=False)
            nc.tensor.matmul(c_ps[:, 0:EW], w, agg, start=False, stop=True).then_inc(S(f"ln_c{s}"), 1)
            yield at[2]
            pe.wait_ge(S(f"squares{s}"), c + 1)
            if j_free is not None:
                pe.wait_ge(*j_free)
            nc.tensor.matmul(j_ps[:, 0:EW], blk_j[:, :], sq, start=True, stop=True).then_inc(S(f"means{s}"), 1)

        def x1_act(act, at, s, n, c, bias, sq, c_ps, j_ps):
            yield at[1]
            act.wait_ge(S(f"ln_c{s}"), n + 1)
            nc.scalar.activation(sq, c_ps[:, 0:EW], ACT.Square, bias=bias).then_inc(S(f"squares{s}"), 1)
            yield at[3]
            act.wait_ge(S(f"means{s}"), c + 1)
            nc.scalar.activation(sq, j_ps[:, 0:EW], ACT.Abs_reciprocal_sqrt, bias=col(EPSV)).then_inc(S(f"rstds{s}"), 1)

        AT2 = (6, 8, 10, 12)
        ATL = (3, 4, 5, 6)

        def dst1_pe(pe, par, i, g):
            yield 2
            pe.wait_ge(S("ln_rows_e"), g + 1)
            pe.wait_ge(S("scores_out"), HEAD + NGR + g)
            for q in range(Q):
                last_t = nc.tensor.transpose(psE[0][:, P * q:P * q + P], g_s[par][0:P, 128 * q:128 * q + 128], ident[0:P, 0:P])
            last_t.then_inc(S("edge_t"), 1)
            yield from x1_pe(pe, AT2, "_e", (S("edge_a"), NGR + g + 1), g, g, xg(g), wt[:, A2C, :], e_a[:, 0:EW], e_b[:, 0:EW], psE[1], psE[0])
            yield 16
            pe.wait_ge(S("edge_x"), NGR + g + 1)
            for q in range(Q):
                last_s = nc.tensor.matmul(psE[0][0:P, 2 * q:2 * q + 2], e_c[:, P * q:P * q + P], att[:, 3, :],
                                          start=True, stop=True)
            last_s.then_inc(S("scores_ps"), 1)

        def dst1_act(act, par, i, g):
            yield 4
            act.wait_ge(S("edge_t"), NGR + g + 1)
            nc.scalar.activation(e_a[:, 0:EW], psE[0][:, 0:EW], ACT.Identity).then_inc(S("edge_a"), 1)
            yield from x1_act(act, AT2, "_e", g, g, col(CB0), e_b[:, 0:EW], psE[1], psE[0])
            yield 16
            act.wait_ge(S("edge_x"), NGR + g + 1)
            nc.scalar.activation(xg(g), e_c[:, 0:EW], ACT.Identity).then_inc(S("d1_kept"), 1)

        def dst1_dve(dve, par, i, g):
            yield 0
            dve.wait_ge(S(f"moved{par}"), moved(2, par, i))
            dve.wait_ge(S("edge_t"), NGR + g)
            nc.vector.tensor_copy(t3(g_s[par][0:P, :]), ag[0:P, :, bass.ds(g * GC, GC)].rearrange("p d t -> p t d")).then_inc(
                S("ln_rows_e"), 1)
            nc.vector.tensor_copy(ix_a[par][:, :], grp(last_i, g)).then_inc(S("d1_idx"), 1)
            yield 14
            dve.wait_ge(S("rstds_e"), g + 1)
            dve.wait_ge(S("d1_kept"), HEAD + g)
            nc.vector.scalar_tensor_tensor(e_c[:, 0:EW], psE[1][:, 0:EW], col(CB0), e_b[:, 0:EW], ALU.add,
                                           ALU.mult).then_inc(S("edge_x"), 1)
            yield 18
            dve.wait_ge(S("scores_ps"), NGR + g + 1)
            nc.vector.tensor_copy(grp(score, g), psE[0][0:P, 0:GC]).then_inc(S("scores_out"), 1)

        NDENSE = 2 * NGR - 1

        def lane_count(l, loop, i):
            return 4 * NDENSE + {3: i, 4: of_parity(l) + 3 * i, 5: 4 * of_parity(l) + i}[loop]

        def src1_pe(pe, l, i, g):
            A, B, G, H = psL[l]
            yield 1
            pe.wait_ge(S(f"moved{l}"), moved(3, l, i + 1))
            pe.wait_ge(S(f"ln_rows{l}"), i + 1)
            pe.wait_ge(S(f"s1_msg{l}"), HEAD + i)
            for q in range(Q):
                nc.tensor.transpose(A[:, P * q:P * q + P], xin[l][0:P, 128 * q:128 * q + 128], ident[0:P, 0:P])
                last_t = nc.tensor.transpose(B[:, P * q:P * q + P], g_s[l][0:P, 128 * q:128 * q + 128], ident[0:P, 0:P])
            last_t.then_inc(S(f"ln_t{l}"), 1)
            yield from x1_pe(pe, ATL, l, (S(f"ln_at{l}"), i + 1), i, lane_count(l, 3, i), b_x1[l][:, 0:EW], wt[:, A2C, :], b_gl[l][:, 0:EW], b_s[l][:, 0:EW], B, G)
            yield 8
            pe.wait_ge(S(f"ln_x{l}"), i + 1)
            for q in range(Q):
                lhs = b_h[l][:, P * q:P * q + P]
                nc.tensor.matmul(H[0:P, 2 * q:2 * q + 2], lhs, att[:, 2, :], start=True, stop=True)
                nc.tensor.matmul(A[0:P, 128 * q:128 * q + 128], lhs, wt[:, PHY, :], start=True, stop=True)
                last_m = nc.tensor.matmul(G[0:P, 128 * q:128 * q + 128], lhs, wt[:, NEU, :], start=True, stop=True)
            last_m.then_inc(S(f"rows_ps{l}"), 1)

        def src1_act(act, l, i, g):
            A, B, G, H = psL[l]
            yield 2
            act.wait_ge(S(f"ln_t{l}"), HEAD + i + 1)
            nc.scalar.activation(b_x1[l][:, 0:EW], A[:, 0:EW], ACT.Identity)
            nc.scalar.activation(b_gl[l][:, 0:EW], B[:, 0:EW], ACT.Identity).then_inc(S(f"ln_at{l}"), 1)
            yield from x1_act(act, ATL, l, i, lane_count(l, 3, i), col(CB0), b_s[l][:, 0:EW], B, G)

        def src1_dve(dve, l, i, g):
            A, B, G, H = psL[l]
            yield 0
            dve.wait_ge(S(f"ln_t{l}"), HEAD + i)
            nc.vector.tensor_copy(xin[l][0:P, :], xsg(g)).then_inc(S(f"ln_rows{l}"), 1)
            yield 2
            dve.wait_ge(S(f"ln_t{l}"), HEAD + i + 1)
            nc.vector.tensor_copy(ix_b[l][:, :], grp(src_i, g + 2)).then_inc(S(f"idx{l}"), 1)
            yield 7
            dve.wait_ge(S(f"rstds{l}"), lane_count(l, 3, i) + 1)
            nc.vector.scalar_tensor_tensor(b_h[l][:, 0:EW], B[:, 0:EW], col(CB0), b_s[l][:, 0:EW], ALU.add,
                                           ALU.mult).then_inc(S(f"ln_x{l}"), 1)
            yield 9
            dve.wait_ge(S(f"rows_ps{l}"), i + 1)
            nc.vector.tensor_tensor(grp(score, g), H[0:P, 0:GC], grp(score, g), ALU.add)
            nc.vector.tensor_tensor(t3(b_gl[l][0:P, 512:1024]), t3(A[0:P, :]), bc(grp(ew, g), D), ALU.mult).then_inc(
                S(f"part{l}"), 1)
            dve.wait_ge(S(f"part{l}"), i + 1)
            nc.vector.tensor_tensor(xsg(g), G[0:P, :], b_gl[l][0:P, 512:1024], ALU.add).then_inc(S(f"s1_msg{l}"), 1)

        def unique_pe(pe, l, n):
            pe.wait_ge(S(f"msg_sf{l}"), n + 1)
            for k in range(GC):
                o = psL_GH[l][0:P, 512 * (k // 4) + P * (k % 4):512 * (k // 4) + P * (k % 4) + P]
                last_b = nc.tensor.matmul(o, sf[l][:, k:k + 1].broadcast_to((P, P)), ident[0:P, 0:P], start=True, stop=True)
            last_b.then_inc(S(f"msg_src_ps{l}"), 1)

        def summed_pe(pe, l, n, o):
            pe.wait_ge(S(f"msg_same{l}"), n + 1)
            pe.wait_ge(S(f"msg_zs{l}"), n + 1)
            for k in range(GC):
                last_z = nc.tensor.matmul(o[0:P, D * k:D * k + D], same_src[l][0:P, P * k:P * k + P],
                                          zs[l][0:P, D * k:D * k + D], start=True, stop=True)
            last_z.then_inc(S(f"msg_z_ps{l}"), 1)

        def same_dve(dve, l, n):
            dve.wait_ge(S(f"msg_src_ps{l}"), n + 1)
            for b in range(2):
                last_m = nc.vector.tensor_tensor(t3(same_src[l][0:P, 4 * P * b:4 * P * b + 4 * P], 4),
                                                 t3(psL_GH[l][0:P, 512 * b:512 * b + 4 * P], 4),
                                                 bc(sf[l][:, 4 * b:4 * b + 4], P), ALU.is_equal)
            last_m.then_inc(S(f"msg_same{l}"), 1)

        def dst2_pe(pe, l, i, g):
            A, B, G, H = psL[l]
            n, c = of_parity(l) + i, lane_count(l, 4, i)
            yield 0
            unique_pe(pe, l, i)
            yield 1
            pe.wait_ge(S(f"ln_rows{l}"), n + 1)
            for q in range(Q):
                last_t = nc.tensor.transpose(A[:, P * q:P * q + P], g_s[l][0:P, 128 * q:128 * q + 128], ident[0:P, 0:P])
            last_t.then_inc(S(f"ln_t{l}"), 1)
            yield from x1_pe(pe, ATL, l, (S(f"ln_at{l}"), n + 1), n, c, xg(g), blk_c[:, :], b_gl[l][:, 0:EW], b_s[l][:, 0:EW], B, G,
                             (S(f"msg_same{l}"), i + 1))
            yield from mlp_pe(pe, 7, l, NDENSE + i, c + 1, EW, P, psL[l], psL_BG[l])
            yield 21
            for q in range(Q):
                last_z = nc.tensor.matmul(B[0:P, 128 * q:128 * q + 128], b_h[l][:, P * q:P * q + P], wt[:, L2W, :],
                                          start=True, stop=True)
            last_z.then_inc(S(f"rows_ps{l}"), 1)
            yield 24
            pe.wait_ge(S(f"e2_xrow{l}"), i + 1)
            summed_pe(pe, l, i, A)

        def dst2_act(act, l, i, g):
            A, B, G, H = psL[l]
            n, c = of_parity(l) + i, lane_count(l, 4, i)
            yield 2
            act.wait_ge(S(f"ln_t{l}"), HEAD + n + 1)
            nc.scalar.activation(b_gl[l][:, 0:EW], A[:, 0:EW], ACT.Gelu).then_inc(S(f"ln_at{l}"), 1)
            yield 4
            act.wait_ge(S(f"ln_c{l}"), n + 1)
            nc.scalar.activation(b_s[l][:, 0:EW], B[:, 0:EW], ACT.Square).then_inc(S(f"squares{l}"), 1)
            yield 6
            act.wait_ge(S(f"means{l}"), c + 1)
            nc.scalar.activation(b_s[l][:, 0:EW], G[:, 0:EW], ACT.Abs_reciprocal_sqrt,
                                 bias=col(EPSV)).then_inc(S(f"rstds{l}"), 1)
            yield from mlp_act(act, 7, l, NDENSE + i, c + 1, EW, psL[l], psL_BG[l])
            yield 21
            act.wait_ge(S(f"mlp_x2{l}"), NDENSE + i + 1)
            nc.scalar.activation(xg(g), b_h[l][:, 0:EW], ACT.Identity).then_inc(S(f"e2_kept{l}"), 1)

        def dst2_dve(dve, l, i, g):
            A, B, G, H = psL[l]
            n, c = of_parity(l) + i, lane_count(l, 4, i)
            yield 0
            dve.wait_ge(S(f"e2_idx{l}"), HEAD + 4 * i)
            nc.vector.tensor_copy(sf[l][:, :], grp(src_i, g)).then_inc(S(f"msg_sf{l}"), 1)
            dve.wait_ge(S(f"ln_t{l}"), HEAD + n)
            nc.vector.tensor_copy(t3(g_s[l][0:P, :]), ag[0:P, :, bass.ds(g * GC, GC)].rearrange("p d t -> p t d")).then_inc(
                S(f"ln_rows{l}"), 1)
            yield 2
            same_dve(dve, l, i)
            yield 4
            dve.wait_ge(S(f"msg_same{l}"), i + 1)
            nc.vector.tensor_tensor(t3(dup[l][0:P, :]), t3(same_src[l][0:P, :]),
                                    low[0:P, 0:P].unsqueeze(1).broadcast_to((P, GC, P)), ALU.mult).then_inc(S(f"e2_idx{l}"), 1)
            yield 6
            dve.wait_ge(S(f"e2_idx{l}"), HEAD + 4 * i + 1)
            nc.vector.tensor_reduce(cnt[l][:, :], t3(dup[l][0:P, :]), AX.X, ALU.add).then_inc(S(f"e2_idx{l}"), 1)
            yield 7
            dve.wait_ge(S(f"rstds{l}"), c + 1)
            dve.wait_ge(S(f"e2_kept{l}"), HEAD + i)
            nc.vector.scalar_tensor_tensor(b_h[l][:, 0:EW], B[:, 0:EW], col(G1), b_s[l][:, 0:EW], ALU.mult,
                                           ALU.mult).then_inc(S(f"mlp_h{l}"), 1)
            yield from mlp_dve(dve, 7, l, NDENSE + i, c + 1, EW, psL[l], xg(g))
            yield 22
            dve.wait_ge(S(f"mlp_t9{l}"), NDENSE + i + 1)
            dve.wait_ge(S(f"moved{l}"), moved(4, l, i))
            nc.vector.tensor_copy(ix_a[l][:, :], grp(last_i, g))
            nc.vector.tensor_tensor(t3(xrow[l][0:P, :]), t3(A[0:P, :]), b2_row[0:P, :].unsqueeze(1).broadcast_to((P, GC, D)),
                                    ALU.add).then_inc(S(f"e2_xrow{l}"), 1)
            dve.wait_ge(S(f"rows_ps{l}"), n + 1)
            nc.vector.tensor_tensor(t3(zs[l][0:P, :]), t3(B[0:P, :]), bc(grp(dis, g), D), ALU.mult).then_inc(S(f"msg_zs{l}"), 1)
            yield 23
            dve.wait_ge(S(f"e2_idx{l}"), HEAD + 4 * i + 2)
            nc.vector.tensor_scalar(cnt[l][:, :], cnt[l][:, :], 1.0, float(SKIP), ALU.min, ALU.mult)
            nc.vector.scalar_tensor_tensor(sf[l][:, :], sf[l][:, :], float(K), chain_of[:, :], ALU.mult, ALU.add).then_inc(
                S(f"e2_idx{l}"), 1)
            dve.wait_ge(S(f"e2_idx{l}"), HEAD + 4 * i + 3)
            for c in range(K):
                dve.wait_ge(S(f"added{c}{l}"), added(4, l, i))
            nc.vector.tensor_tensor(grp(acc_i, g), cnt[l][:, :], sf[l][:, :], ALU.add)
            nc.vector.tensor_tensor(ix_b[l][:, :], cnt[l][:, :], sf[l][:, :], ALU.add).then_inc(S(f"e2_idx{l}"), 1)
            yield 25
            dve.wait_ge(S(f"msg_z_ps{l}"), i + 1)
            nc.vector.tensor_copy(zrow[l][0:P, :], A[0:P, :]).then_inc(S(f"msg_zrow{l}"), 1)

        def dst3_pe(pe, l, i, g):
            A, B, G, H = psL[l]
            n, c = 2 * of_parity(l) + i, lane_count(l, 5, i)
            yield 0
            unique_pe(pe, l, of_parity(l) + i)
            yield 1
            pe.wait_ge(S(f"ln_rows{l}"), n + 1)
            for q in range(Q):
                last_t = nc.tensor.transpose(A[:, P * q:P * q + P], xin[l][0:P, 128 * q:128 * q + 128], ident[0:P, 0:P])
            last_t.then_inc(S(f"ln_t{l}"), 1)
            yield from x1_pe(pe, ATL, l, (S(f"ln_at{l}"), n + 1), n, c, xg(g), blk_c[:, :], b_x1[l][:, 0:EW], b_s[l][:, 0:EW], B, G,
                             (S(f"msg_same{l}"), of_parity(l) + i + 1))
            yield 8
            pe.wait_ge(S(f"ln_x{l}"), of_parity(l) + i + 1)
            for q in range(Q):
                last_t = nc.tensor.transpose(A[0:P, 128 * q:128 * q + 128], b_h[l][:, P * q:P * q + P], ident[:, :])
            last_t.then_inc(S(f"rows_ps{l}"), 1)
            yield 10
            summed_pe(pe, l, of_parity(l) + i, B)

        def dst3_act(act, l, i, g):
            A, B, G, H = psL[l]
            n, c = 2 * of_parity(l) + i, lane_count(l, 5, i)
            yield 2
            act.wait_ge(S(f"ln_t{l}"), HEAD + n + 1)
            nc.scalar.activation(b_x1[l][:, 0:EW], A[:, 0:EW], ACT.Identity).then_inc(S(f"ln_at{l}"), 1)
            yield from x1_act(act, ATL, l, n, c, col(C2), b_s[l][:, 0:EW], B, G)

        def dst3_dve(dve, l, i, g):
            A, B, G, H = psL[l]
            n, m, c = 2 * of_parity(l) + i, of_parity(l) + i, lane_count(l, 5, i)
            yield 0
            nc.vector.tensor_copy(sf[l][:, :], grp(src_i, g)).then_inc(S(f"msg_sf{l}"), 1)
            dve.wait_ge(S(f"moved{l}"), moved(5, l, i + 1))
            a = g_a[l][0:P, :].rearrange("p (c k d) -> p c k d", c=GC, k=K)
            nc.vector.tensor_tensor(t3(b_gl[l][0:P, 0:512]), a[:, :, 0, :], a[:, :, 1, :], ALU.add).then_inc(S(f"part{l}"), 1)
            nc.vector.tensor_copy(ix_a[l][:, :], grp(dst_i, g + 2)).then_inc(S(f"idx{l}"), 1)
            dve.wait_ge(S(f"part{l}"), of_parity(l) + i + 1)
            nc.vector.tensor_tensor(t3(xin[l][0:P, :]), t3(b_gl[l][0:P, 0:512]), bc(grp(dis, g), D), ALU.mult).then_inc(
                S(f"ln_rows{l}"), 1)
            yield 2
            same_dve(dve, l, m)
            yield 7
            dve.wait_ge(S(f"rstds{l}"), c + 1)
            nc.vector.scalar_tensor_tensor(b_h[l][:, 0:EW], B[:, 0:EW], col(C2), b_s[l][:, 0:EW], ALU.add,
                                           ALU.mult).then_inc(S(f"ln_x{l}"), 1)
            yield 9
            dve.wait_ge(S(f"rows_ps{l}"), n + 1)
            nc.vector.tensor_tensor(t3(zs[l][0:P, :]), t3(A[0:P, :]), bc(grp(ew, g), D), ALU.mult).then_inc(S(f"msg_zs{l}"), 1)
            yield 11
            dve.wait_ge(S(f"msg_z_ps{l}"), m + 1)
            for c in range(K):
                dve.wait_ge(S(f"added{c}{l}"), added(5, l, i))
            nc.vector.tensor_copy(ix_b[l][:, :], grp(acc_i, g))
            nc.vector.tensor_copy(zrow[l][0:P, :], B[0:P, :]).then_inc(S(f"msg_zrow{l}"), 1)

        at_[0] = 0
        f_x2 = [[in_ag(R * D) for _ in range(2)] for _ in LANES]
        f_a2 = [[in_ag(R * K * D) for _ in range(2)] for _ in LANES]
        f_dis = [[in_ag(R) for _ in range(2)] for _ in LANES]
        f_u = [[in_xsn(R * D), in_xsn(R * D)], [in_xsn(R * D), xsf[:, 0:R * D]]]
        l_st = [in_ag(R * 6) for _ in LANES]
        l_m, l_d, l_v, l_rs, l_nb = ([in_ag(R) for _ in LANES] for _ in range(5))
        assert NTILE == 2 * NGR

        def t3r(a):
            return a.rearrange("p (r d) -> p r d", r=R)

        def by_rows(table, row):
            return table[bass.ds(row, NT), :].rearrange("(p r) d -> p (r d)", p=P)

        def variance_dve(dve, l, n, u):
            def own(k, ins):
                ins.then_inc(S(f"l_step{l}"), 1)
                dve.wait_ge(S(f"l_step{l}"), n + k)

            for r in range(R):
                st = nc.vector.bn_stats(l_st[l][0:P, 6 * r:6 * r + 6], u[0:P, D * r:D * r + D])
            own(1, st)
            s = l_st[l][0:P, :].rearrange("p (r c) -> p r c", c=6)
            me, ve, mo, vo = s[:, :, 1], s[:, :, 2], s[:, :, 4], s[:, :, 5]
            nc.vector.tensor_tensor(l_m[l][0:P, :], me, mo, ALU.add)
            nc.vector.tensor_tensor(l_v[l][0:P, :], ve, vo, ALU.add)
            own(2, nc.vector.tensor_tensor(l_d[l][0:P, :], me, mo, ALU.subtract))
            own(3, nc.vector.scalar_tensor_tensor(l_d[l][0:P, :], l_d[l][0:P, :], 0.25, l_d[l][0:P, :], ALU.mult, ALU.mult))
            nc.vector.scalar_tensor_tensor(l_v[l][0:P, :], l_v[l][0:P, :], 1.0 / D, l_d[l][0:P, :], ALU.mult,
                                           ALU.add).then_inc(S(f"l_stats{l}"), 1)

        def shift_dve(dve, l):
            nc.vector.scalar_tensor_tensor(l_nb[l][0:P, :], l_m[l][0:P, :], -0.5, l_rs[l][0:P, :], ALU.mult,
                                           ALU.mult).then_inc(S(f"l_stats{l}"), 1)

        def rstd_act(l):
            nc.scalar.activation(l_rs[l][0:P, :], l_v[l][0:P, :], ACT.Abs_reciprocal_sqrt, bias=vec[0:P, EPSV:EPSV + 1]).then_inc(
                S(f"l_act{l}"), 1)

        def normalise_act(l, rows_, u, o):
            for r in rows_:
                last_n = nc.scalar.activation(o[0:P, D * r:D * r + D], u[0:P, D * r:D * r + D], ACT.Identity,
                                              bias=l_nb[l][0:P, r:r + 1], scale=l_rs[l][0:P, r:r + 1])
            last_n.then_inc(S(f"l_act{l}"), 1)

        AT_SUM, AT_VARIANCE, AT_RSTD, AT_SHIFT, AT_NORMALISE = (2.2, 9.2), (3.5, 11.4), (4.5, 12), (6.5, 13), (8.5, 14)

        def all_load(sp, l, t, g):
            row, s = (2 * g + t) * NT, S(f"l_in{'ab'[t]}{l}")
            sp.dma_start(f_x2[l][t][0:P, :], by_rows(x2tab, row)).then_inc(s, 16)
            sp.dma_start(f_a2[l][t][0:P, :], by_rows(acc2, row)).then_inc(s, 16)
            sp.dma_start(f_dis[l][t][0:P, :], distab[bass.ds(row, NT)].rearrange("(p r) -> p r", p=P)).then_inc(s, 16)

        def all_act(act, l, i, g):
            for t in range(2):
                n = 2 * i + t
                yield AT_RSTD[t]
                act.wait_ge(S(f"l_stats{l}"), 2 * n + 1)
                act.wait_ge(S(f"l_act{l}"), HEAD + 2 * n)
                rstd_act(l)
                yield AT_NORMALISE[t]
                act.wait_ge(S(f"l_stats{l}"), 2 * n + 2)
                normalise_act(l, range(R), f_u[l][t], f_u[l][t])
                act.wait_ge(S(f"l_act{l}"), HEAD + 2 * n + 2)
                act.dma_start(by_rows(x2tab, (2 * g + t) * NT), f_u[l][t][0:P, :]).then_inc(
                    S(f"l_out{'ab'[t]}{l}"), 16)

        def all_dve(dve, l, i, g):
            for t in range(2):
                n = 2 * i + t

                def own(k, ins):
                    ins.then_inc(S(f"l_step{l}"), 1)
                    dve.wait_ge(S(f"l_step{l}"), 5 * n + k)

                yield AT_SUM[t]
                dve.wait_ge(S(f"l_in{'ab'[t]}{l}"), 48 * (i + 1))
                dve.wait_ge(S(f"l_out{'ab'[t]}{l}"), HEAD + 16 * i)
                a = f_a2[l][t][0:P, :].rearrange("p (r k d) -> p r k d", r=R, k=K)
                u = f_u[l][t][0:P, :]
                own(1, nc.vector.tensor_tensor(t3r(u), a[:, :, 0, :], a[:, :, 1, :], ALU.add))
                own(2, nc.vector.tensor_tensor(t3r(u), t3r(u), bc(f_dis[l][t][0:P, :], D), ALU.mult))
                nc.vector.tensor_tensor(u, u, f_x2[l][t][0:P, :], ALU.add).then_inc(S(f"l_read{l}"), 1)
                yield AT_VARIANCE[t]
                dve.wait_ge(S(f"l_read{l}"), n + 1)
                dve.wait_ge(S(f"l_act{l}"), HEAD + 2 * n)
                variance_dve(dve, l, 5 * n + 2, f_u[l][t])
                yield AT_SHIFT[t]
                dve.wait_ge(S(f"l_act{l}"), HEAD + 2 * n + 1)
                shift_dve(dve, l)

        xt_[0] = 0
        l_x3, l_out = ([in_xsn(R * D) for _ in LANES] for _ in range(2))
        l_a3 = [in_xsn(R * K * D) for _ in LANES]
        l_u = [in_xsn(R * D) for _ in LANES]

        def tiles_before(l):
            return 2 * of_parity(l)

        def tiles(eng, steps):
            with eng.Fori(0, NTILE // 2) as i:
                both(steps(eng, 0, i), steps(eng, 1, i))

        def last_load(sp, l, i, row):
            sp.wait_ge(S(f"l_sums{l}"), 2 * i)
            sp.dma_start(l_x3[l][0:P, :], by_rows(x2tab, row)).then_inc(S(f"l_ina{l}"), 16)
            sp.dma_start(l_a3[l][0:P, :], by_rows(acc3, row)).then_inc(S(f"l_ina{l}"), 16)

        def last_pool(pool, l, i):
            yield 0
            pool.wait_ge(S(f"l_ina{l}"), 48 * of_parity(l) + 32 * (i + 1))
            pool.sem_inc(S("pool_turn"))
            a3 = l_a3[l][0:P, :].rearrange("p (r k d) -> p r k d", r=R, k=K)
            nc.gpsimd.tensor_tensor(a3[:, :, 0, :], a3[:, :, 0, :], a3[:, :, 1, :], ALU.add).then_inc(S(f"l_sums{l}"), 1)
            pool.wait_ge(S(f"l_sums{l}"), 2 * i + 1)
            pool.wait_ge(S(f"l_act{l}"), HEAD + 2 * tiles_before(l) + 3 * i)
            pool.sem_inc(S("pool_turn"))
            nc.gpsimd.tensor_tensor(t3r(l_u[l][0:P, :]), a3[:, :, 0, :], t3r(l_x3[l][0:P, :]), ALU.add).then_inc(
                S(f"l_sums{l}"), 1)

        def last_act(act, l, i):
            b, c = 2 * tiles_before(l) + 2 * i, 2 * tiles_before(l) + 3 * i
            yield 2
            act.wait_ge(S(f"l_stats{l}"), b + 1)
            act.wait_ge(S(f"l_act{l}"), HEAD + c)
            rstd_act(l)
            yield 4
            act.wait_ge(S(f"l_stats{l}"), b + 2)
            act.wait_ge(S(f"l_outa{l}"), HEAD + 16 * (of_parity(l) + i))
            normalise_act(l, range(R // 2), l_u[l], l_out[l])
            yield 6
            act.wait_ge(S(f"l_act{l}"), HEAD + c + 3)
            act.dma_start(by_rows(out, (2 * i + l) * NT), l_out[l][0:P, :]).then_inc(S(f"l_outa{l}"), 16)

        def last_dve(dve, l, i):
            c = 2 * tiles_before(l) + 3 * i
            yield 1
            dve.wait_ge(S(f"l_sums{l}"), 2 * i + 2)
            variance_dve(dve, l, 5 * tiles_before(l) + 3 * i, l_u[l])
            yield 3
            dve.wait_ge(S(f"l_act{l}"), HEAD + c + 1)
            shift_dve(dve, l)
            yield 5
            dve.wait_ge(S(f"l_stats{l}"), 2 * tiles_before(l) + 2 * i + 2)
            dve.wait_ge(S(f"l_outa{l}"), HEAD + 16 * (of_parity(l) + i))
            for r in range(R // 2, R):
                last_n = nc.vector.tensor_scalar(l_out[l][0:P, D * r:D * r + D], l_u[l][0:P, D * r:D * r + D],
                                                 l_rs[l][0:P, r:r + 1], l_nb[l][0:P, r:r + 1], ALU.mult, ALU.add)
            last_n.then_inc(S(f"l_act{l}"), 1)

        VECS = ((B0, bias0), (G1, ln1_g), (LB1, ln1_b), (G2, ln2_g), (LB2, ln2_b), (MB2, mlp_b2), (L2B, L2_b))
        MATS = ((0, W2), (1, W1[:, 0:D]), (2, W_phys), (3, W_neur), (4, L2_W))

        @block.sync
        def _(sp):
            for name in HEADED:
                sp.sem_inc(S(name), HEAD)
            sp.wait_ge(S("cleared"), 1)
            n = 0

            def get(o, a):
                nonlocal n
                sp.dma_start(o, a).then_inc(S("loaded"), 16)
                n += 16

            for v, a in VECS:
                for h in range(2):
                    get(vec[64 * h:64 * h + 64, v:v + 1], a.rearrange("(d o) -> d o", o=1))
            get(col(MB1), mlp_b1.rearrange("(d o) -> d o", o=1))
            get(col(FUS), fusion.rearrange("(a o) -> a o", o=1).broadcast_to((128, 1)))
            for m, a in MATS:
                for h in range(2):
                    get(wbd[64 * h:64 * h + 64, m, 64 * h:64 * h + 64], a)
            for h in range(2):
                get(w1d[:, 64 * h:64 * h + 64], mlp_w1)
                for m, a in ((0, attn[0:D]), (1, attn[D:2 * D]), (2, att_w[0:D]), (3, att_w[D:2 * D])):
                    get(att[64 * h:64 * h + 64, m, h:h + 1], a.rearrange("(d o) -> d o", o=1))
            get(w2s[0:D, :], mlp_w2)
            get(w1e_s[0:D, :], W1[:, D:D + DE])
            get(b2_row[:, :], L2_b.rearrange("(o d) -> o d", o=1).broadcast_to((128, D)))
            get(src_i[:, 0:TC], src.rearrange("(p t) -> p t", p=P))
            get(dst_i[:, 0:TC], dst.rearrange("(p t) -> p t", p=P))
            get(ew[:, :], edge_weight.rearrange("(p t) -> p t", p=P))
            prev_i, next_i = prev_f.bitcast(i32), next_f.bitcast(i32)
            get(prev_i[1:P, :], dst[TC - 1:E - 1].rearrange("(p t) -> p t", t=TC))
            get(prev_i[0:1, 1:TC], dst[0:TC - 1].rearrange("(o t) -> o t", o=1))
            get(next_i[0:P - 1, :], dst[1:E - TC + 1].rearrange("(p t) -> p t", t=TC))
            get(next_i[P - 1:P, 0:TC - 1], dst[E - TC + 1:E].rearrange("(o t) -> o t", o=1))
            assert n == LOADED

            def fill(table, part, parts, s):
                v = table.rearrange("n d -> (n d)").rearrange("(p r f) -> p r f", p=128, f=zero.shape[1])
                n = v.shape[1] // parts
                sp.dma_start(v[:, bass.ds(part * n, n), :], zero[:, :].unsqueeze(1).broadcast_to((128, n, v.shape[2]))).then_inc(
                    S(s), 16)

            fill(agg0, 0, 1, "zeroed0")
            sp.wait_ge(S("w1e_t"), 1)
            for c in range(GC):
                sp.dma_start(w_e[DE * c:DE * c + DE, c // 2, 64 * (c % 2):64 * (c % 2) + 64], w1e_t[0:DE, :]).then_inc(
                    S("w_e_in"), 16)
            sp.wait_ge(S("dis_made"), 1)
            sp.dma_start(distab.rearrange("(p h) -> p h", p=128), deg).then_inc(S("dis_out"), 16)

            eav = edge_attr.rearrange("(p t) d -> p (t d)", p=P)

            def edge_load(par, i, g):
                sp.dma_start(ea_s[par][0:P, :], eav[:, bass.ds(g * (GC * DE), GC * DE)]).then_inc(S(f"ea_in{par}"), 16)

            def feed(loop, par, i, g):
                peeled = isinstance(g, int)
                n = turn(loop, g)
                ends = (loop == 0 and peeled and g == NGR - 1, loop == 1 and peeled and g == NGR - 1)
                if not (ends[0] or ends[1]):
                    for l in LANES:
                        dense_load(sp, l, n + 1, row(loop, g + 1, l))
                if not ends[0]:
                    for l in LANES:
                        if ends[1] and l == 1:
                            sp.wait_ge(S("blk_st0"), HEAD + 16 * NDENSE)
                            sp.wait_ge(S("blk_st1"), HEAD + 16 * (NDENSE - 1))
                        dense_store(sp, l, n, row(loop, g, l))
                fill((acc2, acc3)[loop], g, NGR, f"zeroed{2 + loop}")
                if loop == 0 and not (peeled and g + 2 >= NGR):
                    sp.wait_ge(S(f"rows0_used{par}"), HEAD + i + 1)
                    edge_load(par, i + 1, g + 2)

            edge_load(0, 0, 0)
            edge_load(1, 0, 1)
            for l in LANES:
                dense_load(sp, l, 0, l * NB)
            for loop in range(2):
                with sp.Fori(0, NGR // 2 - 1) as i:
                    for par in LANES:
                        feed(loop, par, i, 2 * i + par)
                for g in range(NGR - 3, NGR):
                    feed(loop, g % 2, g // 2, g)

            for par in LANES:
                sp.wait_ge(S(f"moved{par}"), moved(5, par, 0))
                for c in range(K):
                    sp.wait_ge(S(f"added{c}{par}"), added(5, par, 0))
            for t in range(2):
                for l in LANES:
                    all_load(sp, l, t, l)
            with sp.Fori(0, NGR // 2 - 1) as i:
                for t in range(2):
                    for l in LANES:
                        sp.wait_ge(S(f"l_read{l}"), 2 * i + t + 1)
                        all_load(sp, l, t, 2 * i + 2 + l)
            for t in range(2):
                sp.wait_ge(S("l_read0"), NGR - 2 + t)
                all_load(sp, 0, t, NGR - 1)
            for par in LANES:
                for c in range(K):
                    sp.wait_ge(S(f"added{c}{par}"), added(6, par, 0))
                for t in "ab":
                    sp.wait_ge(S(f"l_out{t}{par}"), HEAD + 16 * of_parity(par))
            for l in LANES:
                last_load(sp, l, 0, l * NT)
            with sp.Fori(0, NTILE // 2 - 1) as i:
                for l in LANES:
                    last_load(sp, l, i + 1, (2 * i + 2 + l) * NT)
            for l in LANES:
                sp.wait_ge(S(f"l_outa{l}"), HEAD + 16 * (of_parity(l) + NTILE // 2))

        @block.gpsimd
        def _(pool):
            nc.gpsimd.memset(ident[:, :], 1.0).then_inc(S("pool_c"), 1)
            nc.gpsimd.memset(low[:, :], 1.0).then_inc(S("pool_c"), 1)
            pool.wait_ge(S("pool_c"), 2)
            nc.gpsimd.affine_select(out=ident[:, :], in_=ident[:, :], pattern=[[-1, 128]], compare_op=ALU.is_equal, fill=0.0,
                                    base=0, channel_multiplier=1).then_inc(S("pool_c"), 1)
            nc.gpsimd.affine_select(out=low[:, :], in_=low[:, :], pattern=[[-1, 128]], compare_op=ALU.is_gt, fill=0.0,
                                    base=0, channel_multiplier=1).then_inc(S("pool_c"), 1)
            nc.gpsimd.iota(iota_lo32, pattern=[[1, 128]], base=0, channel_multiplier=0,
                           allow_small_or_imprecise_dtypes=True).then_inc(S("pool_c"), 1)
            nc.gpsimd.iota(iota_hi32, pattern=[[1, HB]], base=0, channel_multiplier=0,
                           allow_small_or_imprecise_dtypes=True).then_inc(S("pool_c"), 1)
            nc.gpsimd.iota(chain_of[:, :], pattern=[[0, GC // K], [1, K]], base=0, channel_multiplier=0,
                           allow_small_or_imprecise_dtypes=True).then_inc(S("pool_c"), 1)

            def at(ap):
                return bass.IndirectOffsetOnAxis(ap=ap, axis=0)

            def gather(o, table, ix, s):
                pool.indirect_dma_start(out=o, out_offset=None, in_=table, in_offset=at(ix)).then_inc(s, 16)

            def scatter(table, rows_n, ix, a, s, add=False):
                kw = dict(compute_op=ALU.add) if add else {}
                pool.indirect_dma_start(out=table, out_offset=at(ix), in_=a, in_offset=None, bounds_check=rows_n - 1,
                                        oob_is_err=False, **kw).then_inc(s, 16)

            def cols(a, k, w=D):
                return a[0:P, w * k:w * k + w]

            def g0(par, i, g):
                pool.wait_ge(S(f"idx{par}"), i + 1)
                pool.wait_ge(S(f"rows0_used{par}"), HEAD + i)
                pool.sem_inc(S("pool_turn"))
                for k in range(GC):
                    gather(cols(g_s[par], k), x, ix_a[par][:, k:k + 1], S(f"moved{par}"))
                    gather(cols(g_d[par], k), x, ix_b[par][:, k:k + 1], S(f"moved{par}"))
            groups(pool, g0)

            pool.wait_ge(S("dis_out"), 16)
            pool.wait_ge(S("w_made"), 1)
            for t in range(TC):
                gather(dis[:, t:t + 1], distab.rearrange("(n o) -> n o", o=1), dst_i[:, t:t + 1], S(f"added{t % K}{t // K % 2}"))

            def s1(par, i, g):
                pool.wait_ge(S("d1_idx"), g + 1)
                pool.sem_inc(S("pool_turn"))
                for k in range(GC):
                    scatter(agg0, N, ix_a[par][:, k:k + 1], cols(g_s[par], k), S(f"moved{par}"))
            pool.wait_ge(S("zeroed0"), 16)
            groups(pool, s1)

            for par in LANES:
                pool.wait_ge(S(f"moved{par}"), moved(3, par, 0))

            def g3(par, i, g):
                pool.wait_ge(S(f"idx{par}"), of_parity(par) + 1 + i + 1)
                pool.sem_inc(S("pool_turn"))
                for k in range(GC):
                    gather(cols(g_s[par], k), agg0, ix_b[par][:, k:k + 1], S(f"moved{par}"))
            groups(pool, g3)

            for l in LANES:
                pool.wait_ge(S(f"blk_st{l}"), HEAD + 16 * NDENSE)
            pool.wait_ge(S("zeroed2"), 16 * NGR)

            def chain_wait(loop, c, par, i, k):
                if k >= K:
                    pool.wait_ge(S(f"added{c}{par}"), added(loop, par, i) + 16 * (k // K))
                elif par == 0:
                    pool.wait_ge(S(f"added{c}1"), added(loop, 1, i))
                else:
                    pool.wait_ge(S(f"added{c}0"), added(loop, 0, i + 1))
                pool.sem_inc(S("pool_turn"))

            def s2(par, i, g):
                pool.wait_ge(S(f"e2_xrow{par}"), i + 1)
                pool.sem_inc(S("pool_turn"))
                for k in range(GC // 2):
                    scatter(x2tab, N, ix_a[par][:, k:k + 1], cols(xrow[par], k), S(f"moved{par}"))
                pool.wait_ge(S(f"msg_zrow{par}"), i + 1)
                for k in range(GC):
                    chain_wait(4, k % K, par, i, k)
                    scatter(acc2_rows, N * K, ix_b[par][:, k:k + 1], cols(zrow[par], k), S(f"added{k % K}{par}"), add=True)
                    if k % 2:
                        j = GC // 2 + k // 2
                        scatter(x2tab, N, ix_a[par][:, j:j + 1], cols(xrow[par], j), S(f"moved{par}"))
            groups(pool, s2)

            for c in range(K):
                for par in LANES:
                    pool.wait_ge(S(f"added{c}{par}"), added(5, par, 0))
            for par in LANES:
                pool.wait_ge(S(f"moved{par}"), moved(5, par, 0))
            pool.wait_ge(S("zeroed3"), 16 * NGR)

            def g6(par, i, g):
                pool.wait_ge(S(f"idx{par}"), 2 * (of_parity(par) + 1) + i + 1)
                pool.sem_inc(S("pool_turn"))
                for k in range(GC):
                    gather(cols(g_a[par], k, K * D), acc2, ix_a[par][:, k:k + 1], S(f"moved{par}"))

            def s3(par, i, g):
                pool.wait_ge(S(f"msg_zrow{par}"), of_parity(par) + i + 1)
                for k in range(GC):
                    chain_wait(5, k % K, par, i, k)
                    scatter(acc3_rows, N * K, ix_b[par][:, k:k + 1], cols(zrow[par], k), S(f"added{k % K}{par}"), add=True)

            g6(0, 0, 0)
            g6(1, 0, 1)
            with pool.Fori(0, NGR // 2 - 1) as i:
                g6(0, i + 1, 2 * i + 2)
                g6(1, i + 1, 2 * i + 3)
                s3(0, i, 2 * i)
                s3(1, i, 2 * i + 1)
            g6(0, NGR // 2, NGR - 1)
            for g in range(NGR - 3, NGR):
                s3(g % 2, g // 2, g)

            tiles(pool, last_pool)

        @block.tensor
        def _(pe):
            pe.wait_ge(S("pool_c"), 7)
            pe.wait_ge(S("consts"), 1)
            z = oh_hi[0][0:P, 0:HH]
            pe.wait_ge(S("hist_ready"), 1)
            for h in range(2):
                last_h = nc.tensor.matmul(psGH[0][:, 512 * h:512 * h + HH], oh_lo[0][0:P, :], z, start=True, stop=False)
            last_h.then_inc(S("hist_pe"), 1)
            with pe.Fori(0, TC // 2) as i:
                for l in LANES:
                    pe.wait_ge(S(f"onehot{l}"), i + 1)
                    for h in range(2):
                        last_h = nc.tensor.matmul(psGH[0][:, 512 * h:512 * h + HH], oh_lo[l][0:P, :],
                                                  oh_hi[l][0:P, HH * h:HH * h + HH], start=False, stop=False)
                    last_h.then_inc(S(f"onehot_used{l}"), 1)
            pe.wait_ge(S("hist_ready"), 2)
            for h in range(2):
                last_h = nc.tensor.matmul(psGH[0][:, 512 * h:512 * h + HH], oh_lo[0][0:P, :], z, start=False, stop=True)
            last_h.then_inc(S("hist_pe"), 1)
            pe.wait_ge(S("loaded"), LOADED)
            nc.tensor.matmul(psA[0][:, 0:128], wbd[:, 0, :], blk_c[:, :], start=True, stop=True)
            for m in range(1, 4):
                nc.tensor.matmul(psA[0][:, 128 * m:128 * m + 128], wbd[:, m, :], ident[:, :], start=True, stop=True)
            nc.tensor.matmul(psB[0][:, 0:128], wbd[:, 4, :], ident[:, :], start=True, stop=True)
            nc.tensor.transpose(psB[0][:, 128:256], w1d, ident[:, :])
            nc.tensor.matmul(psB[0][:, 256:320], w2s[0:D, :], blk_c[0:D, 0:D], start=True, stop=True)
            nc.tensor.transpose(psB[0][0:DE, 384:384 + D], w1e_s[0:D, :], ident[0:D, 0:D]).then_inc(S("setup_ps"), 1)
            pe.wait_ge(S("w_made"), 1)
            for j, v in enumerate((B0, CR, LB2, L2B)):
                nc.tensor.matmul(psA[1][:, j:j + 1], blk_c[:, :], col(v), start=True, stop=True)
            nc.tensor.matmul(psA[1][:, 4:5], wt[0:D, W1T, :], vec[0:D, LB1:LB1 + 1], start=True, stop=True)
            for f in range(4):
                last_f = nc.tensor.matmul(psB[1][0:D, P * f:P * f + P], ends[:, f:f + 1].broadcast_to((P, D)),
                                          ident[0:P, 0:P], start=True, stop=True)
            last_f.then_inc(S("setup_ps"), 1)
            end_phase(pe, 1)

            groups_and_blocks(pe, 0, scores0_pe, dense_pe)
            end_phase(pe, 2)
            for k, n in enumerate((1, 1, 1, 1, D, D)):
                carries_pe(pe, k + 1, n)
            end_phase(pe, 3)
            groups_and_blocks(pe, 1, dst1_pe, dense_pe)
            end_phase(pe, 4)
            group_pairs(pe, src1_pe)
            end_phase(pe, 5)
            for k, n in enumerate((1, 1, 1, 1, D, D)):
                carries_pe(pe, 6 + k + 1, n)
            end_phase(pe, 6)
            group_pairs(pe, dst2_pe)
            end_phase(pe, 7)
            group_pairs(pe, dst3_pe)

        @block.scalar
        def _(act):
            act.wait_ge(S("loaded"), LOADED)
            nc.scalar.activation(col(FUN), col(FUS), ACT.Sigmoid).then_inc(S("fusion"), 1)
            act.wait_ge(S("deg_max"), 1)
            nc.scalar.activation(deg, deg, ACT.Abs_reciprocal_sqrt).then_inc(S("deg_rs"), 1)
            end_phase(act, 1)
            groups_and_blocks(act, 0, scores0_act, dense_act)
            end_phase(act, 2)
            softmax_act(act, 0)
            end_phase(act, 3)
            groups_and_blocks(act, 1, dst1_act, dense_act)
            end_phase(act, 4)
            group_pairs(act, src1_act)
            end_phase(act, 5)
            softmax_act(act, 1)
            end_phase(act, 6)
            group_pairs(act, dst2_act)
            end_phase(act, 7)
            group_pairs(act, dst3_act, all_act)
            tiles(act, last_act)

        @block.vector
        def _(dve):
            step = [0]

            def own(ins):
                step[0] += 1
                ins.then_inc(S("seg_step"), 1)
                dve.wait_ge(S("seg_step"), step[0])

            nc.vector.memset(wbd, 0.0)
            nc.vector.memset(w_e, 0.0)
            nc.vector.memset(att[:, :, :], 0.0)
            nc.vector.memset(zero[:, :], 0.0)
            nc.vector.memset(src_i[:, :], 0)
            nc.vector.memset(dst_i[:, :], 0)
            nc.vector.memset(last_i[:, :], 0)
            nc.vector.memset(acc_i[:, :], 0)
            nc.vector.memset(prev_f.bitcast(i32)[0:P, :], -1)
            nc.vector.memset(next_f.bitcast(i32)[0:P, :], -1)
            nc.vector.memset(col(EPSV), EPS)
            own(nc.vector.memset(w2p[:, :, :], 0.0))
            dve.drain().then_inc(S("cleared"), 1)
            own(nc.vector.memset(blk_j[:, :], 0.0))
            nc.vector.memset(blk_j[0:64, 0:64], 1.0 / D)
            own(nc.vector.memset(blk_j[64:128, 64:128], 1.0 / D))
            dve.wait_ge(S("pool_c"), 7)
            nc.vector.tensor_tensor(blk_c[:, :], ident[:, :], blk_j[:, :], ALU.subtract).then_inc(S("consts"), 1)
            dve.wait_ge(S("loaded"), LOADED)

            own(nc.vector.tensor_copy(dst_f[0:P, :], src_i[:, 0:TC]))
            own(nc.vector.tensor_scalar(src_hi[0:P, :], dst_f[0:P, :], 1.0 / HB, None, ALU.mult))
            own(nc.vector.tensor_copy(tmp_i[0:P, :], src_hi[0:P, :]))
            own(nc.vector.tensor_copy(src_lo[0:P, :], tmp_i[0:P, :]))
            own(nc.vector.scalar_tensor_tensor(src_hi[0:P, :], src_lo[0:P, :], -float(HB), dst_f[0:P, :], ALU.mult, ALU.add))
            for op, bound, sign in ((ALU.is_lt, 0.0, 1.0), (ALU.is_ge, float(HB), -1.0)):
                own(nc.vector.tensor_scalar(tmp_f[0:P, :], src_hi[0:P, :], bound, sign, op, ALU.mult))
                own(nc.vector.tensor_tensor(src_lo[0:P, :], src_lo[0:P, :], tmp_f[0:P, :], ALU.subtract))
                own(nc.vector.scalar_tensor_tensor(src_hi[0:P, :], tmp_f[0:P, :], float(HB), src_hi[0:P, :], ALU.mult, ALU.add))
            nc.vector.memset(oh_lo[0][0:P, :], 0.0)
            own(nc.vector.memset(oh_hi[0][0:P, :], 0.0))
            nc.vector.tensor_copy(iota_lo, iota_lo32)
            nc.vector.tensor_copy(iota_hi, iota_hi32)
            dve.drain().then_inc(S("hist_ready"), 1)
            dve.wait_ge(S("hist_pe"), 1)
            with dve.Fori(0, TC // 2) as i:
                for l in LANES:
                    dve.wait_ge(S(f"onehot_used{l}"), HEAD + i)
                    nc.vector.tensor_scalar(oh_lo[l][0:P, :], iota_lo[0:P, :], src_lo[0:P, bass.ds(2 * i + l, 1)], None,
                                            ALU.is_equal)
                    nc.vector.tensor_scalar(oh_hi[l][0:P, :], iota_hi[0:P, :], src_hi[0:P, bass.ds(2 * i + l, 1)], None,
                                            ALU.is_equal).then_inc(S(f"onehot{l}"), 1)
            dve.wait_ge(S("onehot_used0"), HEAD + TC // 2)
            nc.vector.memset(oh_lo[0][0:P, :], 0.0)
            nc.vector.memset(oh_hi[0][0:P, :], 0.0).then_inc(S("hist_ready"), 1)
            dve.wait_ge(S("hist_pe"), 2)
            d_ps = psGH[0][:, :].rearrange("p (h c) -> p h c", h=2)[:, :, 0:HH]
            nc.vector.tensor_scalar(deg_on.rearrange("p (h c) -> p h c", h=2), d_ps, 0.0, None, ALU.is_gt)
            nc.vector.tensor_scalar(deg.rearrange("p (h c) -> p h c", h=2), d_ps, 1.0, None, ALU.max).then_inc(S("deg_max"), 1)

            dve.wait_ge(S("setup_ps"), 1)
            nc.vector.tensor_copy(w1e_t[0:DE, :], psB[0][0:DE, 384:384 + D]).then_inc(S("w1e_t"), 1)
            dve.wait_ge(S("fusion"), 1)
            own(nc.vector.tensor_scalar(col(T0), col(FUN), -1.0, 1.0, ALU.mult, ALU.add))
            nc.vector.tensor_copy(wt[:, 0:2, :].rearrange("p w c -> p (w c)"), psA[0][:, 0:256])
            nc.vector.tensor_scalar(wt[:, PHY, :], psA[0][:, 256:384], col(FUN), None, ALU.mult)
            nc.vector.tensor_scalar(wt[:, NEU, :], psA[0][:, 384:512], col(T0), None, ALU.mult)
            nc.vector.tensor_copy(wt[:, L2W:L2W + 2, :].rearrange("p w c -> p (w c)"), psB[0][:, 0:256])
            nc.vector.tensor_scalar(wt[:, DG2, :], blk_c[:, :], col(G2), None, ALU.mult)
            nc.vector.tensor_copy(w2p[:, 0, 0:64], psB[0][:, 256:320])
            nc.vector.tensor_copy(w2p[:, 1, 64:128], psB[0][:, 256:320])
            nc.vector.tensor_tensor(col(CR), col(LB1), col(MB2), ALU.add)

            own(nc.vector.tensor_copy(tmp_f[0:P, :], prev_f.bitcast(i32)[0:P, :]))
            own(nc.vector.tensor_copy(src_lo[0:P, :], next_f.bitcast(i32)[0:P, :]))
            own(nc.vector.tensor_copy(dst_f[0:P, :], dst_i[:, 0:TC]))
            nc.vector.tensor_tensor(same[:, :], dst_f[0:P, :], tmp_f[0:P, :], ALU.is_equal)
            own(nc.vector.tensor_tensor(nxt[:, :], dst_f[0:P, :], src_lo[0:P, :], ALU.is_equal))
            nc.vector.tensor_scalar(last[:, :], nxt[:, :], -1.0, 1.0, ALU.mult, ALU.add)
            nc.vector.tensor_scalar(pen_f[:, :], same[:, :], 1.0, -NEG, ALU.subtract, ALU.mult)
            nc.vector.tensor_scalar(pen_b[:, :], nxt[:, :], 1.0, -NEG, ALU.subtract, ALU.mult)
            own(nc.vector.scalar_tensor_tensor(tmp_f[0:P, :], nxt[:, :], float(SKIP), dst_f[0:P, :], ALU.mult, ALU.add))
            nc.vector.tensor_copy(last_i[:, 0:TC], tmp_f[0:P, :])
            for f, a in enumerate((same, nxt, pen_f, pen_b)):
                nc.vector.tensor_reduce(ends[:, f:f + 1], a[:, :], AX.X, ALU.min)
            for l in LANES:
                nc.vector.tensor_copy(ix_a[l][:, :], src_i[:, GC * l:GC * l + GC])
                nc.vector.tensor_copy(ix_b[l][:, :], dst_i[:, GC * l:GC * l + GC])
            dve.drain().then_inc(S("w_made"), 1)
            nc.vector.nop().then_inc(S("idx0"), 1)
            nc.vector.nop().then_inc(S("idx1"), 1)
            dve.wait_ge(S("deg_rs"), 1)
            nc.vector.tensor_tensor(deg, deg, deg_on, ALU.mult).then_inc(S("dis_made"), 1)
            dve.wait_ge(S("setup_ps"), 2)
            nc.vector.tensor_copy(vec[:, CB0:CB0 + 4], psA[1][:, 0:4])
            nc.vector.tensor_tensor(col(HB1), psA[1][:, 4:5], col(MB1), ALU.add)
            nc.vector.tensor_copy(row_flags[:, :, :].rearrange("d f p -> d (f p)"), psB[1][0:D, 0:4 * P])
            end_phase(dve, 1)

            groups_and_blocks(dve, 0, scores0_dve, dense_dve)
            end_phase(dve, 2)
            softmax_dve(dve, 0, step)
            sums_dve(dve, 0, step)
            end_phase(dve, 3)
            groups_and_blocks(dve, 1, dst1_dve, dense_dve)
            for l in LANES:
                nc.vector.tensor_copy(ix_b[l][:, :], src_i[:, GC * l:GC * l + GC]).then_inc(S(f"idx{l}"), 1)
            for l in LANES:
                dve.wait_ge(S(f"blk_st{l}"), HEAD + 16 * NDENSE)
            end_phase(dve, 4)
            group_pairs(dve, src1_dve)
            end_phase(dve, 5)
            softmax_dve(dve, 1, step)
            sums_dve(dve, 1, step)
            for par in LANES:
                for c in range(K):
                    dve.wait_ge(S(f"added{c}{par}"), added(4, par, 0))
            end_phase(dve, 6)
            group_pairs(dve, dst2_dve)
            for par in LANES:
                dve.wait_ge(S(f"moved{par}"), moved(5, par, 0))
                for c in range(K):
                    dve.wait_ge(S(f"added{c}{par}"), added(5, par, 0))
            for l in LANES:
                nc.vector.tensor_copy(ix_a[l][:, :], dst_i[:, GC * l:GC * l + GC]).then_inc(S(f"idx{l}"), 1)
            end_phase(dve, 7)
            group_pairs(dve, dst3_dve, all_dve)
            tiles(dve, last_dve)


_INS = ['x', 'src', 'dst', 'edge_attr_16', 'edge_weight', 'L0_gnn_W1', 'L0_gnn_W2', 'L0_gnn_attn', 'L0_gnn_bias',
        'L1_gnn_W_phys', 'L1_gnn_W_neur', 'L1_gnn_att_w', 'L1_gnn_channel_fusion', 'L1_gnn_mlp_w1', 'L1_gnn_mlp_b1',
        'L1_gnn_mlp_w2', 'L1_gnn_mlp_b2', 'L1_gnn_ln1_g', 'L1_gnn_ln1_b', 'L1_gnn_ln2_g', 'L1_gnn_ln2_b', 'L2_gnn_W',
        'L2_gnn_b']


def kernel(**inputs):
    import numpy as _np
    import concourse.bacc as _bacc
    from concourse import mybir as _mybir
    from concourse.bass_utils import run_bass_kernel_spmd as _run

    nc = _bacc.Bacc("TRN2", target_bir_lowering=False, num_devices=1)
    arrays, args = {}, []
    for name in _INS:
        a = _np.ascontiguousarray(inputs[name])
        if a.ndim == 0:
            a = a.reshape(1)
        arrays[f"in_{name}_dram"] = a
        args.append(nc.dram_tensor(f"in_{name}_dram", a.shape, _mybir.dt.from_np(a.dtype), kind="ExternalInput").ap())
    shape = inputs["x"].shape
    args.append(nc.dram_tensor("out_0_dram", shape, _mybir.dt.float32, kind="ExternalOutput").ap())
    gnn_resnorm_kernel(nc, *args)
    r = _run(nc, [arrays], core_ids=[0])
    return r.results[0]["out_0_dram"]
```
